# Optimizing a Trainium2 kernel written in Bass

```python
import numpy as np
import jax
import jax.numpy as jnp

def _softmax(x, axis=-1):
    return jax.nn.softmax(x, axis=axis)

def _gelu(x):
    return jax.nn.gelu(x, approximate=True)

def _silu(x):
    return jax.nn.silu(x)

def _sigmoid(x):
    return jax.nn.sigmoid(x)

def _layernorm(x, axis=-1, eps=1e-05):
    m = jnp.mean(x, axis=axis, keepdims=True)
    v = jnp.var(x, axis=axis, keepdims=True)
    return (x - m) / jnp.sqrt(v + eps)

def _scatter_add(tgt, idx, src, axis=0):
    return tgt.at[idx].add(src)

def _segment_sum(src, seg, n):
    return jax.ops.segment_sum(src, seg, n)
kernel_name = 'mk_cond_seq_d4_seqx_r4_bf9d7d'

def setup_inputs(seed: int=0):
    np.random.seed(seed)
    _w = jnp.asarray

    def _rec_inputs():
        import jax
        import jax.numpy as jnp
        _rk = jax.random.key(seed)
        x = 1.648e-05 + 1 * jax.random.normal(jax.random.fold_in(_rk, 1), (4, 512, 288), jnp.float32)
        _lenS = 512 - jax.random.randint(jax.random.fold_in(_rk, 7), (4,), 0, max(1, 512 // 4) + 1, jnp.int32)
        _lenS2 = 512 - jax.random.randint(jax.random.fold_in(_rk, 8), (4,), 0, max(1, 512 // 4) + 1, jnp.int32)
        cond_1152 = 0.00914911 + 1.00357 * jax.random.normal(jax.random.fold_in(_rk, 11), (4, 288), jnp.float32)
        return (x, cond_1152)
    x, cond_1152 = _rec_inputs()

    def _L0_cond_setup():
        import jax, jax.numpy as jnp
        import numpy as np
        NUM_HEADS = 16
        NUM_EXPERTS = 4
        TOP_K = 2
        LN_EPS = 1e-06

        def _ln(h):
            mu = jnp.mean(h, axis=-1, keepdims=True)
            var = jnp.var(h, axis=-1, keepdims=True)
            return (h - mu) * jax.lax.rsqrt(var + LN_EPS)

        def _modulate(h, shift, scale):
            return h * (1.0 + scale[:, None, :]) + shift[:, None, :]
        key = jax.random.key(seed)
        ks = jax.random.split(key, 12)
        B, N, C = (8, 256, 288)
        H = 4 * C
        E = NUM_EXPERTS
        s = 0.02
        return {'x': jax.random.normal(ks[0], (B, N, C), jnp.float32), 'c': jax.random.normal(ks[1], (B, C), jnp.float32), 'w_adaln': jax.random.normal(ks[2], (C, 6 * C), jnp.float32) * s, 'b_adaln': jnp.zeros((6 * C,), jnp.float32), 'w_qkv': jax.random.normal(ks[3], (C, 3 * C), jnp.float32) * s, 'b_qkv': jnp.zeros((3 * C,), jnp.float32), 'w_proj': jax.random.normal(ks[4], (C, C), jnp.float32) * s, 'b_proj': jnp.zeros((C,), jnp.float32), 'w_gate': jax.random.normal(ks[5], (C, E), jnp.float32) * s, 'w1': jax.random.normal(ks[6], (E, C, H), jnp.float32) * s, 'b1': jnp.zeros((E, H), jnp.float32), 'w2': jax.random.normal(ks[7], (E, H, C), jnp.float32) * s, 'b2': jnp.zeros((E, C), jnp.float32)}
    _L0_cond_all = _L0_cond_setup()
    _L0_cond_in = {k: v for k, v in _L0_cond_all.items() if k in ('w_adaln', 'b_adaln', 'w_qkv', 'b_qkv', 'w_proj', 'b_proj', 'w_gate', 'w1', 'b1', 'w2', 'b2')}
    del _L0_cond_all

    def _L1_cond_setup():
        import math
        import jax, jax.numpy as jnp
        import numpy as np
        B, T, D = (8, 256, 288)
        H = 16
        E = 4
        EPS = 1e-06

        def _layer_norm(x):
            mu = jnp.mean(x, axis=-1, keepdims=True)
            var = jnp.mean(jnp.square(x - mu), axis=-1, keepdims=True)
            return (x - mu) * jax.lax.rsqrt(var + EPS)

        def _modulate(x, shift, scale):
            return x * (1.0 + scale) + shift

        def _attention(y, qkv_w, qkv_b, out_w, out_b):
            b, t, d = y.shape
            hd = d // H
            qkv = y @ qkv_w + qkv_b
            q, k, v = jnp.split(qkv, 3, axis=-1)
            q = q.reshape(b, t, H, hd).transpose(0, 2, 1, 3)
            k = k.reshape(b, t, H, hd).transpose(0, 2, 1, 3)
            v = v.reshape(b, t, H, hd).transpose(0, 2, 1, 3)
            scores = jnp.einsum('bhqd,bhkd->bhqk', q, k) / math.sqrt(hd)
            attn = jax.nn.softmax(scores, axis=-1)
            out = jnp.einsum('bhqk,bhkd->bhqd', attn, v)
            out = out.transpose(0, 2, 1, 3).reshape(b, t, d)
            return out @ out_w + out_b
        key = jax.random.key(seed)
        ks = jax.random.split(key, 12)
        std = 0.02
        return {'x': jax.random.normal(ks[0], (B, T, D), dtype=jnp.float32), 'c': jax.random.normal(ks[1], (B, D), dtype=jnp.float32), 'qkv_w': jax.random.normal(ks[2], (D, 3 * D), dtype=jnp.float32) * std, 'qkv_b': jnp.zeros((3 * D,), dtype=jnp.float32), 'out_w': jax.random.normal(ks[3], (D, D), dtype=jnp.float32) * std, 'out_b': jnp.zeros((D,), dtype=jnp.float32), 'w1': jax.random.normal(ks[4], (D, E * D), dtype=jnp.float32) * std, 'b1': jnp.zeros((E * D,), dtype=jnp.float32), 'w2': jax.random.normal(ks[5], (E * D, D), dtype=jnp.float32) * std, 'b2': jnp.zeros((D,), dtype=jnp.float32), 'ada_w': jax.random.normal(ks[6], (D, 6 * D), dtype=jnp.float32) * std, 'ada_b': jnp.zeros((6 * D,), dtype=jnp.float32)}
    _L1_cond_all = _L1_cond_setup()
    _L1_cond_in = {k: v for k, v in _L1_cond_all.items() if k in ('qkv_w', 'qkv_b', 'out_w', 'out_b', 'w1', 'b1', 'w2', 'b2', 'ada_w', 'ada_b')}
    del _L1_cond_all

    def _L2_cond_setup():
        import jax, jax.numpy as jnp
        import numpy as np
        B, L, C = (8, 256, 288)
        H = 16
        D = C // H
        FF = int(C * 4.0)
        EPS = 1e-06

        def _layernorm(x):
            mu = jnp.mean(x, axis=-1, keepdims=True)
            var = jnp.mean(jnp.square(x - mu), axis=-1, keepdims=True)
            return (x - mu) * jax.lax.rsqrt(var + EPS)

        def _modulate(x, shift, scale):
            return x * (1.0 + scale) + shift

        def _attention(h, W_qkv, b_qkv, W_proj, b_proj):
            b, l, c = h.shape
            qkv = h @ W_qkv + b_qkv
            qkv = qkv.reshape(b, l, 3, H, D)
            q, k, v = (qkv[:, :, 0], qkv[:, :, 1], qkv[:, :, 2])
            scale = D ** (-0.5)
            scores = jnp.einsum('blhd,bmhd->bhlm', q * scale, k)
            attn = jax.nn.softmax(scores, axis=-1)
            o = jnp.einsum('bhlm,bmhd->blhd', attn, v).reshape(b, l, c)
            return o @ W_proj + b_proj
        key = jax.random.key(seed)
        ks = jax.random.split(key, 12)
        s = 0.02
        return {'x': jax.random.normal(ks[0], (B, L, C), jnp.float32), 'c': jax.random.normal(ks[1], (B, 1, C), jnp.float32), 'W_qkv': jax.random.normal(ks[2], (C, 3 * C), jnp.float32) * s, 'b_qkv': jnp.zeros((3 * C,), jnp.float32), 'W_proj': jax.random.normal(ks[3], (C, C), jnp.float32) * s, 'b_proj': jnp.zeros((C,), jnp.float32), 'W_fc1': jax.random.normal(ks[4], (C, FF), jnp.float32) * s, 'b_fc1': jnp.zeros((FF,), jnp.float32), 'W_fc2': jax.random.normal(ks[5], (FF, C), jnp.float32) * s, 'b_fc2': jnp.zeros((C,), jnp.float32), 'W_ada': jax.random.normal(ks[6], (C, 6 * C), jnp.float32) * s, 'b_ada': jnp.zeros((6 * C,), jnp.float32)}
    _L2_cond_all = _L2_cond_setup()
    _L2_cond_in = {k: v for k, v in _L2_cond_all.items() if k in ('W_qkv', 'b_qkv', 'W_proj', 'b_proj', 'W_fc1', 'b_fc1', 'W_fc2', 'b_fc2', 'W_ada', 'b_ada')}
    del _L2_cond_all

    def _L3_cond_setup():
        import jax, jax.numpy as jnp
        import numpy as np
        from jax.scipy.linalg import expm
        N, D, COND_DIM = (288, 64, 288)
        B, T = (16, 256)

        def _rotation(cond, W, b):
            v = jax.nn.silu(cond) @ W.T + b
            iu, ju = jnp.triu_indices(D, k=1)
            A = jnp.zeros((cond.shape[0], D, D), dtype=v.dtype)
            A = A.at[:, iu, ju].set(v).at[:, ju, iu].set(-v)
            return expm(A)
        key = jax.random.key(seed)
        k1, k2, k3, k4, k5 = jax.random.split(key, 5)
        x = jax.random.normal(k1, (B, T, N), dtype=jnp.float32)
        cond = jax.random.normal(k2, (B, COND_DIM), dtype=jnp.float32)
        P = jax.random.normal(k3, (N, D), dtype=jnp.float32)
        n_skew = D * (D - 1) // 2
        bound = 1.0 / np.sqrt(COND_DIM)
        W = jax.random.uniform(k4, (n_skew, COND_DIM), minval=-bound, maxval=bound, dtype=jnp.float32)
        b = jax.random.uniform(k5, (n_skew,), minval=-bound, maxval=bound, dtype=jnp.float32)
        return {'x': x, 'cond': cond, 'P': P, 'W': W, 'b': b}
    _L3_cond_all = _L3_cond_setup()
    _L3_cond_in = {k: v for k, v in _L3_cond_all.items() if k in ('P', 'W', 'b')}
    del _L3_cond_all
    return {'x': x, 'cond_1152': cond_1152, 'L0_cond_w_adaln': _L0_cond_in['w_adaln'], 'L0_cond_b_adaln': _L0_cond_in['b_adaln'], 'L0_cond_w_qkv': _L0_cond_in['w_qkv'], 'L0_cond_b_qkv': _L0_cond_in['b_qkv'], 'L0_cond_w_proj': _L0_cond_in['w_proj'], 'L0_cond_b_proj': _L0_cond_in['b_proj'], 'L0_cond_w_gate': _L0_cond_in['w_gate'], 'L0_cond_w1': _L0_cond_in['w1'], 'L0_cond_b1': _L0_cond_in['b1'], 'L0_cond_w2': _L0_cond_in['w2'], 'L0_cond_b2': _L0_cond_in['b2'], 'L1_cond_qkv_w': _L1_cond_in['qkv_w'], 'L1_cond_qkv_b': _L1_cond_in['qkv_b'], 'L1_cond_out_w': _L1_cond_in['out_w'], 'L1_cond_out_b': _L1_cond_in['out_b'], 'L1_cond_w1': _L1_cond_in['w1'], 'L1_cond_b1': _L1_cond_in['b1'], 'L1_cond_w2': _L1_cond_in['w2'], 'L1_cond_b2': _L1_cond_in['b2'], 'L1_cond_ada_w': _L1_cond_in['ada_w'], 'L1_cond_ada_b': _L1_cond_in['ada_b'], 'L2_cond_W_qkv': _L2_cond_in['W_qkv'], 'L2_cond_b_qkv': _L2_cond_in['b_qkv'], 'L2_cond_W_proj': _L2_cond_in['W_proj'], 'L2_cond_b_proj': _L2_cond_in['b_proj'], 'L2_cond_W_fc1': _L2_cond_in['W_fc1'], 'L2_cond_b_fc1': _L2_cond_in['b_fc1'], 'L2_cond_W_fc2': _L2_cond_in['W_fc2'], 'L2_cond_b_fc2': _L2_cond_in['b_fc2'], 'L2_cond_W_ada': _L2_cond_in['W_ada'], 'L2_cond_b_ada': _L2_cond_in['b_ada'], 'L3_cond_P': _L3_cond_in['P'], 'L3_cond_W': _L3_cond_in['W'], 'L3_cond_b': _L3_cond_in['b']}

def reference(x, cond_1152, L0_cond_w_adaln, L0_cond_b_adaln, L0_cond_w_qkv, L0_cond_b_qkv, L0_cond_w_proj, L0_cond_b_proj, L0_cond_w_gate, L0_cond_w1, L0_cond_b1, L0_cond_w2, L0_cond_b2, L1_cond_qkv_w, L1_cond_qkv_b, L1_cond_out_w, L1_cond_out_b, L1_cond_w1, L1_cond_b1, L1_cond_w2, L1_cond_b2, L1_cond_ada_w, L1_cond_ada_b, L2_cond_W_qkv, L2_cond_b_qkv, L2_cond_W_proj, L2_cond_b_proj, L2_cond_W_fc1, L2_cond_b_fc1, L2_cond_W_fc2, L2_cond_b_fc2, L2_cond_W_ada, L2_cond_b_ada, L3_cond_P, L3_cond_W, L3_cond_b):
    import jax
    import jax.numpy as jnp

    def _L0_cond_ref(x, c, w_adaln, b_adaln, w_qkv, b_qkv, w_proj, b_proj, w_gate, w1, b1, w2, b2):
        import jax, jax.numpy as jnp
        import numpy as np
        NUM_HEADS = 16
        NUM_EXPERTS = 4
        TOP_K = 2
        LN_EPS = 1e-06

        def _ln(h):
            mu = jnp.mean(h, axis=-1, keepdims=True)
            var = jnp.var(h, axis=-1, keepdims=True)
            return (h - mu) * jax.lax.rsqrt(var + LN_EPS)

        def _modulate(h, shift, scale):
            return h * (1.0 + scale[:, None, :]) + shift[:, None, :]
        B, N, C = x.shape
        nh = NUM_HEADS
        hd = C // nh
        mod = jax.nn.silu(c) @ w_adaln + b_adaln
        sh_msa, sc_msa, g_msa, sh_mlp, sc_mlp, g_mlp = jnp.split(mod, 6, axis=-1)
        h = _modulate(_ln(x), sh_msa, sc_msa)
        qkv = (h @ w_qkv + b_qkv).reshape(B, N, 3, nh, hd).transpose(2, 0, 3, 1, 4)
        q, k, v = (qkv[0], qkv[1], qkv[2])
        attn = jax.nn.softmax(jnp.einsum('bhqd,bhkd->bhqk', q, k) * hd ** (-0.5), axis=-1)
        o = jnp.einsum('bhqk,bhkd->bhqd', attn, v).transpose(0, 2, 1, 3).reshape(B, N, C)
        o = o @ w_proj + b_proj
        x = x + g_msa[:, None, :] * o
        xn = _modulate(_ln(x), sh_mlp, sc_mlp)
        xf = xn.reshape(-1, C)
        gate_logits = xf @ w_gate
        topk_logits, topk_idx = jax.lax.top_k(gate_logits, TOP_K)
        gates = jax.nn.softmax(topk_logits, axis=-1)
        cw = jnp.sum(jax.nn.one_hot(topk_idx, NUM_EXPERTS, dtype=xf.dtype) * gates[..., None], axis=1)
        hmid = jax.nn.gelu(jnp.einsum('tc,ech->eth', xf, w1) + b1[:, None, :], approximate=True)
        eo = jnp.einsum('eth,ehc->etc', hmid, w2) + b2[:, None, :]
        moe = jnp.einsum('te,etc->tc', cw, eo).reshape(B, N, C)
        return x + g_mlp[:, None, :] * moe

    def _L1_cond_ref(x, c, qkv_w, qkv_b, out_w, out_b, w1, b1, w2, b2, ada_w, ada_b):
        import math
        import jax, jax.numpy as jnp
        import numpy as np
        B, T, D = (8, 256, 288)
        H = 16
        E = 4
        EPS = 1e-06

        def _layer_norm(x):
            mu = jnp.mean(x, axis=-1, keepdims=True)
            var = jnp.mean(jnp.square(x - mu), axis=-1, keepdims=True)
            return (x - mu) * jax.lax.rsqrt(var + EPS)

        def _modulate(x, shift, scale):
            return x * (1.0 + scale) + shift

        def _attention(y, qkv_w, qkv_b, out_w, out_b):
            b, t, d = y.shape
            hd = d // H
            qkv = y @ qkv_w + qkv_b
            q, k, v = jnp.split(qkv, 3, axis=-1)
            q = q.reshape(b, t, H, hd).transpose(0, 2, 1, 3)
            k = k.reshape(b, t, H, hd).transpose(0, 2, 1, 3)
            v = v.reshape(b, t, H, hd).transpose(0, 2, 1, 3)
            scores = jnp.einsum('bhqd,bhkd->bhqk', q, k) / math.sqrt(hd)
            attn = jax.nn.softmax(scores, axis=-1)
            out = jnp.einsum('bhqk,bhkd->bhqd', attn, v)
            out = out.transpose(0, 2, 1, 3).reshape(b, t, d)
            return out @ out_w + out_b
        mods = (jax.nn.silu(c) @ ada_w + ada_b)[:, None, :]
        m0, m1, m2, m3, m4, m5 = jnp.split(mods, 6, axis=-1)
        y = _modulate(_layer_norm(x), m0, m1)
        x = x + m2 * _attention(y, qkv_w, qkv_b, out_w, out_b)
        y = _modulate(_layer_norm(x), m3, m4)
        y = jax.nn.gelu(y @ w1 + b1, approximate=True)
        x = x + m5 * (y @ w2 + b2)
        return x

    def _L2_cond_ref(x, c, W_qkv, b_qkv, W_proj, b_proj, W_fc1, b_fc1, W_fc2, b_fc2, W_ada, b_ada):
        import jax, jax.numpy as jnp
        import numpy as np
        B, L, C = (8, 256, 288)
        H = 16
        D = C // H
        FF = int(C * 4.0)
        EPS = 1e-06

        def _layernorm(x):
            mu = jnp.mean(x, axis=-1, keepdims=True)
            var = jnp.mean(jnp.square(x - mu), axis=-1, keepdims=True)
            return (x - mu) * jax.lax.rsqrt(var + EPS)

        def _modulate(x, shift, scale):
            return x * (1.0 + scale) + shift

        def _attention(h, W_qkv, b_qkv, W_proj, b_proj):
            b, l, c = h.shape
            qkv = h @ W_qkv + b_qkv
            qkv = qkv.reshape(b, l, 3, H, D)
            q, k, v = (qkv[:, :, 0], qkv[:, :, 1], qkv[:, :, 2])
            scale = D ** (-0.5)
            scores = jnp.einsum('blhd,bmhd->bhlm', q * scale, k)
            attn = jax.nn.softmax(scores, axis=-1)
            o = jnp.einsum('bhlm,bmhd->blhd', attn, v).reshape(b, l, c)
            return o @ W_proj + b_proj
        ada = jax.nn.silu(c) @ W_ada + b_ada
        shift_msa, scale_msa, gate_msa, shift_mlp, scale_mlp, gate_mlp = jnp.split(ada, 6, axis=-1)
        h = _modulate(_layernorm(x), shift_msa, scale_msa)
        x = x + gate_msa * _attention(h, W_qkv, b_qkv, W_proj, b_proj)
        h = _modulate(_layernorm(x), shift_mlp, scale_mlp)
        mlp = jax.nn.gelu(h @ W_fc1 + b_fc1, approximate=True) @ W_fc2 + b_fc2
        x = x + gate_mlp * mlp
        return x

    def _L3_cond_ref(x, cond, P, W, b):
        import jax, jax.numpy as jnp
        import numpy as np
        from jax.scipy.linalg import expm
        N, D, COND_DIM = (288, 64, 288)
        B, T = (16, 256)

        def _rotation(cond, W, b):
            v = jax.nn.silu(cond) @ W.T + b
            iu, ju = jnp.triu_indices(D, k=1)
            A = jnp.zeros((cond.shape[0], D, D), dtype=v.dtype)
            A = A.at[:, iu, ju].set(v).at[:, ju, iu].set(-v)
            return expm(A)
        U, _ = jnp.linalg.qr(P)
        R = _rotation(cond, W, b)
        z = jnp.einsum('btn,nd->btd', x, U)
        z_rot = jnp.einsum('btd,bde->bte', z, R)
        x_rot = x + jnp.einsum('btd,nd->btn', z_rot - z, U)
        return x_rot
    x = _L0_cond_ref(x, cond_1152, L0_cond_w_adaln, L0_cond_b_adaln, L0_cond_w_qkv, L0_cond_b_qkv, L0_cond_w_proj, L0_cond_b_proj, L0_cond_w_gate, L0_cond_w1, L0_cond_b1, L0_cond_w2, L0_cond_b2)
    x = _L1_cond_ref(x, cond_1152, L1_cond_qkv_w, L1_cond_qkv_b, L1_cond_out_w, L1_cond_out_b, L1_cond_w1, L1_cond_b1, L1_cond_w2, L1_cond_b2, L1_cond_ada_w, L1_cond_ada_b)
    x = _L2_cond_ref(x, cond_1152[:, None, :], L2_cond_W_qkv, L2_cond_b_qkv, L2_cond_W_proj, L2_cond_b_proj, L2_cond_W_fc1, L2_cond_b_fc1, L2_cond_W_fc2, L2_cond_b_fc2, L2_cond_W_ada, L2_cond_b_ada)
    x = _L3_cond_ref(x, cond_1152, L3_cond_P, L3_cond_W, L3_cond_b)
    return x

_drawn_inputs = setup_inputs


def setup_inputs(seed=0):
    import zlib

    import numpy as np

    out = dict(_drawn_inputs(seed))
    spreads = {'L0_cond_b_adaln': (0.0, 0.431),
     'L0_cond_b_qkv': (0.0, 0.8),
     'L0_cond_b_proj': (0.0, 0.355),
     'L0_cond_b1': (0.0, 0.8),
     'L0_cond_b2': (0.0, 0.511),
     'L1_cond_qkv_b': (0.0, 0.8),
     'L1_cond_out_b': (0.0, 0.383),
     'L1_cond_b1': (0.0, 0.8),
     'L1_cond_b2': (0.0, 0.36),
     'L1_cond_ada_b': (0.0, 0.411),
     'L2_cond_b_qkv': (0.0, 0.8),
     'L2_cond_b_proj': (0.0, 0.332),
     'L2_cond_b_fc1': (0.0, 2.0),
     'L2_cond_b_fc2': (0.0, 0.344),
     'L2_cond_b_ada': (0.0, 0.377)}
    factors = {'L0_cond_w_qkv': 8.0,
     'L0_cond_w_proj': 5.511,
     'L0_cond_w_gate': 2.865,
     'L0_cond_w1': 2.707,
     'L1_cond_qkv_w': 8.0,
     'L1_cond_out_w': 6.166,
     'L2_cond_W_qkv': 8.0,
     'L2_cond_W_proj': 5.325,
     'L2_cond_W_fc1': 3.486}
    for name, (base, spread) in spreads.items():
        noise = np.random.default_rng([zlib.crc32(name.encode()), seed]).standard_normal(out[name].shape)
        drawn = base * np.exp(spread * noise) if base else spread * noise
        out[name] = jnp.asarray(drawn.astype(out[name].dtype))
    for name, factor in factors.items():
        out[name] = (out[name] * factor).astype(out[name].dtype)
    return out
```

```python
import concourse.bass as bass
from concourse import mybir
from contextlib import ExitStack

F32 = mybir.dt.float32
F32R = mybir.dt.float32r
BF16 = mybir.dt.bfloat16
I32 = mybir.dt.int32
ALU = mybir.AluOpType
ACT = mybir.ActivationFunctionType
AX = mybir.AxisListType
ADD = bass.bass_isa.ReduceOp.add

B, N, C = 4, 512, 288
TOK = B * N
HEADS, HD = 16, 18
HID = 4 * C
EXPERTS = 4
LAYERS = 3
P = 128
TT = N // P
NT = TOK // P
KC = C // P
TAIL = C - KC * P
T3 = 3 * TAIL
TB = T3 + 2
HG = HEADS // 4
QM = C // 96
HM = HID // P
STK = 6 * HD
Q_PART = [0, 0, 1, 0, 1, 2]
K_PART = [0, 1, 0, 2, 1, 0]
XNW = KC * P + T3
SETS = [(0, e) for e in range(EXPERTS)] + [(1, 0), (2, 0)]
UNITS = B * HM
LN_EPS = 1e-6
SCALE = float(HD) ** -0.5
D3 = 64
SKEW = D3 * (D3 - 1) // 2
VP = 126
VT_ = SKEW // VP
TAYLOR = 11
SQUARINGS = 16
QR_OPS = 24
RSQRT_MAGIC = 1597463007.0
TINY = 1e-37
V_SET, EXPM_SET, U_SET = 1, 4, 5


def build(nc, x, cond, layers, l3_P, l3_W, l3_b, out):
    ctx = ExitStack()
    with ctx:
        BASE = (nc.sbuf_base + 31) // 32 * 32
        top = [BASE]

        def at(name, shape, dt, offset):
            return nc.alloc_sbuf_tensor_at(name, shape, dt, offset=offset)

        def new(name, shape, dt):
            size = 2 if dt == BF16 else 4
            for n in shape[1:]:
                size *= n
            t = at(name, shape, dt, top[0])
            top[0] += (size + 31) // 32 * 32
            return t

        def region(size):
            top[0] += size
            return top[0] - size

        XR = new("residual", [P, NT, C], F32)
        xo = region(2 * KC * TOK * 4)
        XH = at("x_hi", [P, KC, TOK], F32R, xo)
        XL = at("x_lo", [P, KC, TOK], F32R, xo + KC * TOK * 4)
        OT = at("o_t", [P, 4 * HG, N], F32, xo)
        XT = new("x_tail", [TB, TOK], F32R)

        ra = region(32768)
        Q6 = at("q_stack", [STK + 1, HG, 4, N], BF16, ra)
        K6 = at("k_stack", [STK + 1, HG, 4, N], BF16, ra + 16384)
        XN = [at(f"x_norm{i}", [P, TT, XNW], F32, ra + i * 5632) for i in range(2)]
        FX = at("x_mod", [P, KC + 1, N], F32, ra + 11264)
        QF = at("qk_f", [96, 2, N], F32, ra + 17408)
        QR = at("qk_r", [96, 2, N], F32, ra + 21504)
        PT = at("qk_parts", [96, 2, 3, N], BF16, ra + 25600)
        OH_ = at("o_hi", [P, KC, N], F32R, ra + 17408)
        OL = at("o_lo", [P, KC, N], F32R, ra + 21504)
        OX = at("o_tail", [TB, N], F32R, ra + 25600)
        HF = at("hid_f", [P, 2, N], F32, ra + 28672)
        L3W = at("l3_w", [VP, VT_, C], F32, ra)
        SCB = at("silu_c_all", [P, B, C], F32, ra + 18432)
        L3J = at("l3_junk", [VP, C], F32, ra + 23040)
        UT0 = ra
        ID8 = at("ident8", [D3, 8, D3], F32, UT0)
        AS = at("skew_pm", [D3, 2, B, D3], F32, UT0 + 2048)
        NRM = at("skew_norm", [D3, 16], F32, UT0 + 4096)
        NBC = at("norm_rows", [B, 4 + D3], F32, UT0 + 4160)
        MK = at("sq_mask", [D3, 2, B, SQUARINGS], F32, UT0 + 4448)
        MKH = at("sq_half", [D3, B, SQUARINGS], F32, UT0 + 4960)
        THR = at("sq_thr", [D3, SQUARINGS], F32, UT0 + 5216)
        NW = at("wy", [D3, 8, D3], F32, UT0)
        VTR = at("v_t", [D3, C], F32, UT0 + 2048)
        ET = at("e_t", [D3, C], F32, UT0 + 3200)

        rb = region(59392)
        PE_ = at("probs", [P, TT, 4, N], F32, rb)
        VST = at("v_stage", [P, HG, TT, 4, 32], F32, rb + 32768)
        V = at("v", [P, NT, C], F32, rb + 40960)
        WQH = at("wqkv_hi", [P, KC, 3 * C], F32R, rb)
        WQL = at("wqkv_lo", [P, KC, 3 * C], F32R, rb + 6912)
        WQT = at("wqkv_tail", [TB, 3 * C], F32R, rb + 13824)
        W1H = at("w1_hi", [P, KC, HID], F32R, rb)
        W1L = at("w1_lo", [P, KC, HID], F32R, rb + 9216)
        W1T = at("w1_tail", [TB, HID], F32R, rb + 18432)
        W2H = at("w2_hi", [P, HM, C], F32R, rb + 23040)
        W2L = at("w2_lo", [P, HM, C], F32R, rb + 33408)
        HH = at("hid_hi", [P, 3, N], F32R, rb + 43776)
        HL = at("hid_lo", [P, 3, N], F32R, rb + 49920)

        RAWA = new("raw_a", [P, 3 * HID], F32)
        RAWB = new("raw_b", [P, HM * C], F32)
        ADA = [RAWA[:, 0:9 * C].rearrange("p (k n) -> p k n", k=3), RAWB[:, :].rearrange("p (k n) -> p k n", k=3)]
        RAWQ = RAWA[:, 0:9 * C].rearrange("p (k n) -> p k n", k=3)
        RAW1 = RAWA[:, :].rearrange("p (k n) -> p k n", k=3)
        RAWP = RAWB[:, 0:3 * C].rearrange("p (k n) -> p k n", k=3)
        RAW2 = RAWB[:, :].rearrange("p (k n) -> p k n", k=HM)
        WPH = new("wproj_hi", [P, KC, C], F32R)
        WPL = new("wproj_lo", [P, KC, C], F32R)
        WPT = new("wproj_tail", [TB, C], F32R)
        GMSA = new("gate_msa", [P, B, C], F32)
        GMLP = new("gate_mlp", [P, B, C], F32)
        B2B = new("b2_rows", [P, 2, C], F32)
        T1 = new("branch", [P, TT, C], F32)
        GROW = at("gate_rows", [B, 2, C], F32, top[0] - TT * C * 4)
        MODC = new("mod_cols", [P, LAYERS, 4, KC + 1, B], F32)
        MV = new("ln_stats", [P, NT, 2], F32)
        BN6 = new("bn6", [P, TT, 6], F32)
        RST = new("rstd", [P, NT], F32)
        NWT = new("newton", [P, 3, NT], F32)
        RC = new("recip", [P, HEADS], F32)
        MX = new("row_max", [P, 2, 16], F32)
        MXT = new("row_max_t", [16, 2, P], BF16)
        ONE = new("ones_bf", [16, P], BF16)
        SC = new("silu_c", [97, 3, B], F32)
        SCT = new("silu_tmp", [96, 2, 3 * B], F32)
        IDN = new("ident", [P, P], F32)
        WGR = new("wgate_raw", [P, KC + 1, EXPERTS], F32)
        WGH = new("wgate_hi", [P, KC, EXPERTS], F32R)
        WGL = new("wgate_lo", [P, KC, EXPERTS], F32R)
        WGT = new("wgate_tail", [T3, EXPERTS], F32R)
        LG = new("logits", [P, NT, EXPERTS], F32)
        RK = new("rank", [P, NT, EXPERTS], F32)
        CMP = new("compare", [P, NT], F32)
        CW = new("expert_w", [P, NT, EXPERTS], F32)
        QA = new("qr_a", [96, 3, D3], F32)
        QV = new("qr_v", [96, 3, D3], F32)
        QG = new("qr_rows_ge", [96, 3, D3], F32)
        QO = new("qr_onehot", [96, D3], F32)
        QM1 = new("qr_m", [96, 3, D3], F32)
        QI = new("qr_in", [96, 2, D3], F32)
        QS = new("qr_sums", [96, 2, D3], F32)
        QC = new("qr_cols", [96, 24], F32)
        QW = new("qr_w", [96, D3], F32)
        UO = new("skew_upper", [D3, B, D3], F32)
        RR = new("rot", [D3, 2, B, D3], F32)
        VC = new("skew_col", [VP, B, VT_], F32)
        BL = new("skew_bias", [VP, VT_], F32)
        SU = new("strict_upper", [D3, D3], F32)
        UU = new("u", [P, 3, D3], F32)
        UTT = new("u_t", [D3, C], F32)
        ZT = at("z_t", [D3, 2, N], F32, ra + 17408)
        assert top[0] <= nc.sbuf_usable_end, (top[0], nc.sbuf_usable_end)

        psum = ctx.enter_context(nc.psum_tensor("psum", [P, 8, 512], F32))

        def bk(i):
            return psum[:, i, :]

        QKD = [nc.dram_tensor(f"qk_parts_d{l}", [2, 3, C, TOK], BF16, kind="Internal").ap() for l in range(LAYERS)]
        ONED = nc.dram_tensor("ones_d", [16, P], BF16, kind="Internal").ap()
        GD = [nc.dram_tensor(f"gates_d{l}", [2, B, C], F32, kind="Internal").ap() for l in range(LAYERS)]
        VD = nc.dram_tensor("skew_d", [B, SKEW], F32, kind="Internal").ap()
        SCD = nc.dram_tensor("silu_d", [B, C], F32, kind="Internal").ap()

        def sem(name):
            return ctx.enter_context(nc.semaphore(name))

        s_x = sem("x_loaded")
        s_in = sem("cond_loaded")
        s_ra = sem("raw_a_loaded")
        s_rb = sem("raw_b_loaded")
        s_wg = sem("wgate_loaded")
        s_cst = sem("constants_made")
        s_sce = sem("exp_of_minus_c")
        s_sc = sem("silu_made")
        s_mod = sem("mod_products")
        s_gr = sem("gate_rows_copied")
        s_gd = sem("gate_rows_stored")
        s_gm = sem("gate_msa_loaded")
        s_gl = sem("gate_mlp_loaded")
        s_mc_ = sem("mod_cols_made")
        s_wsp = sem("weight_hi_made")
        s_wl = sem("weight_lo_made")
        s_dv = sem("vector_steps")
        s_xn = sem("x_normalised")
        s_tr = sem("x_transposed")
        s_fx = sem("x_modulated")
        s_hi = sem("x_hi_made")
        s_lo = sem("x_lo_made")
        s_qk = sem("qk_products")
        s_qf = sem("qk_copied")
        s_p1 = sem("qk_part0")
        s_p3 = sem("qk_part2")
        s_pd = [sem(f"qk_parts_stored{i}") for i in range(2)]
        s_vm = sem("v_products")
        s_v = sem("v_copied")
        s_one = sem("ones_stored")
        s_ld = [sem(f"stacks_loaded{g}") for g in range(HG)]
        s_s = sem("scores_for_max")
        s_mx = sem("row_max_made")
        s_mt = sem("row_max_turned")
        s_mc = sem("row_max_copied")
        s_mr = [sem(f"row_max_placed{g}") for g in range(2)]
        s_vs = sem("v_staged")
        s_st = sem("scores_t")
        s_e = sem("probs_made")
        s_av = sem("probs_used")
        s_ot = sem("o_t_copied")
        s_to = sem("o_turned")
        s_on = sem("o_normalised")
        s_pj = sem("proj_products")
        s_dvp = sem("proj_copied")
        s_xr = sem("residual_updated")
        s_wl2 = sem("wgate_split")
        s_lg = sem("gate_logits")
        s_cw = sem("expert_logits_shifted")
        s_ce = sem("expert_exp")
        s_f1 = sem("hidden_products")
        s_g = sem("gelu_made")
        s_h = sem("hidden_lo_made")
        s_h2 = sem("hidden_used")
        s_f2 = sem("ffn_products")
        s_ev = sem("ffn_copied")
        s_b2 = [sem(f"b2_loaded{i}") for i in range(2)]
        s_scd = sem("silu_stored")
        s_l3 = sem("l3_loaded")
        s_vc = sem("skew_made")
        s_vd = sem("skew_stored")
        s_uo = sem("skew_placed")
        s_p = sem("p_loaded")
        s_qr = sem("qr_steps")
        s_pace = sem("qr_pace")
        s_pp = sem("l3_products")
        s_pv = sem("l3_copied")
        s_zt = sem("last_turned")
        s_zf = sem("last_x_copied")
        s_zp = sem("last_z_products")
        s_zc = sem("last_z_copied")
        s_zo = sem("last_products")
        s_fin = sem("last_added")
        s_out = sem("stored")

        QR_END = 8 + D3 * QR_OPS

        def tn(l, s, b):
            return 12 * l + 4 * s + b

        def first_set(l):
            return 0 if l == 0 else EXPERTS + l - 1

        def sets_of(l):
            return [f for f, (a, _) in enumerate(SETS) if a == l]

        events = []
        for l in range(LAYERS):
            events += [("q", l), ("p", l)]
            for f in sets_of(l):
                events += [("1", f), ("2", f)]
        split_no = {k: i for i, k in enumerate(events)}

        def loads(order):
            total, res = 0, {}
            for key, n in order:
                total += 16 * n
                res[key] = total
            return res

        order_a, order_b = [(("a", 0), 2)], [(("a", 0), 2)]
        for l in range(LAYERS):
            order_a.append((("q", l), 6))
            order_b.append((("p", l), 6))
            if l + 1 < LAYERS:
                order_a.append((("a", l + 1), 2))
                order_b.append((("a", l + 1), 2))
            for f in sets_of(l):
                order_a.append((("1", f), 6))
                order_b.append((("2", f), 1))
        RA, RB = loads(order_a), loads(order_b)

        def xr_count(l, f=None):
            n = 0
            for k in range(LAYERS):
                n += NT
                if k == l and f is None:
                    return n
                for g in sets_of(k):
                    n += NT
                    if g == f:
                        return n
            return n

        def split_terms(H, L, T, XHi, XLo, XTa, wc, xc, tail):
            terms = []
            for c in range(KC):
                terms += [(H[:, c, wc], XHi[:, c, xc]), (L[:, c, wc], XHi[:, c, xc]), (H[:, c, wc], XLo[:, c, xc])]
            return terms + [(T[0:tail, wc], XTa[0:tail, xc])]

        block = ctx.enter_context(nc.Block())

        @block.sync
        def _(sp):
            x_v = x.rearrange("b (t p) c -> b p t c", p=P)

            def load_k288(dst, w, bias, s):
                sp.dma_start(dst[:, 0:KC, :], w[0:KC * P, :].rearrange("(k p) n -> p k n", p=P)).then_inc(s, 16)
                for r in range(3):
                    sp.dma_start(dst[r * TAIL:(r + 1) * TAIL, KC, :], w[KC * P:C, :]).then_inc(s, 16)
                for r in range(2):
                    sp.dma_start(dst[T3 + r:T3 + r + 1, KC, :], bias.unsqueeze(0)).then_inc(s, 16)

            def load_ada(l):
                for h, s in ((0, s_ra), (1, s_rb)):
                    cols = slice(3 * C * h, 3 * C * (h + 1))
                    sp.dma_start(ADA[h][0:96, :, :], layers[l]["ada_w"][:, cols].rearrange("(k p) n -> p k n", p=96)).then_inc(s, 16)
                    sp.dma_start(ADA[h][96:97, 0, :], layers[l]["ada_b"][cols].unsqueeze(0)).then_inc(s, 16)

            def ffn_weights(f):
                l, e = SETS[f]
                w = layers[l]
                if l == 0:
                    return w["w1"][e], w["b1"][e], w["w2"][e], w["b2"][e]
                return w["w1"], w["b1"], w["w2"], w["b2"]

            def load_w1(f):
                w1, b1, _, _ = ffn_weights(f)
                load_k288(RAW1, w1, b1, s_ra)

            def load_w2(f):
                _, _, w2, b2 = ffn_weights(f)
                sp.dma_start(RAW2, w2.rearrange("(k p) n -> p k n", p=P)).then_inc(s_rb, 16)
                sp.dma_start(B2B[:, f % 2, :], b2.partition_broadcast(P)).then_inc(s_b2[f % 2], 16)

            def store_gates(l):
                sp.wait_ge(s_gr, 2 * (l + 1))
                sp.dma_start(GD[l].rearrange("g b c -> b g c"), GROW[:, :, :]).then_inc(s_gd, 16)
                sp.wait_ge(s_gd, 16 * (l + 1))

            def load_gate(l, g):
                sp.dma_start((GMSA, GMLP)[g][:, :, :], GD[l][g].partition_broadcast(P)).then_inc((s_gm, s_gl)[g], 16)

            with nc.allow_non_contiguous_dma("columns of the condition"):
                for k in range(3):
                    sp.dma_start(SC[0:96, k, :], cond[:, 96 * k:96 * k + 96].rearrange("b p -> p b")).then_inc(s_in, 16)
            load_ada(0)
            for b in range(B):
                sp.dma_start(XR[:, TT * b:TT * b + TT, :], x_v[b]).then_inc(s_x, 16)
            sp.dma_start(QA[:, :, :], l3_P.rearrange("(k p) d -> p k d", p=96)).then_inc(s_p, 16)
            wg = layers[0]["w_gate"]
            with nc.allow_non_contiguous_dma("narrow gate weight"):
                sp.dma_start(WGR[:, 0:KC, :], wg[0:KC * P, :].rearrange("(k p) n -> p k n", p=P)).then_inc(s_wg, 16)
                for r in range(3):
                    sp.dma_start(WGR[r * TAIL:(r + 1) * TAIL, KC, :], wg[KC * P:C, :]).then_inc(s_wg, 16)
            sp.wait_ge(s_cst, 2)
            sp.dma_start(ONED, ONE[:, :]).then_inc(s_one, 16)
            sp.wait_ge(s_mod, 1)
            load_k288(RAWQ, layers[0]["qkv_w"], layers[0]["qkv_b"], s_ra)
            load_k288(RAWP, layers[0]["out_w"], layers[0]["out_b"], s_rb)
            store_gates(0)
            load_gate(0, 0)
            load_gate(0, 1)
            sp.wait_ge(s_sc, 2)
            with nc.allow_non_contiguous_dma("columns of the condition"):
                for k in range(3):
                    sp.dma_start(SCD[:, 96 * k:96 * k + 96].rearrange("b p -> p b"), SC[0:96, k, :]).then_inc(s_scd, 16)

            for l in range(LAYERS):
                for b in range(B):
                    for m in range(2 * QM):
                        i = 2 * QM * (B * l + b) + m
                        sp.wait_ge(s_p3, i + 1)
                        sp.dma_start(QKD[l][m // QM, :, 96 * (m % QM):96 * (m % QM) + 96, N * b:N * b + N].rearrange("a p t -> p a t"),
                                     PT[:, i % 2, :, :]).then_inc(s_pd[i % 2], 16)

                def load_stacks(bb, g):
                    for src, part, dst in ((0, Q_PART, Q6), (1, K_PART, K6)):
                        for j in range(6):
                            rows = QKD[l][src, part[j]].rearrange("(h d) t -> d h t", d=HD)
                            sp.dma_start(dst[HD * j:HD * j + HD, g, :, :], rows[:, 4 * g:4 * g + 4, bass.ds(bb * N, N)]).then_inc(s_ld[g], 16)
                    sp.dma_start(K6[STK:STK + 1, g, :, :], ONED.rearrange("a p -> (a p)").rearrange("(o h n) -> o h n", o=1, h=4)).then_inc(s_ld[g], 16)

                def place_max(bb, g):
                    sp.wait_ge(s_mc, 16 * l + 4 * bb + g + 1)
                    sp.dma_start(Q6[STK:STK + 1, g, :, :].rearrange("o h n -> o (h n)").rearrange("o (r p) -> o r p", p=P),
                                 MXT[:, g % 2, :]).then_inc(s_mr[g % 2], 16)

                for i in range(2):
                    sp.wait_ge(s_pd[i], 16 * QM * B * (l + 1))
                sp.wait_ge(s_one, 16)
                sp.wait_ge(s_tr, 3 * tn(l, 1, 0))
                sp.wait_ge(s_lo, tn(l, 1, 0))
                for g in range(3):
                    load_stacks(0, g)
                place_max(0, 0)
                if l + 1 < LAYERS:
                    sp.wait_ge(s_wl, split_no["p", l] + 1)
                    load_ada(l + 1)

                def attention_loads(bb, last):
                    for g in range(HG):
                        if not (last and g >= 1):
                            sp.wait_ge(s_st, 256 * l + 16 * (4 * bb + g) + 1)
                            load_stacks(bb + (g + 3) // 4, (g + 3) % 4)
                        if not (last and g == 3):
                            place_max(bb + (g + 1) // 4, (g + 1) % 4)

                with sp.Fori(0, B - 1) as bb:
                    attention_loads(bb, False)
                attention_loads(B - 1, True)

                if l + 1 < LAYERS:
                    sp.wait_ge(s_mod, l + 2)
                else:
                    sp.wait_ge(s_wl, split_no["p", l] + 1)
                f0 = first_set(l)
                load_w1(f0)
                if f0 >= 2:
                    sp.wait_ge(s_ev, 16 * (f0 - 1))
                load_w2(f0)
                if l + 1 < LAYERS:
                    store_gates(l + 1)
                    sp.wait_ge(s_xr, xr_count(l))
                    load_gate(l + 1, 0)
                for f in sets_of(l):
                    last = f == sets_of(l)[-1]
                    sp.wait_ge(s_wl, split_no["1", f] + 1)
                    if not last:
                        load_w1(f + 1)
                    elif l + 1 < LAYERS:
                        load_k288(RAWQ, layers[l + 1]["qkv_w"], layers[l + 1]["qkv_b"], s_ra)
                    sp.wait_ge(s_wl, split_no["2", f] + 1)
                    if not last:
                        if f >= 1:
                            sp.wait_ge(s_ev, 16 * f)
                        load_w2(f + 1)
                    elif l + 1 < LAYERS:
                        load_k288(RAWP, layers[l + 1]["out_w"], layers[l + 1]["out_b"], s_rb)
                    if f == V_SET:
                        sp.wait_ge(s_scd, 48)
                        sp.dma_start(L3W[:, :, :], l3_W.rearrange("(p t) c -> p t c", t=VT_)).then_inc(s_l3, 16)
                        sp.dma_start(SCB[:, :, :], SCD.partition_broadcast(P)).then_inc(s_l3, 16)
                        sp.dma_start(BL[:, :], l3_b.rearrange("(p t) -> p t", t=VT_)).then_inc(s_l3, 16)
                    if f == V_SET + 1:
                        sp.wait_ge(s_vc, 1)
                        sp.dma_start(VD.rearrange("b (p t) -> p b t", t=VT_), VC[:, :, :]).then_inc(s_vd, 16)
                        sp.wait_ge(s_vd, 16)
                        with nc.allow_non_contiguous_dma("the last row has one entry"):
                            for i in range(D3 - 1):
                                o = i * (D3 - 1) - i * (i - 1) // 2
                                sp.dma_start(UO[i:i + 1, :, i + 1:D3], VD[:, o:o + D3 - 1 - i].unsqueeze(0)).then_inc(s_uo, 16)
                if l + 1 < LAYERS:
                    sp.wait_ge(s_xr, xr_count(l, sets_of(l)[-1]))
                    load_gate(l + 1, 1)

            out_v = out.rearrange("b (t p) c -> b p t c", p=P)
            for b in range(B):
                sp.wait_ge(s_fin, TT * (b + 1))
                sp.dma_start(out_v[b], XR[:, TT * b:TT * b + TT, :]).then_inc(s_out, 16)
            sp.wait_ge(s_out, 16 * B)

        @block.gpsimd
        def _(gp):
            gp.memset(IDN[:, :], 0.0).then_inc(s_qr, 1)
            gp.memset(QG[:, :, :], 1.0).then_inc(s_qr, 1)
            gp.memset(QO[:, :], 0.0).then_inc(s_qr, 1)
            gp.memset(SU[:, :], 1.0).then_inc(s_qr, 1)
            gp.memset(QC[:, :], 0.5).then_inc(s_qr, 1)
            gp.wait_ge(s_qr, 5)
            gp.affine_select(out=IDN[:, :], in_=IDN[:, :], compare_op=ALU.not_equal, fill=1.0, base=0,
                             pattern=[[-1, P]], channel_multiplier=1).then_inc(s_cst, 1)
            gp.affine_select(out=QG[:, :, :], in_=QG[:, :, :], compare_op=ALU.is_ge, fill=0.0, base=0,
                             pattern=[[96, 3], [-1, D3]], channel_multiplier=1).then_inc(s_qr, 1)
            gp.affine_select(out=QO[:, :], in_=QO[:, :], compare_op=ALU.not_equal, fill=1.0, base=0,
                             pattern=[[-1, D3]], channel_multiplier=1).then_inc(s_qr, 1)
            gp.affine_select(out=SU[:, :], in_=SU[:, :], compare_op=ALU.is_gt, fill=0.0, base=0,
                             pattern=[[1, D3]], channel_multiplier=-1).then_inc(s_qr, 1)
            gp.wait_ge(s_qr, 8)
            gp.wait_ge(s_p, 16)

            half, vcol, oneh, sal = QC[:, 0:1], QC[:, 1:4], QC[:, 4:5], QC[:, 5:7]
            nrm, sg, sn, t_, d_, rs = (QC[:, i:i + 1] for i in range(7, 13))
            ohs, ucol, mhalf = QC[:, 13:14], QC[:, 14:17], QC[:, 17:18]
            s_, al = QC[:, 5:6], QC[:, 6:7]

            with gp.Fori(0, D3) as k:
                done = [0]

                def step(i, pace=False):
                    i.then_inc(s_qr, 1)
                    done[0] += 1
                    gp.wait_ge(s_qr, 8 + QR_OPS * k + done[0])
                    if pace:
                        gp.sem_inc(s_pace, 1)

                kk = bass.ds(k, 1)
                step(gp.memset(mhalf, -0.5))
                step(gp.tensor_tensor(vcol, QA[:, :, kk].rearrange("p c o -> p (c o)"), QG[:, :, kk].rearrange("p c o -> p (c o)"), ALU.mult))
                step(gp.tensor_copy(oneh, QO[:, kk]))
                step(gp.tensor_tensor(QM1[:, :, :], QA[:, :, :], vcol.unsqueeze(2).to_broadcast([96, 3, D3]), ALU.mult))
                step(gp.tensor_tensor(QI[:, 0, :], QM1[:, 0, :], QM1[:, 1, :], ALU.add))
                step(gp.tensor_tensor(QI[:, 0, :], QI[:, 0, :], QM1[:, 2, :], ALU.add))
                step(gp.tensor_tensor(QI[:, 1, :], QA[:, 0, :], oneh.to_broadcast([96, D3]), ALU.mult), pace=True)
                step(gp.partition_all_reduce(QS[:, :, :].rearrange("p a d -> p (a d)"), QI[:, :, :].rearrange("p a d -> p (a d)"), channels=96, reduce_op=ADD))
                step(gp.tensor_copy(sal, QS[:, :, kk].rearrange("p a o -> p (a o)")))
                step(gp.tensor_tensor(nrm, s_, half, ALU.pow), pace=True)
                step(gp.tensor_scalar(sg, al, 0.0, 2.0, ALU.is_ge, ALU.mult), pace=True)
                step(gp.tensor_scalar(sn, sg, -1.0, nrm, ALU.add, ALU.mult))
                step(gp.tensor_tensor(t_, al, sn, ALU.mult), pace=True)
                step(gp.tensor_scalar(d_, t_, s_, TINY, ALU.add, ALU.max))
                step(gp.tensor_tensor(rs, d_, mhalf, ALU.pow), pace=True)
                step(gp.tensor_scalar(QW[:, :], QS[:, 1, :], sn, rs, ALU.mult, ALU.mult), pace=True)
                step(gp.tensor_scalar(QI[:, 0, :], QS[:, 0, :], rs, 1.0, ALU.mult, ALU.mult))
                step(gp.tensor_tensor(QW[:, :], QW[:, :], QI[:, 0, :], ALU.add))
                step(gp.tensor_tensor(ohs, oneh, sn, ALU.mult))
                step(gp.tensor_tensor(vcol[:, 0:1], vcol[:, 0:1], ohs, ALU.add))
                step(gp.tensor_tensor(ucol, vcol, rs.to_broadcast([96, 3]), ALU.mult))
                step(gp.tensor_copy(QV[:, :, kk].rearrange("p c o -> p (c o)"), ucol))
                step(gp.tensor_tensor(QM1[:, :, :], ucol.unsqueeze(2).to_broadcast([96, 3, D3]), QW[:, :].unsqueeze(1).to_broadcast([96, 3, D3]), ALU.mult))
                step(gp.tensor_tensor(QA[:, :, :], QA[:, :, :], QM1[:, :, :], ALU.subtract))
                assert done[0] == QR_OPS

        @block.scalar
        def _(act):
            def mod_rows(l):
                for g in range(2):
                    act.wait_ge(s_mod, l + 1)
                    act.activation(GROW[:, g, :], psum[0:B, 4 + g, 0:C], ACT.Copy).then_inc(s_gr, 1)

            def split_hi(kind, n, raw, H, T, s, value):
                act.wait_ge(s, value)
                if T is None:
                    act.activation(H[:, :, :], raw, ACT.Copy).then_inc(s_wsp, 1)
                else:
                    act.activation(H[:, :, :], raw[:, 0:KC, :], ACT.Copy)
                    act.activation(T[0:TB, :], raw[0:TB, KC, :], ACT.Copy).then_inc(s_wsp, 1)

            def turned(l, s, b):
                n = tn(l, s, b)
                for c in range(KC + 1):
                    rows = P if c < KC else T3
                    act.wait_ge(s_tr, 3 * n + c + 1)
                    if n >= 1:
                        act.wait_ge(s_lo, n)
                    if s == 1:
                        act.activation(FX[0:rows, c, :], psum[0:rows, c, :], ACT.Copy).then_inc(s_fx, 1)
                    else:
                        act.activation(FX[0:rows, c, :], psum[0:rows, c, :], ACT.Identity,
                                       bias=MODC[0:rows, l, s, c, b:b + 1], scale=MODC[0:rows, l, s + 1, c, b:b + 1]).then_inc(s_fx, 1)
                    act.wait_ge(s_fx, 3 * n + c + 1)
                    if s == 1:
                        if b >= 1:
                            act.wait_ge(s_pj, NT * l + TT * b)
                        dst = OH_[:, c, :] if c < KC else OX[0:T3, :]
                    else:
                        dst = XH[:, c, N * b:N * b + N] if c < KC else XT[0:T3, N * b:N * b + N]
                    act.activation(dst, FX[0:rows, c, :], ACT.Copy).then_inc(s_hi, 1)

            def qk_parts(l, b):
                for m in range(2 * QM):
                    i = 2 * QM * (B * l + b) + m
                    act.wait_ge(s_qk, i + 1)
                    if i >= 2:
                        act.wait_ge(s_p3, i - 1)
                        act.wait_ge(s_pd[i % 2], 16 * (i // 2))
                    act.activation(QF[:, i % 2, :], psum[0:96, 3 + i % 2, :], ACT.Copy).then_inc(s_qf, 1)
                    act.activation(PT[:, i % 2, 0, :], psum[0:96, 3 + i % 2, :], ACT.Copy).then_inc(s_p1, 1)

            def attention(l, bb):
                for g in range(HG):
                    i = 4 * bb + g
                    for v in range(16):
                        act.wait_ge(s_st, 256 * l + 16 * i + v + 1)
                        if v % 4 == 0 and g >= 1:
                            act.wait_ge(s_av, 64 * l + 4 * i + v // 4 - 3)
                        act.activation(PE_[:, v // 4, v % 4, :], psum[:, 4 + v % 2, :], ACT.Exp, scale=SCALE).then_inc(s_e, 1)
                        if v == 5 and g >= 1:
                            act.wait_ge(s_av, 64 * l + 4 * i)
                            act.activation(OT[:, bass.ds(i - 1, 1), :].rearrange("p o n -> p (o n)"), bk(6), ACT.Copy).then_inc(s_ot, 1)
                act.wait_ge(s_av, 64 * l + 16 * bb + 16)
                act.activation(OT[:, bass.ds(4 * bb + 3, 1), :].rearrange("p o n -> p (o n)"), bk(6), ACT.Copy).then_inc(s_ot, 1)

            act.wait_ge(s_in, 48)
            act.activation(SCT[:, 0, :], SC[0:96, :, :].rearrange("p k b -> p (k b)"), ACT.Exp, scale=-1.0).then_inc(s_sce, 1)
            mod_rows(0)
            for l in range(LAYERS):
                if l >= 1:
                    act.wait_ge(s_f2, 16 * (sets_of(l - 1)[-1] + 1))
                split_hi("q", l, RAWQ, WQH, WQT, s_ra, RA["q", l])
                split_hi("p", l, RAWP, WPH, WPT, s_rb, RB["p", l])
                act.wait_ge(s_mc_, l + 1)
                turned(l, 0, 0)
                turned(l, 0, 1)
                qk_parts(l, 0)
                turned(l, 0, 2)
                qk_parts(l, 1)
                turned(l, 0, 3)
                qk_parts(l, 2)
                qk_parts(l, 3)
                with act.Fori(0, B) as bb:
                    attention(l, bb)
                if l + 1 < LAYERS:
                    mod_rows(l + 1)
                for b in range(B):
                    turned(l, 1, b)
                for b in range(B):
                    turned(l, 2, b)
                    if b == 0:
                        f = first_set(l)
                        split_hi("1", f, RAW1, W1H, W1T, s_ra, RA["1", f])
                        split_hi("2", f, RAW2, W2H, None, s_rb, RB["2", f])
                if l == 0:
                    act.wait_ge(s_wg, 64)
                    act.activation(WGH[:, :, :], WGR[:, 0:KC, :], ACT.Copy)
                    act.activation(WGT[:, :], WGR[0:T3, KC, :], ACT.Copy).then_inc(s_ce, 1)
                    act.wait_ge(s_cw, 1)
                    act.activation(CW[:, :, :], LG[:, :, :], ACT.Exp).then_inc(s_ce, 1)
                for f in sets_of(l):
                    for u in range(UNITS):
                        i = UNITS * f + u
                        act.wait_ge(s_f1, i + 1)
                        if i >= 2:
                            act.wait_ge(s_h, i - 1)
                        act.activation(HF[:, i % 2, :], bk(u % 3), ACT.Gelu_apprx_tanh).then_inc(s_g, 1)
                    if f != sets_of(l)[-1]:
                        split_hi("1", f + 1, RAW1, W1H, W1T, s_ra, RA["1", f + 1])
                        act.wait_ge(s_f2, 16 * (f + 1))
                        split_hi("2", f + 1, RAW2, W2H, None, s_rb, RB["2", f + 1])

            for b in range(B):
                for c in range(KC + 1):
                    rows = P if c < KC else TAIL
                    act.wait_ge(s_zt, 3 * b + c + 1)
                    if b >= 1:
                        act.wait_ge(s_zp, 2 * b - 1)
                    act.activation(FX[0:rows, c, :], psum[0:rows, c, :], ACT.Copy).then_inc(s_zf, 1)
                for j in range(2):
                    act.wait_ge(s_zp, 2 * b + j + 1)
                    if b >= 1 and j == 1:
                        act.wait_ge(s_zo, TT * b)
                    act.activation(ZT[:, j, :], psum[0:D3, 3 + j, :], ACT.Copy).then_inc(s_zc, 1)

        @block.tensor
        def _(pe):
            def products(dst, terms, stop=True):
                for n, (a, r) in enumerate(terms):
                    i = pe.matmul(dst, a, r, start=(n == 0), stop=(n == len(terms) - 1))
                return i

            def mods(l):
                pe.wait_ge(s_ra, RA["a", l])
                pe.wait_ge(s_rb, RB["a", l])
                for v, vec in enumerate((0, 1, 3, 4)):
                    w = ADA[vec // 3]
                    col = (vec % 3) * C
                    for c in range(KC + 1):
                        o = P + (v * (KC + 1) + c) * B
                        for r in range(1 if c < KC else 3):
                            width = P if c < KC else TAIL
                            for k in range(3):
                                K = 97 if k == 0 else 96
                                pe.matmul(psum[r * TAIL:r * TAIL + width, 7, o:o + B], w[0:K, k, col + c * P:col + c * P + width],
                                          SC[0:K, k, :], start=(k == 0), stop=(k == 2))
                for g in range(2):
                    for k in range(3):
                        K = 97 if k == 0 else 96
                        i = pe.matmul(psum[0:B, 4 + g, 0:C], SC[0:K, k, :], ADA[g][0:K, k, 2 * C:3 * C], start=(k == 0), stop=(k == 2))
                i.then_inc(s_mod, 1)

            def turn(l, s, b):
                n = tn(l, s, b)
                pe.wait_ge(s_xn, n + 1)
                for c in range(KC + 1):
                    rows = P if c < KC else T3
                    if n >= 1:
                        pe.wait_ge(s_fx, 3 * n - 2 + c)
                    for t in range(TT):
                        i = pe.transpose(psum[0:rows, c, P * t:P * t + P], XN[n % 2][:, t, P * c:P * c + rows], IDN[:, :])
                    i.then_inc(s_tr, 1)

            def qkv(l, b):
                pe.wait_ge(s_lo, tn(l, 0, b) + 1)
                if b == 0:
                    pe.wait_ge(s_wl, split_no["q", l] + 1)
                xc = slice(N * b, N * b + N)
                for m in range(2 * QM):
                    i = 2 * QM * (B * l + b) + m
                    if i >= 2:
                        pe.wait_ge(s_p1, i - 1)
                    products(psum[0:96, 3 + i % 2, :], split_terms(WQH, WQL, WQT, XH, XL, XT, slice(96 * m, 96 * m + 96), xc, TB)).then_inc(s_qk, 1)
                for t in range(TT):
                    i = NT * l + TT * b + t
                    if i >= 2:
                        pe.wait_ge(s_v, i - 1)
                    xt = slice(N * b + P * t, N * b + P * t + P)
                    terms = split_terms(WQH, WQL, WQT, XH, XL, XT, slice(2 * C, 3 * C), xt, TB)
                    products(psum[:, 5 + i % 2, 0:C], [(r, a) for a, r in terms]).then_inc(s_vm, 1)

            def scores(l, bb, g, u):
                i = 4 * bb + g
                if u == 0:
                    pe.wait_ge(s_ld[g], 832 * l + 208 * (bb + 1))
                need = 128 * l + 8 * i + u - 1
                if not isinstance(need, int) or need > 0:
                    pe.wait_ge(s_mx, need)
                for j in range(2):
                    qt = 2 * (u % 2) + j
                    mm = pe.matmul(psum[:, 2 * (u % 2) + j, :], Q6[0:STK, g, u // 2, P * qt:P * qt + P], K6[0:STK, g, u // 2, :], start=True, stop=True)
                mm.then_inc(s_s, 1)

            def turn_max(l, bb, g):
                i = 4 * bb + g
                pe.wait_ge(s_mx, 128 * l + 8 * (i + 1))
                pe.wait_ge(s_mc, 16 * l + i)
                pe.transpose(psum[0:16, 7, 0:P], MX[:, g % 2, :], IDN[:, :]).then_inc(s_mt, 1)

            def scores_t(l, bb, g, v):
                i = 4 * bb + g
                if v == 0:
                    pe.wait_ge(s_mr[g % 2], 128 * l + 16 * (2 * bb + g // 2 + 1))
                if g >= 1 or v >= 2:
                    pe.wait_ge(s_e, 256 * l + 16 * i + v - 1)
                kt, h = v // 4, v % 4
                pe.matmul(psum[:, 4 + v % 2, :], K6[0:STK + 1, g, h, P * kt:P * kt + P], Q6[0:STK + 1, g, h, :], start=True, stop=True).then_inc(s_st, 1)

            def use_probs(l, bb, g, kt):
                i = 4 * bb + g
                pe.wait_ge(s_e, 256 * l + 16 * i + 4 * kt + 4)
                if kt == 0:
                    pe.wait_ge(s_vs, 16 * l + i + 1)
                    if g >= 1:
                        pe.wait_ge(s_ot, 16 * l + i)
                for h in range(4):
                    mm = pe.matmul(psum[32 * h:32 * h + 32, 6, :], VST[:, g, kt, h, :], PE_[:, kt, h, :], start=(kt == 0), stop=(kt == TT - 1))
                mm.then_inc(s_av, 1)

            def attention(l, bb, last):
                for g in range(HG):
                    for u in range(8):
                        if u == 1 and not (last and g == 3):
                            turn_max(l, bb + (g + 1) // 4, (g + 1) % 4)
                        if not (last and g >= 2):
                            scores(l, bb + (g + 2) // 4, (g + 2) % 4, u)
                        scores_t(l, bb, g, 2 * u)
                        scores_t(l, bb, g, 2 * u + 1)
                        if u in (0, 2) and g >= 1:
                            use_probs(l, bb, g - 1, 2 + u // 2)
                        if u in (4, 6):
                            use_probs(l, bb, g, u // 2 - 2)
                for kt in (2, 3):
                    use_probs(l, bb, 3, kt)

            def turn_o(l, b):
                for t in range(TT):
                    i = NT * l + TT * b + t
                    if b == 0:
                        pe.wait_ge(s_ot, 16 * (l + 1))
                    if i >= 2:
                        pe.wait_ge(s_on, i - 1)
                    for g in range(HG):
                        mm = pe.transpose(psum[:, 3 + t % 2, P * g:P * g + P], OT[:, 4 * b + g, P * t:P * t + P], IDN[:, :])
                    mm.then_inc(s_to, 1)

            def proj(l, b):
                pe.wait_ge(s_lo, tn(l, 1, b) + 1)
                if b == 0:
                    pe.wait_ge(s_wl, split_no["p", l] + 1)
                for t in range(TT):
                    i = NT * l + TT * b + t
                    if i % NT >= 2:
                        pe.wait_ge(s_dvp, i - 1)
                    terms = split_terms(WPH, WPL, WPT, OH_, OL, OX, slice(0, C), slice(P * t, P * t + P), TB)
                    products(psum[:, 5 + i % 2, 0:C], [(r, a) for a, r in terms]).then_inc(s_pj, 1)

            def hidden(f, u):
                l = SETS[f][0]
                b, m = u // HM, u % HM
                i = UNITS * f + u
                if u == 0:
                    pe.wait_ge(s_wl, split_no["1", f] + 1)
                if m == 0:
                    pe.wait_ge(s_lo, tn(l, 2, b) + 1)
                if i >= 3:
                    pe.wait_ge(s_g, i - 2)
                products(bk(u % 3), split_terms(W1H, W1L, W1T, XH, XL, XT, slice(P * m, P * m + P), slice(N * b, N * b + N), TB)).then_inc(s_f1, 1)

            def second(f, u):
                b, m = u // HM, u % HM
                grp = B * f + b
                pe.wait_ge(s_h, UNITS * f + u + 1)
                if u == 0:
                    pe.wait_ge(s_wl, split_no["2", f] + 1)
                for t in range(TT):
                    if m == 0 and grp >= 1:
                        pe.wait_ge(s_ev, TT * (grp - 1) + t + 1)
                    c = slice(P * t, P * t + P)
                    for n, (h, w) in enumerate(((HH, W2H), (HH, W2L), (HL, W2H))):
                        mm = pe.matmul(psum[:, 4 + t, 0:C], h[:, m % 3, c], w[:, m, :], start=(m == 0 and n == 0), stop=(m == HM - 1 and n == 2))
                    if m == HM - 1:
                        mm.then_inc(s_f2, 1)
                if m < HM - 1:
                    mm.then_inc(s_h2, 1)

            def l3_begin(n):
                pe.wait_ge(s_pv, n)

            def expm_step(n):
                if n == 0:
                    pe.wait_ge(s_uo, 16 * (D3 - 1))
                l3_begin(n)
                if n == 0:
                    for b in range(B):
                        mm = pe.transpose(psum[0:D3, 3, D3 * b:D3 * b + D3], UO[:, b, :], IDN[0:D3, 0:D3])
                elif n == 1:
                    mm = pe.transpose(psum[0:B, 3, 0:D3], NRM[:, 0:B], IDN[0:D3, 0:D3])
                elif n == 2:
                    mm = pe.matmul(psum[0:D3, 3, 0:B], NBC[:, 4:4 + D3], IDN[0:B, 0:B], start=True, stop=True)
                else:
                    for s in range(2):
                        for b in range(B):
                            lhs = AS[:, 1 - s, b, :] if n < 3 + TAYLOR - 1 else RR[:, 1 - s, b, :]
                            mm = pe.matmul(psum[0:D3, 3, D3 * (B * s + b):D3 * (B * s + b + 1)], lhs, RR[:, s, b, :], start=True, stop=True)
                mm.then_inc(s_pp, 1)

            def u_step(n):
                if n == 0:
                    pe.wait_ge(s_qr, QR_END)
                l3_begin(EXPM_STEPS + n)
                o = psum[0:D3, 3, 0:D3]
                o2 = psum[0:D3, 3, D3:2 * D3]
                if n == 0:
                    for c in range(3):
                        mm = pe.matmul(o, QV[:, c, :], QV[:, c, :], start=(c == 0), stop=(c == 2))
                elif n == 1:
                    for c in range(3):
                        mm = pe.transpose(psum[0:D3, 3, 96 * c:96 * c + 96], QV[:, c, :], IDN[0:96, 0:96])
                elif n == 2:
                    mm = pe.transpose(o, NW[:, 0, :], IDN[0:D3, 0:D3])
                elif n < 3 + 12:
                    if n % 2 == 1:
                        mm = pe.matmul(o, NW[:, 1, :], NW[:, 2, :], start=True, stop=True)
                    else:
                        pe.matmul(o, NW[:, 3, :], NW[:, 4, :], start=True, stop=True)
                        mm = pe.matmul(o2, NW[:, 4, :], NW[:, 3, :], start=True, stop=True)
                elif n == 15:
                    mm = pe.matmul(o, NW[:, 3, :], VTR[:, 0:D3], start=True, stop=True)
                elif n == 16:
                    mm = pe.matmul(psum[0:D3, 3, 0:C], NW[:, 5, :], VTR[:, :], start=True, stop=True)
                else:
                    for c in range(KC + 1):
                        rows = P if c < KC else TAIL
                        mm = pe.transpose(psum[0:rows, 3, D3 * c:D3 * c + D3], UTT[:, P * c:P * c + rows], IDN[0:D3, 0:D3])
                mm.then_inc(s_pp, 1)

            pe.wait_ge(s_cst, 2)
            pe.wait_ge(s_sc, 2)
            mods(0)
            for l in range(LAYERS):
                turn(l, 0, 0)
                turn(l, 0, 1)
                qkv(l, 0)
                turn(l, 0, 2)
                qkv(l, 1)
                turn(l, 0, 3)
                qkv(l, 2)
                qkv(l, 3)
                pe.wait_ge(s_v, NT * (l + 1))
                for g in range(2):
                    for u in range(8):
                        scores(l, 0, g, u)
                    if g == 0:
                        turn_max(l, 0, 0)
                with pe.Fori(0, B - 1) as bb:
                    attention(l, bb, False)
                attention(l, B - 1, True)
                if l + 1 < LAYERS:
                    pe.wait_ge(s_mc, 16 * (l + 1))
                    mods(l + 1)
                    pe.wait_ge(s_gr, 2 * (l + 2))
                turn_o(l, 0)
                turn_o(l, 1)
                turn(l, 1, 0)
                proj(l, 0)
                turn(l, 1, 1)
                turn_o(l, 2)
                proj(l, 1)
                turn(l, 1, 2)
                turn_o(l, 3)
                proj(l, 2)
                turn(l, 1, 3)
                proj(l, 3)
                for b in range(B):
                    turn(l, 2, b)
                if l == 0:
                    pe.wait_ge(s_lo, tn(0, 2, B - 1) + 1)
                    pe.wait_ge(s_wl2, 1)
                    for t in range(NT):
                        terms = split_terms(WGH, WGL, WGT, XH, XL, XT, slice(0, EXPERTS), slice(P * t, P * t + P), T3)
                        mm = products(psum[:, 7, EXPERTS * t:EXPERTS * t + EXPERTS], [(r, a) for a, r in terms])
                    mm.then_inc(s_lg, 1)
                    pe.wait_ge(s_cw, 1)
                pe.wait_ge(s_fx, 3 * tn(l, 2, B))
                for f in sets_of(l):
                    for u in range(UNITS):
                        hidden(f, u)
                        if u >= 2:
                            second(f, u - 2)
                        if f == EXPM_SET and u < EXPM_STEPS:
                            expm_step(u)
                        if f == U_SET and u < U_STEPS:
                            u_step(u)
                    second(f, UNITS - 2)
                    second(f, UNITS - 1)

            pe.wait_ge(s_pv, EXPM_STEPS + U_STEPS)
            pe.wait_ge(s_ev, NT * len(SETS))
            for b in range(B):
                pe.wait_ge(s_xr, xr_count(LAYERS - 1, len(SETS) - 1) - NT + TT * (b + 1))
                for c in range(KC + 1):
                    rows = P if c < KC else TAIL
                    if b >= 1:
                        pe.wait_ge(s_zf, 3 * b - 2 + c)
                    for t in range(TT):
                        mm = pe.transpose(psum[0:rows, c, P * t:P * t + P], XR[:, TT * b + t, P * c:P * c + rows], IDN[:, :])
                    mm.then_inc(s_zt, 1)
                pe.wait_ge(s_zf, 3 * b + 3)
                for c in range(KC + 1):
                    rows = P if c < KC else TAIL
                    mm = pe.matmul(psum[0:D3, 3, :], UU[0:rows, c, :], FX[0:rows, c, :], start=(c == 0), stop=(c == KC))
                mm.then_inc(s_zp, 1)
                pe.wait_ge(s_zc, 2 * b + 1)
                pe.matmul(psum[0:D3, 4, :], RR[:, 0, b, :], ZT[:, 0, :], start=True, stop=True).then_inc(s_zp, 1)
                pe.wait_ge(s_zc, 2 * b + 2)
                for t in range(TT):
                    i = TT * b + t
                    if i >= 2:
                        pe.wait_ge(s_fin, i - 1)
                    pe.matmul(psum[:, 5 + i % 2, 0:C], ZT[:, 1, P * t:P * t + P], UTT[:, :], start=True, stop=True).then_inc(s_zo, 1)

        @block.vector
        def _(dve):
            steps = [0]

            def link(i):
                i.then_inc(s_dv, 1)
                steps[0] += 1
                dve.wait_ge(s_dv, steps[0])

            def mods(l):
                dve.wait_ge(s_mod, l + 1)
                mp = psum[:, 7, P:P + 4 * (KC + 1) * B].rearrange("p (v n) -> p v n", v=4)
                mc = MODC[:, l, :, :, :].rearrange("p v c b -> p v (c b)")
                for rows, cols in ((P, slice(0, KC * B)), (T3, slice(KC * B, (KC + 1) * B))):
                    dve.tensor_copy(mc[0:rows, 0:4:2, cols], mp[0:rows, 0:4:2, cols])
                    i = dve.tensor_scalar(mc[0:rows, 1:4:2, cols], mp[0:rows, 1:4:2, cols], 1.0, None, ALU.add)
                i.then_inc(s_mc_, 1)

            def split_lo(key, raw, H, L, T):
                n = split_no[key]
                dve.wait_ge(s_wsp, n + 1)
                if T is None:
                    dve.tensor_tensor(L[:, :, :], raw, H[:, :, :].bitcast(F32), ALU.subtract).then_inc(s_wl, 1)
                    return
                dve.tensor_tensor(L[:, :, :], raw[:, 0:KC, :], H[:, :, :].bitcast(F32), ALU.subtract)
                dve.tensor_tensor(T[TAIL:2 * TAIL, :], raw[TAIL:2 * TAIL, KC, :], T[TAIL:2 * TAIL, :].bitcast(F32), ALU.subtract)
                dve.tensor_tensor(T[T3:T3 + 1, :], raw[T3:T3 + 1, KC, :], T[T3:T3 + 1, :].bitcast(F32), ALU.subtract).then_inc(s_wl, 1)

            def stats(b):
                for t in range(TT):
                    i = dve.bn_stats(BN6[:, t, :], XR[:, TT * b + t, :])
                link(i)
                for t in range(TT):
                    i = dve.bn_aggr(MV[:, TT * b + t, :], BN6[:, t, :])
                link(i)

            def rstd():
                v, y, t = NWT[:, 0, :], NWT[:, 1, :], NWT[:, 2, :]
                link(dve.tensor_scalar(v, MV[:, :, 1], LN_EPS, None, ALU.add))
                link(dve.tensor_scalar(t.bitcast(I32), v.bitcast(I32), 1, None, ALU.arith_shift_right))
                link(dve.tensor_scalar(y.bitcast(I32), t.bitcast(I32), -1.0, RSQRT_MAGIC, ALU.mult, ALU.add))
                for n in range(4):
                    link(dve.scalar_tensor_tensor(t, y, -0.5, y, ALU.mult, ALU.mult))
                    link(dve.tensor_tensor(t, t, v, ALU.mult))
                    link(dve.scalar_tensor_tensor(y if n < 3 else RST[:, :], t, 1.5, y, ALU.add, ALU.mult))

            def normalise(l, s, b):
                n = tn(l, s, b)
                if n >= 2:
                    dve.wait_ge(s_tr, 3 * (n - 1))
                for t in range(TT):
                    i = dve.tensor_scalar(XN[n % 2][:, t, 0:C], XR[:, TT * b + t, :], MV[:, TT * b + t, 0:1], RST[:, TT * b + t:TT * b + t + 1],
                                          ALU.subtract, ALU.mult)
                link(i)
                tails(n)

            def tails(n):
                for r in range(2):
                    i = dve.tensor_copy(XN[n % 2][:, :, C + TAIL * r:C + TAIL * (r + 1)], XN[n % 2][:, :, KC * P:C])
                i.then_inc(s_xn, 1)

            def low(l, s, b):
                n = tn(l, s, b)
                dve.wait_ge(s_hi, 3 * n + 3)
                if s == 1:
                    H, L, T, cols = OH_, OL, OX, slice(0, N)
                    if b >= 1:
                        dve.wait_ge(s_pj, NT * l + TT * b)
                else:
                    H, L, T, cols = XH, XL, XT, slice(N * b, N * b + N)
                dve.tensor_tensor(L[:, :, cols], FX[:, 0:KC, :], H[:, :, cols].bitcast(F32), ALU.subtract)
                dve.tensor_tensor(T[2 * TAIL:T3, cols], FX[2 * TAIL:T3, KC, :], T[2 * TAIL:T3, cols].bitcast(F32), ALU.subtract).then_inc(s_lo, 1)

            def qkv(l, b):
                for m in range(2 * QM):
                    i = 2 * QM * (B * l + b) + m
                    dve.wait_ge(s_p1, i + 1)
                    if i >= 2:
                        dve.wait_ge(s_p3, i - 1)
                    link(dve.tensor_tensor(QR[:, i % 2, :], QF[:, i % 2, :], PT[:, i % 2, 0, :], ALU.subtract))
                    link(dve.tensor_copy(PT[:, i % 2, 1, :], QR[:, i % 2, :]))
                    dve.tensor_tensor(PT[:, i % 2, 2, :], QR[:, i % 2, :], PT[:, i % 2, 1, :], ALU.subtract).then_inc(s_p3, 1)
                for t in range(TT):
                    i = NT * l + TT * b + t
                    dve.wait_ge(s_vm, i + 1)
                    dve.tensor_copy(V[:, TT * b + t, :], psum[:, 5 + i % 2, 0:C]).then_inc(s_v, 1)

            def row_max(l, bb, g, u):
                i = 4 * bb + g
                dve.wait_ge(s_s, 128 * l + 8 * i + u + 1)
                o = 2 * (u % 2)
                dve.tensor_reduce(MX[:, g % 2, 2 * u:2 * u + 2], psum[:, o:o + 2, :], AX.X, ALU.max).then_inc(s_mx, 1)

            def stage(l, bb, g):
                i = 4 * bb + g
                dve.wait_ge(s_mt, 16 * l + i + 1)
                dve.tensor_scalar(MXT[:, g % 2, :], psum[0:16, 7, 0:P], -1.0, None, ALU.mult).then_inc(s_mc, 1)
                src = V[:, bass.ds(TT * bb, TT), 4 * HD * g:4 * HD * (g + 1)].rearrange("p t (h d) -> p t h d", d=HD)
                dst = VST[:, g, :, :, 0:HD]
                dve.tensor_copy(dst, src).then_inc(s_vs, 1)

            def attention(l, bb, last):
                for g in range(HG):
                    for u in range(8):
                        if not (last and g >= 2):
                            row_max(l, bb + (g + 2) // 4, (g + 2) % 4, u)
                        if u == 2 and not (last and g == 3):
                            stage(l, bb + (g + 1) // 4, (g + 1) % 4)

            def o_rows(l, b):
                n = tn(l, 1, b)
                for t in range(TT):
                    i = NT * l + TT * b + t
                    dve.wait_ge(s_to, i + 1)
                    if t == 0:
                        dve.wait_ge(s_tr, 3 * (n - 1))
                    if b == 0 and t == 0:
                        dve.memset(OX[T3:TB, :].bitcast(F32), 1.0)
                    if i >= 1:
                        dve.wait_ge(s_on, i)
                    src = psum[:, 3 + t % 2, :].rearrange("p (h d) -> p h d", d=32)
                    link(dve.reciprocal(RC[:, :], src[:, :, HD:HD + 1].rearrange("p h o -> p (h o)")))
                    j = dve.tensor_tensor(XN[n % 2][:, t, 0:C].rearrange("p (h d) -> p h d", d=HD), src[:, :, 0:HD],
                                          RC[:, :].unsqueeze(2).to_broadcast([P, HEADS, HD]), ALU.mult)
                    j.then_inc(s_on, 1)
                dve.wait_ge(s_on, NT * l + TT * b + TT)
                tails(n)

            def attn_residual(l, b):
                if b == 0:
                    dve.wait_ge(s_gm, 16 * (l + 1))
                    if l + 1 < LAYERS:
                        dve.wait_ge(s_gd, 16 * (l + 2))
                for t in range(TT):
                    i = NT * l + TT * b + t
                    dve.wait_ge(s_pj, i + 1)
                    dve.tensor_tensor(T1[:, t, :], psum[:, 5 + i % 2, 0:C], GMSA[:, b, :], ALU.mult).then_inc(s_dvp, 1)
                dve.wait_ge(s_dvp, NT * l + TT * b + TT)
                dve.tensor_tensor(XR[:, TT * b:TT * b + TT, :], XR[:, TT * b:TT * b + TT, :], T1[:, :, :], ALU.add).then_inc(s_xr, TT)
                dve.wait_ge(s_xr, xr_count(l) - NT + TT * (b + 1))
                stats(b)

            def gates():
                dve.wait_ge(s_lg, 1)
                link(dve.tensor_copy(LG[:, :, :], psum[:, 7, 0:NT * EXPERTS].rearrange("p (t e) -> p t e", e=EXPERTS)))
                link(dve.memset(RK[:, :, :], 0.0))
                for e in range(EXPERTS):
                    for o in range(EXPERTS):
                        if o != e:
                            link(dve.tensor_tensor(CMP[:, :], LG[:, :, o], LG[:, :, e], ALU.is_ge if o < e else ALU.is_gt))
                            link(dve.tensor_tensor(RK[:, :, e], RK[:, :, e], CMP[:, :], ALU.add))
                link(dve.tensor_reduce(CMP[:, :], LG[:, :, :], AX.X, ALU.max))
                link(dve.tensor_scalar(RK[:, :, :], RK[:, :, :], 2.0, None, ALU.is_lt))
                dve.tensor_tensor(LG[:, :, :], LG[:, :, :], CMP[:, :].unsqueeze(2).to_broadcast([P, NT, EXPERTS]), ALU.subtract).then_inc(s_cw, 1)
                dve.wait_ge(s_ce, 2)
                link(dve.tensor_tensor(CW[:, :, :], CW[:, :, :], RK[:, :, :], ALU.mult))
                link(dve.tensor_reduce(CMP[:, :], CW[:, :, :], AX.X, ALU.add))
                link(dve.reciprocal(CMP[:, :], CMP[:, :]))
                link(dve.tensor_tensor(CW[:, :, :], CW[:, :, :], CMP[:, :].unsqueeze(2).to_broadcast([P, NT, EXPERTS]), ALU.mult))

            def hidden_parts(f, u):
                b, m = u // HM, u % HM
                i = UNITS * f + u
                grp = B * f + b
                dve.wait_ge(s_g, i + 1)
                if m >= 3:
                    dve.wait_ge(s_h2, (HM - 1) * grp + m - 2)
                elif grp >= 1:
                    if m == 2:
                        dve.wait_ge(s_f2, TT * grp)
                    else:
                        dve.wait_ge(s_h2, (HM - 1) * (grp - 1) + m + 7)
                link(dve.tensor_copy(HH[:, m % 3, :], HF[:, i % 2, :]))
                dve.tensor_tensor(HL[:, m % 3, :], HF[:, i % 2, :], HH[:, m % 3, :].bitcast(F32), ALU.subtract).then_inc(s_h, 1)

            def ffn_take(f, b):
                grp = B * f + b
                if b == 0:
                    dve.wait_ge(s_b2[f % 2], 16 * (f // 2 + 1))
                for t in range(TT):
                    dve.wait_ge(s_f2, TT * grp + t + 1)
                    dve.tensor_tensor(T1[:, t, :], psum[:, 4 + t, 0:C], B2B[:, f % 2, :], ALU.add).then_inc(s_ev, 1)

            def ffn_add(f, b):
                l, e = SETS[f]
                if b == 0 and e == 0:
                    dve.wait_ge(s_gl, 16 * (l + 1))
                dve.wait_ge(s_ev, TT * (B * f + b + 1))
                for t in range(TT):
                    w = CW[:, TT * b + t, e:e + 1] if l == 0 else 1.0
                    i = dve.scalar_tensor_tensor(T1[:, t, :], T1[:, t, :], w, GMLP[:, b, :], ALU.mult, ALU.mult)
                link(i)
                dve.tensor_tensor(XR[:, TT * b:TT * b + TT, :], XR[:, TT * b:TT * b + TT, :], T1[:, :, :], ALU.add).then_inc(s_xr, TT)
                dve.wait_ge(s_xr, xr_count(l, f) - NT + TT * (b + 1))
                if f == sets_of(l)[-1] and l + 1 < LAYERS:
                    stats(b)

            def skew_entries(u):
                if u == 0:
                    dve.wait_ge(s_l3, 48)
                t, half = u // 2, u % 2
                for b in (2 * half, 2 * half + 1):
                    link(dve.scalar_tensor_tensor(L3J[:, :], L3W[:, t, :], 1.0, SCB[0:VP, b, :], ALU.mult, ALU.mult, accum_out=VC[:, b, t:t + 1]))
                if u == 2 * VT_ - 1:
                    dve.tensor_tensor(VC[:, :, :], VC[:, :, :], BL[:, :].unsqueeze(1).to_broadcast([VP, B, VT_]), ALU.add).then_inc(s_vc, 1)

            def expm_step(n):
                dve.wait_ge(s_pp, n + 1)
                flat = "p s b d -> p (s b) d"
                p8 = psum[0:D3, 3, :].rearrange("p (s d) -> p s d", d=D3)
                if n == 0:
                    dve.tensor_tensor(AS[:, 0, :, :], UO[:, :, :], p8[:, 0:B, :], ALU.subtract)
                    link(dve.tensor_tensor(AS[:, 1, :, :], p8[:, 0:B, :], UO[:, :, :], ALU.subtract))
                    for j in range(8):
                        dve.tensor_copy(ID8[:, j, :], IDN[0:D3, 0:D3])
                    for j in range(SQUARINGS):
                        dve.memset(THR[:, j:j + 1], float(2 ** j))
                    i = dve.tensor_reduce(NRM[:, 0:B], AS[:, 0, :, :], AX.X, ALU.add, apply_absolute_value=True)
                elif n == 1:
                    link(dve.tensor_reduce(NBC[:, 0:1], psum[0:B, 3, 0:D3], AX.X, ALU.max))
                    i = dve.tensor_copy(NBC[:, 4:4 + D3], NBC[:, 0:1].to_broadcast([B, D3]))
                elif n == 2:
                    link(dve.tensor_copy(NRM[:, 4:4 + B], psum[0:D3, 3, 0:B]))
                    for s in range(2):
                        j = dve.tensor_tensor(MK[:, s, :, :], NRM[:, 4:4 + B].unsqueeze(2).to_broadcast([D3, B, SQUARINGS]),
                                              THR[:, :].unsqueeze(1).to_broadcast([D3, B, SQUARINGS]), ALU.is_gt)
                    link(j)
                    link(dve.tensor_scalar(MKH[:, :, :], MK[:, 0, :, :], -0.5, 1.0, ALU.mult, ALU.add))
                    link(dve.tensor_reduce(NRM[:, 8:8 + B], MKH[:, :, :], AX.X, ALU.mult))
                    for s in range(2):
                        j = dve.tensor_tensor(AS[:, s, :, :], AS[:, s, :, :], NRM[:, 8:8 + B].unsqueeze(2).to_broadcast([D3, B, D3]), ALU.mult)
                    link(j)
                    i = dve.scalar_tensor_tensor(RR[:, :, :, :].rearrange(flat), AS[:, :, :, :].rearrange(flat), 1.0 / TAYLOR, ID8[:, :, :], ALU.mult, ALU.add)
                elif n < 3 + TAYLOR - 1:
                    j = TAYLOR - 1 - (n - 3)
                    i = dve.scalar_tensor_tensor(RR[:, :, :, :].rearrange(flat), p8, 1.0 / j, ID8[:, :, :], ALU.mult, ALU.add)
                else:
                    k = n - (3 + TAYLOR - 1)
                    mask = MK[:, :, :, k].rearrange("p s b -> p (s b)").unsqueeze(2).to_broadcast([D3, 8, D3]).bitcast(I32)
                    i = dve.copy_predicated(RR[:, :, :, :].rearrange(flat), mask, p8)
                    if n == EXPM_STEPS - 1:
                        link(i)
                        i = dve.tensor_tensor(RR[:, 0, :, :], RR[:, 0, :, :], ID8[:, 0:B, :], ALU.subtract)
                i.then_inc(s_pv, 1)

            def u_step(n):
                dve.wait_ge(s_pp, EXPM_STEPS + n + 1)
                o = psum[0:D3, 3, 0:D3]
                o2 = psum[0:D3, 3, D3:2 * D3]
                eye = IDN[0:D3, 0:D3]
                if n == 0:
                    link(dve.memset(ET[:, :], 0.0))
                    dve.tensor_copy(ET[:, 0:D3], eye)
                    link(dve.tensor_tensor(NW[:, 5, :], o, SU[:, :], ALU.mult))
                    dve.tensor_tensor(NW[:, 0, :], NW[:, 5, :], eye, ALU.add)
                    i = dve.tensor_tensor(NW[:, 2, :], eye, NW[:, 5, :], ALU.subtract)
                elif n == 1:
                    i = dve.tensor_copy(VTR[:, :], psum[0:D3, 3, 0:C])
                elif n == 2:
                    link(dve.tensor_copy(NW[:, 1, :], o))
                    i = dve.scalar_tensor_tensor(NW[:, 3, :], eye, 2.0, NW[:, 1, :], ALU.mult, ALU.subtract)
                elif n < 3 + 12:
                    if n % 2 == 1:
                        i = dve.scalar_tensor_tensor(NW[:, 4, :], eye, 2.0, o, ALU.mult, ALU.subtract)
                    else:
                        dve.tensor_copy(NW[:, 2, :], o)
                        i = dve.tensor_copy(NW[:, 3, :], o2)
                elif n == 15:
                    i = dve.tensor_copy(NW[:, 5, :], o)
                elif n == 16:
                    i = dve.tensor_tensor(UTT[:, :], ET[:, :], psum[0:D3, 3, 0:C], ALU.subtract)
                else:
                    dve.tensor_copy(UU[:, 0:KC, :], psum[:, 3, 0:KC * D3].rearrange("p (c d) -> p c d", d=D3))
                    i = dve.tensor_copy(UU[0:TAIL, KC, :], psum[0:TAIL, 3, KC * D3:(KC + 1) * D3])
                i.then_inc(s_pv, 1)

            dve.memset(ONE[:, :], 1.0)
            dve.memset(UO[:, :, :], 0.0)
            dve.memset(SC[96:97, :, :], 1.0)
            dve.memset(XT[T3:TB, :].bitcast(F32), 1.0).then_inc(s_cst, 1)
            dve.wait_ge(s_sce, 1)
            link(dve.tensor_scalar(SCT[:, 0, :], SCT[:, 0, :], 1.0, None, ALU.add))
            link(dve.reciprocal(SCT[:, 1, :], SCT[:, 0, :]))
            sc = SC[0:96, :, :].rearrange("p k b -> p (k b)")
            dve.tensor_tensor(sc, sc, SCT[:, 1, :], ALU.mult).then_inc(s_sc, 2)
            for b in range(B):
                dve.wait_ge(s_x, 16 * B)
                stats(b)
            mods(0)

            for l in range(LAYERS):
                rstd()
                normalise(l, 0, 0)
                normalise(l, 0, 1)
                split_lo(("q", l), RAWQ, WQH, WQL, WQT)
                split_lo(("p", l), RAWP, WPH, WPL, WPT)
                low(l, 0, 0)
                low(l, 0, 1)
                normalise(l, 0, 2)
                qkv(l, 0)
                low(l, 0, 2)
                normalise(l, 0, 3)
                qkv(l, 1)
                low(l, 0, 3)
                qkv(l, 2)
                qkv(l, 3)
                dve.wait_ge(s_v, NT * (l + 1))
                link(dve.memset(VST[:, :, :, :, HD:32], 0.0))
                link(dve.memset(VST[:, :, :, :, HD:HD + 1], 1.0))
                for g in range(2):
                    for u in range(8):
                        row_max(l, 0, g, u)
                    if g == 0:
                        stage(l, 0, 0)
                with dve.Fori(0, B - 1) as bb:
                    attention(l, bb, False)
                attention(l, B - 1, True)
                if l + 1 < LAYERS:
                    mods(l + 1)
                o_rows(l, 0)
                o_rows(l, 1)
                low(l, 1, 0)
                attn_residual(l, 0)
                o_rows(l, 2)
                low(l, 1, 1)
                attn_residual(l, 1)
                o_rows(l, 3)
                low(l, 1, 2)
                attn_residual(l, 2)
                low(l, 1, 3)
                attn_residual(l, 3)
                rstd()
                for b in range(B):
                    normalise(l, 2, b)
                    low(l, 2, b)
                    if b == 0:
                        split_lo(("1", first_set(l)), RAW1, W1H, W1L, W1T)
                        split_lo(("2", first_set(l)), RAW2, W2H, W2L, None)
                if l == 0:
                    dve.wait_ge(s_ce, 1)
                    dve.tensor_tensor(WGL[:, :, :], WGR[:, 0:KC, :], WGH[:, :, :].bitcast(F32), ALU.subtract)
                    dve.tensor_tensor(WGT[TAIL:2 * TAIL, :], WGR[TAIL:2 * TAIL, KC, :], WGT[TAIL:2 * TAIL, :].bitcast(F32), ALU.subtract).then_inc(s_wl2, 1)
                    gates()
                for f in sets_of(l):
                    for u in range(UNITS):
                        hidden_parts(f, u)
                        if u >= HM and u % HM == 1:
                            ffn_take(f, u // HM - 1)
                        if u >= HM and u % HM == 3:
                            ffn_add(f, u // HM - 1)
                        if f == V_SET and u < 2 * VT_:
                            skew_entries(u)
                        if f == EXPM_SET and u < EXPM_STEPS:
                            expm_step(u)
                        if f == U_SET and u < U_STEPS:
                            u_step(u)
                    if f != sets_of(l)[-1]:
                        split_lo(("1", f + 1), RAW1, W1H, W1L, W1T)
                        ffn_take(f, B - 1)
                        split_lo(("2", f + 1), RAW2, W2H, W2L, None)
                    else:
                        ffn_take(f, B - 1)
                    ffn_add(f, B - 1)

            for b in range(B):
                for t in range(TT):
                    i = TT * b + t
                    dve.wait_ge(s_zo, i + 1)
                    dve.tensor_tensor(XR[:, i, :], XR[:, i, :], psum[:, 5 + i % 2, 0:C], ALU.add).then_inc(s_fin, 1)


EXPM_STEPS = 3 + TAYLOR - 1 + SQUARINGS
U_STEPS = 18


_L = [dict(ada_w="L0_cond_w_adaln", ada_b="L0_cond_b_adaln", qkv_w="L0_cond_w_qkv", qkv_b="L0_cond_b_qkv",
           out_w="L0_cond_w_proj", out_b="L0_cond_b_proj", w_gate="L0_cond_w_gate", w1="L0_cond_w1", b1="L0_cond_b1",
           w2="L0_cond_w2", b2="L0_cond_b2"),
      dict(ada_w="L1_cond_ada_w", ada_b="L1_cond_ada_b", qkv_w="L1_cond_qkv_w", qkv_b="L1_cond_qkv_b",
           out_w="L1_cond_out_w", out_b="L1_cond_out_b", w1="L1_cond_w1", b1="L1_cond_b1", w2="L1_cond_w2", b2="L1_cond_b2"),
      dict(ada_w="L2_cond_W_ada", ada_b="L2_cond_b_ada", qkv_w="L2_cond_W_qkv", qkv_b="L2_cond_b_qkv",
           out_w="L2_cond_W_proj", out_b="L2_cond_b_proj", w1="L2_cond_W_fc1", b1="L2_cond_b_fc1", w2="L2_cond_W_fc2", b2="L2_cond_b_fc2")]


def kernel(**inputs):
    import numpy as np
    import concourse.bacc as bacc
    from concourse import mybir as mb
    from concourse.bass_utils import run_bass_kernel_spmd as run

    nc = bacc.Bacc("TRN2", target_bir_lowering=False, num_devices=1)
    arrays, aps = {}, {}
    for name, a in inputs.items():
        a = np.ascontiguousarray(a)
        arrays[f"in_{name}"] = a
        aps[name] = nc.dram_tensor(f"in_{name}", a.shape, mb.dt.from_np(a.dtype), kind="ExternalInput").ap()
    out = nc.dram_tensor("out", inputs["x"].shape, mb.dt.float32, kind="ExternalOutput").ap()
    layers = [{k: aps[v] for k, v in d.items()} for d in _L]
    build(nc, aps["x"], aps["cond_1152"], layers, aps["L3_cond_P"], aps["L3_cond_W"], aps["L3_cond_b"], out)
    r = run(nc, [arrays], core_ids=[0])
    return r.results[0]["out"]
```

```python
import concourse.bass as bass
from concourse import mybir
from contextlib import ExitStack

F32 = mybir.dt.float32
F32R = mybir.dt.float32r
BF16 = mybir.dt.bfloat16
I32 = mybir.dt.int32
ALU = mybir.AluOpType
ACT = mybir.ActivationFunctionType
AX = mybir.AxisListType
ADD = bass.bass_isa.ReduceOp.add

B, N, C = 4, 512, 288
TOK = B * N
HEADS, HD = 16, 18
HID = 4 * C
EXPERTS = 4
LAYERS = 3
P = 128
TT = N // P
NT = TOK // P
KC = C // P
TAIL = C - KC * P
T3 = 3 * TAIL
TB = T3 + 2
HG = HEADS // 4
QM = C // 96
HM = HID // P
STK = 6 * HD
PART_RUNS = [(0, 0, 3), (3, 1, 2), (5, 2, 1)]
XNW = KC * P + T3
SETS = [(0, e) for e in range(EXPERTS)] + [(1, 0), (2, 0)]
UNITS = B * HM
LN_EPS = 1e-6
SCALE = float(HD) ** -0.5
D3 = 64
SKEW = D3 * (D3 - 1) // 2
VP = 126
VT_ = SKEW // VP
TAYLOR = 11
SQUARINGS = 16
QR_OPS = 24
RSQRT_MAGIC = 1597463007.0
TINY = 1e-37
NEWTON = 3
CHUNK_BANK = (2, 3, 3)
QK_BANK = (0, 1, 7)
V_SET, EXPM_SET, U_SET = 1, 2, 5
EXPM_UNIT, U_UNIT = 15, UNITS - HM
PARTS = 5
O_STEPS = 11
NEXT_UNIT = (25, 27, 32)
TAIL_STEPS = {(2, 3): 0, (2, 6): 1, (3, 1): 2, (3, 4): 3, (3, 6): 4}
P_UNIT = 31
W1_UNIT = 8 - O_STEPS
FIRST = len(TAIL_STEPS) - O_STEPS


def build(nc, x, cond, layers, l3_P, l3_W, l3_b, out):
    ctx = ExitStack()
    with ctx:
        BASE = (nc.sbuf_base + 31) // 32 * 32
        top = [BASE]

        def at(name, shape, dt, offset):
            return nc.alloc_sbuf_tensor_at(name, shape, dt, offset=offset)

        def new(name, shape, dt):
            size = 2 if dt == BF16 else 4
            for n in shape[1:]:
                size *= n
            t = at(name, shape, dt, top[0])
            top[0] += (size + 31) // 32 * 32
            return t

        def region(size):
            top[0] += size
            return top[0] - size

        XR = new("residual", [P, NT, C], F32)
        xo = region(2 * KC * TOK * 4)
        XS = at("x_split", [P, B, 2, KC, N], F32R, xo)
        OT = at("o_t", [P, B * HG, N], F32, xo)
        XT = new("x_tail", [TB, TOK], F32R)

        ra = region(32768)
        Q6 = at("q_stack", [STK + 1, HG, 4, N], BF16, ra)
        K6 = at("k_stack", [STK + 1, HG, 4, N], BF16, ra + 16384)
        XN = [at("x_norm0", [P, TT, XNW], F32, ra), at("x_norm1", [P, TT, XNW], F32, ra + 9728)]
        OH_ = at("o_hi", [P, KC, N], F32R, ra + 5632)
        FX = at("x_mod", [P, KC + 1, N], F32, ra + 16384)
        OL = at("o_lo", [P, KC, N], F32R, ra + 22528)
        OX = at("o_tail", [TB, N], F32R, ra + 26624)
        QR = at("qk_r", [96, 3, N], F32, ra + 22528)
        HF = at("hid_f", [P, 2, N], F32, ra + 28672)
        L3W = at("l3_w", [VP, VT_, C], F32, ra)
        SCB = at("silu_c_all", [P, B, C], F32, ra + 18432)
        L3J = at("l3_junk", [VP, C], F32, ra + 23040)
        UT0 = ra
        ID8 = at("ident8", [D3, 8, D3], F32, UT0)
        AS = at("skew_pm", [D3, 2, B, D3], F32, UT0 + 2048)
        NRM = at("skew_norm", [D3, 16], F32, UT0 + 4096)
        NBC = at("norm_rows", [B, 4 + D3], F32, UT0 + 4160)
        MK = at("sq_mask", [D3, 2, B, SQUARINGS], F32, UT0 + 4448)
        MKH = at("sq_half", [D3, B, SQUARINGS], F32, UT0 + 4960)
        THR = at("sq_thr", [D3, SQUARINGS], F32, UT0 + 5216)
        NW = at("wy", [D3, 8, D3], F32, UT0)
        VTR = at("v_t", [D3, C], F32, UT0 + 2048)
        ET = at("e_t", [D3, C], F32, UT0 + 3200)

        rb = region(59392)
        PE_ = at("probs", [P, TT, 4, N], F32, rb)
        VST = at("v_stage", [P, HG, TT, 4, 32], F32, rb + 32768)
        V = at("v", [P, NT, C], F32, rb + 40960)
        WQH = at("wqkv_hi", [P, KC, 3 * C], F32R, rb)
        WQL = at("wqkv_lo", [P, KC, 3 * C], F32R, rb + 6912)
        WQT = at("wqkv_tail", [TB, 3 * C], F32R, rb + 13824)
        PT = at("qk_parts", [96, PARTS, 3, N], BF16, rb + 17408)
        W1H = at("w1_hi", [P, KC, HID], F32R, rb)
        W1L = at("w1_lo", [P, KC, HID], F32R, rb + 9216)
        W1T = at("w1_tail", [TB, HID], F32R, rb + 18432)
        W2H = at("w2_hi", [P, HM, C], F32R, rb + 23040)
        W2L = at("w2_lo", [P, HM, C], F32R, rb + 33408)
        TA = at("attn_branch", [P, 2, C], F32, rb + 56064)
        HH = at("hid_hi", [P, 3, N], F32R, rb + 43776)
        HL = at("hid_lo", [P, 3, N], F32R, rb + 49920)

        RAWA = new("raw_a", [P, 3 * HID], F32)
        RAWB = new("raw_b", [P, HM * C], F32)
        ADA0 = [at(f"ada0_{h}", [P, 3, 3 * C], F32, rb + 17408 + 10368 * h) for h in range(2)]
        ADA = [RAWA[:, 0:9 * C].rearrange("p (k n) -> p k n", k=3), RAWB[:, :].rearrange("p (k n) -> p k n", k=3)]
        RAWQ = RAWA[:, 0:9 * C].rearrange("p (k n) -> p k n", k=3)
        RAW1 = RAWA[:, :].rearrange("p (k n) -> p k n", k=3)
        RAWP = RAWB[:, 0:3 * C].rearrange("p (k n) -> p k n", k=3)
        RAW2 = RAWB[:, :].rearrange("p (k n) -> p k n", k=HM)
        WPH = new("wproj_hi", [P, KC, C], F32R)
        WPL = new("wproj_lo", [P, KC, C], F32R)
        WPT = new("wproj_tail", [TB, C], F32R)
        GMSA = new("gate_msa", [P, B, C], F32)
        GMLP = new("gate_mlp", [P, B, C], F32)
        B2B = new("b2_rows", [P, 2, C], F32)
        T1 = new("branch", [P, TT, C], F32)
        GROW = at("gate_rows", [B, 2, C], F32, top[0] - TT * C * 4)
        MODC = new("mod_cols", [P, LAYERS, 4, KC + 1, B], F32)
        MV = new("ln_stats", [P, NT, 2], F32)
        BN6 = new("bn6", [P, TT, 6], F32)
        RST = new("rstd", [P, NT], F32)
        NWT = new("newton", [P, 3, NT], F32)
        RC = new("recip", [P, HEADS], F32)
        MX = new("row_max", [P, 2, 16], F32)
        MXT = new("row_max_t", [16, 2, P], BF16)
        ONE = new("ones_bf", [16, HG, P], BF16)
        SC = new("silu_c", [97, 3, B], F32)
        SCT = new("silu_tmp", [96, 2, 3 * B], F32)
        IDN = new("ident", [P, P], F32)
        WGR = new("wgate_raw", [P, KC + 1, EXPERTS], F32)
        WGH = new("wgate_hi", [P, KC, EXPERTS], F32R)
        WGL = new("wgate_lo", [P, KC, EXPERTS], F32R)
        WGT = new("wgate_tail", [T3, EXPERTS], F32R)
        LG = new("logits", [P, NT, EXPERTS], F32)
        RK = new("rank", [P, NT, EXPERTS], F32)
        CMP = new("compare", [P, NT], F32)
        CW = new("expert_w", [P, NT, EXPERTS], F32)
        QA = new("qr_a", [96, 3, D3], F32)
        QV = new("qr_v", [96, 3, D3], F32)
        QG = new("qr_rows_ge", [96, 3, D3], F32)
        QO = new("qr_onehot", [96, D3], F32)
        QM1 = new("qr_m", [96, 3, D3], F32)
        MHALF = new("minus_half", [P, TT], F32)
        QI = new("qr_in", [96, 2, D3], F32)
        QS = new("qr_sums", [96, 2, D3], F32)
        QC = new("qr_cols", [96, 24], F32)
        QW = new("qr_w", [96, D3], F32)
        UO = new("skew_upper", [D3, B, D3], F32)
        RR = new("rot", [D3, 2, B, D3], F32)
        VC = new("skew_col", [VP, B, VT_], F32)
        BL = new("skew_bias", [VP, VT_], F32)
        SU = new("strict_upper", [D3, D3], F32)
        UU = new("u", [P, 3, D3], F32)
        UTT = new("u_t", [D3, C], F32)
        ZT = at("z_t", [D3, 2, N], F32, ra + 22528)
        assert top[0] <= nc.sbuf_usable_end, (top[0], nc.sbuf_usable_end)

        psum = ctx.enter_context(nc.psum_tensor("psum", [P, 8, 512], F32))

        def bk(i):
            return psum[:, i, :]

        QKD = [nc.dram_tensor(f"qk_parts_d{l}", [2, 3, B, C, N], BF16, kind="Internal").ap() for l in range(LAYERS)]
        ONED = nc.dram_tensor("ones_d", [HG, 16, P], BF16, kind="Internal").ap()
        GD = [nc.dram_tensor(f"gates_d{l}", [2, B, C], F32, kind="Internal").ap() for l in range(LAYERS)]
        VD = nc.dram_tensor("skew_d", [B, SKEW], F32, kind="Internal").ap()
        SCD = nc.dram_tensor("silu_d", [B, C], F32, kind="Internal").ap()

        def sem(name):
            return ctx.enter_context(nc.semaphore(name))

        s_x = [sem(f"x_loaded{b}") for b in range(B)]
        s_in = sem("cond_loaded")
        s_ra = sem("raw_a_loaded")
        s_rb = sem("raw_b_loaded")
        s_wg = sem("wgate_loaded")
        s_cst = sem("constants_made")
        s_sce = sem("exp_of_minus_c")
        s_sc = sem("silu_made")
        s_mod = sem("mod_products")
        s_gr = sem("gate_rows_copied")
        s_gd = sem("gate_rows_stored")
        s_gm = sem("gate_msa_loaded")
        s_gl = sem("gate_mlp_loaded")
        s_mc_ = sem("mod_cols_made")
        s_wsp = sem("weight_hi_made")
        s_wl = sem("weight_lo_made")
        s_dv = sem("vector_steps")
        s_xn = sem("x_normalised")
        s_tr = sem("x_transposed")
        s_fx = sem("x_modulated")
        s_hi = sem("x_hi_made")
        s_lo = sem("x_lo_made")
        s_qk = sem("qk_products")
        s_p1 = sem("qk_part0")
        s_r1 = sem("qk_rest")
        s_p2 = sem("qk_part1")
        s_p3 = sem("qk_part2")
        s_pd = [sem(f"qk_parts_stored{i}") for i in range(PARTS)]
        s_vm = sem("v_products")
        s_v = sem("v_copied")
        s_one = sem("ones_stored")
        s_or = sem("ones_row_loaded")
        s_ld = [sem(f"stacks_loaded{g}") for g in range(HG)]
        s_s = sem("scores_for_max")
        s_mx = sem("row_max_made")
        s_mt = sem("row_max_turned")
        s_mc = sem("row_max_copied")
        s_mr = [sem(f"row_max_placed{g}") for g in range(2)]
        s_vs = sem("v_staged")
        s_st = sem("scores_t")
        s_e = sem("probs_made")
        s_av = sem("probs_used")
        s_ot = sem("o_t_copied")
        s_to = sem("o_turned")
        s_on = sem("o_normalised")
        s_pj = sem("proj_products")
        s_dvp = sem("proj_copied")
        s_xa = sem("attention_added")
        s_ms = sem("row_moments_made")
        s_rs = sem("rstd_made")
        s_xr = sem("ffn_added")
        s_wl2 = sem("wgate_split")
        s_lg = sem("gate_logits")
        s_lc = sem("gate_logits_copied")
        s_cw = sem("expert_logits_shifted")
        s_ce = sem("expert_exp")
        s_f1 = sem("hidden_products")
        s_g = sem("gelu_made")
        s_h = sem("hidden_lo_made")
        s_h2 = sem("hidden_used")
        s_f2 = sem("ffn_products")
        s_ev = sem("ffn_copied")
        s_b2 = [sem(f"b2_loaded{i}") for i in range(2)]
        s_scd = sem("silu_stored")
        s_l3 = sem("l3_loaded")
        s_vc = sem("skew_made")
        s_vd = sem("skew_stored")
        s_uo = sem("skew_placed")
        s_p = sem("p_loaded")
        s_qr = sem("qr_steps")
        s_pace = sem("qr_pace")
        s_pp = sem("l3_products")
        s_pv = sem("l3_copied")
        s_zt = sem("last_turned")
        s_zf = sem("last_x_copied")
        s_zp = sem("last_z_products")
        s_zc = sem("last_z_copied")
        s_zo = sem("last_products")
        s_fin = sem("last_added")
        s_out = sem("stored")

        LOAD = 16 * 2 * len(PART_RUNS)
        QR_END = 9 + D3 * QR_OPS

        def tn(l, s, b):
            return 12 * l + (b if s == 0 else 3 + s + 2 * b)

        def add_unit(u):
            return 6 if u < UNITS - HM else 2

        POOL_NORMS = [(1, 0, b) for b in range(B)]
        for l in range(1, LAYERS):
            due = [(HM * b + 6 - O_STEPS, (l, 2, b)) for b in range(B)]
            if l + 1 < LAYERS:
                due += [(HM * (b + 1) + add_unit(HM * (b + 1)), (l + 1, 0, b)) for b in range(B - 1)] + [(UNITS, (l + 1, 0, B - 1))]
            POOL_NORMS += [norm for _, norm in sorted(due)]

        def first_set(l):
            return 0 if l == 0 else EXPERTS + l - 1

        def sets_of(l):
            return [f for f, (a, _) in enumerate(SETS) if a == l]

        def steps_of(l):
            return UNITS * len(sets_of(l))

        def split_pieces(l, j):
            f, u = first_set(l) + j // UNITS, j % UNITS
            pieces, more = [], f != sets_of(l)[-1]
            if more and u >= UNITS - HM:
                pieces.append(("1", f + 1, u - (UNITS - HM)))
            if more and u >= UNITS - HM + 3:
                pieces.append(("2", f + 1, u - (UNITS - HM + 3)))
            if f != first_set(l) and u < 3:
                pieces.append(("2", f, HM - 3 + u))
            return pieces

        events = []
        for l in range(LAYERS):
            events += [("q", l, i) for i in range(3 * (KC + 1))] + ([("p", l)] if l == 0 else [])
            events += [("1", first_set(l)), ("2", first_set(l))]
            for j in range(steps_of(l)):
                events += split_pieces(l, j)
            if l + 1 < LAYERS:
                events.append(("p", l + 1))
        split_no = {k: i for i, k in enumerate(events)}

        def split_done(kind, f, m):
            return split_no[(kind, f, m) if (kind, f, m) in split_no else (kind, f)] + 1

        def loads(order):
            total, res = 0, {}
            for key, n in order:
                total += 16 * n
                res[key] = total
            return res

        order_a, order_b = [(("a", 0), 2)], [(("a", 0), 2)]
        for l in range(LAYERS):
            order_a.append((("q", l), 6))
            order_b.append((("p", l), 6))
            if l + 1 < LAYERS:
                order_a.append((("a", l + 1), 2))
                order_b.append((("a", l + 1), 2))
            for f in sets_of(l):
                order_a.append((("1", f), 6))
                order_b.append((("2", f), 1))
        RA, RB = loads(order_a), loads(order_b)

        def split_terms(H, L, T, XHi, XLo, XTa, wc, xc, tail):
            terms = []
            for c in range(KC):
                terms += [(H[:, c, wc], XHi[:, c, xc]), (L[:, c, wc], XHi[:, c, xc]), (H[:, c, wc], XLo[:, c, xc])]
            return terms + [(T[0:tail, wc], XTa[0:tail, xc])]

        def ada(l):
            return ADA0 if l == 0 else ADA

        QKV_CHUNKS = [(RAWQ[:, c, :], WQH[:, c, :]) for c in range(KC)] + [(RAWQ[0:TB, KC, :], WQT[:, :])]

        def qkv_cols(w, i, by_channel):
            cols = w[:, C * i:C * (i + 1)]
            if i == 2:
                return cols
            if by_channel:
                return cols.rearrange("p (g d h) -> p g d h", g=HG, h=4)
            return cols.rearrange("p (g h d) -> p g d h", g=HG, d=HD)

        block = ctx.enter_context(nc.Block())

        @block.sync
        def _(sp):
            x_v = x.rearrange("b (t p) c -> b p t c", p=P)

            def load_k288(dst, w, bias, s):
                sp.dma_start(dst[:, 0:KC, :], w[0:KC * P, :].rearrange("(k p) n -> p k n", p=P)).then_inc(s, 16)
                for r in range(3):
                    sp.dma_start(dst[r * TAIL:(r + 1) * TAIL, KC, :], w[KC * P:C, :]).then_inc(s, 16)
                for r in range(2):
                    sp.dma_start(dst[T3 + r:T3 + r + 1, KC, :], bias.unsqueeze(0)).then_inc(s, 16)

            def load_ada(l, h):
                cols, s = slice(3 * C * h, 3 * C * (h + 1)), (s_ra, s_rb)[h]
                dst = ada(l)[h]
                sp.dma_start(dst[0:96, :, :], layers[l]["ada_w"][:, cols].rearrange("(k p) n -> p k n", p=96)).then_inc(s, 16)
                sp.dma_start(dst[96:97, 0, :], layers[l]["ada_b"][cols].unsqueeze(0)).then_inc(s, 16)

            def ffn_weights(f):
                l, e = SETS[f]
                w = layers[l]
                if l == 0:
                    return w["w1"][e], w["b1"][e], w["w2"][e], w["b2"][e]
                return w["w1"], w["b1"], w["w2"], w["b2"]

            def load_w1(f):
                w1, b1, _, _ = ffn_weights(f)
                load_k288(RAW1, w1, b1, s_ra)

            def load_w2(f):
                _, _, w2, b2 = ffn_weights(f)
                sp.dma_start(RAW2, w2.rearrange("(k p) n -> p k n", p=P)).then_inc(s_rb, 16)
                sp.dma_start(B2B[:, f % 2, :], b2.partition_broadcast(P)).then_inc(s_b2[f % 2], 16)

            def store_gates(l):
                sp.wait_ge(s_gr, 2 * (l + 1))
                sp.dma_start(GD[l].rearrange("g b c -> b g c"), GROW[:, :, :]).then_inc(s_gd, 16)

            def load_gate(l, g):
                sp.wait_ge(s_gd, 16 * (l + 1))
                sp.dma_start((GMSA, GMLP)[g][:, :, :], GD[l][g].partition_broadcast(P)).then_inc((s_gm, s_gl)[g], 16)

            with nc.allow_non_contiguous_dma("columns of the condition"):
                for k in range(3):
                    sp.dma_start(SC[0:96, k, :], cond[:, 96 * k:96 * k + 96].rearrange("b p -> p b")).then_inc(s_in, 16)
            for h in range(2):
                load_ada(0, h)
            for b in range(B):
                sp.dma_start(XR[:, TT * b:TT * b + TT, :], x_v[b]).then_inc(s_x[b], 16)
                if b == 1:
                    sp.wait_ge(s_ra, RA["a", 0])
                    load_k288(RAWQ, layers[0]["qkv_w"], layers[0]["qkv_b"], s_ra)
            sp.dma_start(QA[:, :, :], l3_P.rearrange("(k p) d -> p k d", p=96)).then_inc(s_p, 16)
            wg = layers[0]["w_gate"]
            with nc.allow_non_contiguous_dma("narrow gate weight"):
                sp.dma_start(WGR[:, 0:KC, :], wg[0:KC * P, :].rearrange("(k p) n -> p k n", p=P)).then_inc(s_wg, 16)
                for r in range(3):
                    sp.dma_start(WGR[r * TAIL:(r + 1) * TAIL, KC, :], wg[KC * P:C, :]).then_inc(s_wg, 16)
            sp.wait_ge(s_cst, 2)
            sp.dma_start(ONED.rearrange("g a p -> a g p"), ONE[:, :, :]).then_inc(s_one, 16)
            sp.wait_ge(s_rb, RB["a", 0])
            load_k288(RAWP, layers[0]["out_w"], layers[0]["out_b"], s_rb)
            store_gates(0)
            load_gate(0, 0)
            load_gate(0, 1)
            sp.wait_ge(s_sc, 2)
            with nc.allow_non_contiguous_dma("columns of the condition"):
                for k in range(3):
                    sp.dma_start(SCD[:, 96 * k:96 * k + 96].rearrange("b p -> p b"), SC[0:96, k, :]).then_inc(s_scd, 16)

            for l in range(LAYERS):
                if l + 1 < LAYERS:
                    sp.wait_ge(s_wl, split_no["q", l, 3 * (KC + 1) - 1] + 1)
                    load_ada(l + 1, 0)
                for b in range(B):
                    for m in range(2 * QM):
                        i = 2 * QM * (B * l + b) + m
                        sp.wait_ge(s_p3, i + 1)
                        sp.dma_start(QKD[l][m // QM, :, b, 96 * (m % QM):96 * (m % QM) + 96, :].rearrange("a p t -> p a t"),
                                     PT[:, i % PARTS, :, :]).then_inc(s_pd[i % PARTS], 16)
                    if l == 0 and b == 1:
                        sp.wait_ge(s_wl, split_no["p", 0] + 1)
                        load_ada(1, 1)

                def load_stacks(bb, g):
                    for j, q, count in PART_RUNS:
                        place = slice(HD * j, HD * (j + count))
                        rows = [QKD[l][w, :, bass.ds(bb, 1), 4 * HD * g:4 * HD * (g + 1), :].rearrange("a o (d h) t -> a (o d) (h t)", h=4) for w in range(2)]
                        sp.dma_start(Q6[place, g, :, :].rearrange("p h t -> p (h t)"), rows[0][q:q + 1].to_broadcast([count, HD, 4 * N])).then_inc(s_ld[g], 16)
                        sp.dma_start(K6[place, g, :, :].rearrange("p h t -> p (h t)"), rows[1][0:count]).then_inc(s_ld[g], 16)

                def place_max(bb, g):
                    sp.wait_ge(s_mc, 16 * l + 4 * bb + g + 1)
                    sp.dma_start(Q6[STK:STK + 1, g, :, :].rearrange("o h n -> o (h n)").rearrange("o (r p) -> o r p", p=P),
                                 MXT[:, g % 2, :]).then_inc(s_mr[g % 2], 16)

                tiles = 2 * QM * B * (l + 1)
                for i in range(PARTS):
                    sp.wait_ge(s_pd[i], 16 * ((tiles - i + PARTS - 1) // PARTS))
                sp.wait_ge(s_one, 16)
                sp.wait_ge(s_tr, 3 * tn(l, 1, 0))
                sp.wait_ge(s_lo, tn(l, 1, 0))
                for g in range(3):
                    load_stacks(0, g)
                    if g == 0:
                        sp.dma_start(K6[STK:STK + 1, :, :, :], ONED.rearrange("g a p -> (g a p)").rearrange("(o g h n) -> o g h n", o=1, g=HG, h=4)).then_inc(s_or, 16)
                f0 = first_set(l)
                if l + 1 < LAYERS:
                    store_gates(l + 1)
                    sp.wait_ge(s_mod, l + 2)
                else:
                    sp.wait_ge(s_wl, split_no["p", l] + 1)
                place_max(0, 0)
                load_w1(f0)
                if f0 >= 2:
                    sp.wait_ge(s_ev, 16 * (f0 - 1))
                load_w2(f0)

                def attention_loads(bb, last):
                    for g in range(HG):
                        if not (last and g >= 1):
                            sp.wait_ge(s_st, 256 * l + 16 * (4 * bb + g) + 1)
                            load_stacks(bb + (g + 3) // 4, (g + 3) % 4)
                        if not (last and g == 3):
                            place_max(bb + (g + 1) // 4, (g + 1) % 4)

                with sp.Fori(0, B - 1) as bb:
                    attention_loads(bb, False)
                attention_loads(B - 1, True)

                for f in sets_of(l):
                    last = f == sets_of(l)[-1]
                    sp.wait_ge(s_wl, split_done("1", f, HM - 1))
                    if not last:
                        load_w1(f + 1)
                    elif l + 1 < LAYERS:
                        load_k288(RAWQ, layers[l + 1]["qkv_w"], layers[l + 1]["qkv_b"], s_ra)
                    sp.wait_ge(s_wl, split_done("2", f, HM - 1))
                    if not last:
                        if f >= 1:
                            sp.wait_ge(s_ev, 16 * f)
                        load_w2(f + 1)
                    elif l + 1 < LAYERS:
                        load_k288(RAWP, layers[l + 1]["out_w"], layers[l + 1]["out_b"], s_rb)
                    if f == f0 and l + 1 < LAYERS:
                        sp.wait_ge(s_xa, NT * (l + 1))
                        load_gate(l + 1, 0)
                    if f == V_SET - 1:
                        sp.wait_ge(s_lo, tn(0, 2, B - 1) + 1)
                        sp.wait_ge(s_scd, 48)
                        sp.dma_start(L3W[:, :, :], l3_W.rearrange("(p t) c -> p t c", t=VT_)).then_inc(s_l3, 16)
                        sp.dma_start(SCB[:, :, :], SCD.partition_broadcast(P)).then_inc(s_l3, 16)
                        sp.dma_start(BL[:, :], l3_b.rearrange("(p t) -> p t", t=VT_)).then_inc(s_l3, 16)
                    if f == V_SET:
                        sp.wait_ge(s_vc, 1)
                        sp.dma_start(VD.rearrange("b (p t) -> p b t", t=VT_), VC[:, :, :]).then_inc(s_vd, 16)
                        sp.wait_ge(s_vd, 16)
                        with nc.allow_non_contiguous_dma("the last row has one entry"):
                            for i in range(D3 - 1):
                                o = i * (D3 - 1) - i * (i - 1) // 2
                                sp.dma_start(UO[i:i + 1, :, i + 1:D3], VD[:, o:o + D3 - 1 - i].unsqueeze(0)).then_inc(s_uo, 16)
                if l + 2 < LAYERS:
                    sp.wait_ge(s_wl, split_no["p", l + 1] + 1)
                    load_ada(l + 2, 1)
                if l + 1 < LAYERS:
                    sp.wait_ge(s_xr, NT * (sets_of(l)[-1] + 1))
                    load_gate(l + 1, 1)

            out_v = out.rearrange("b (t p) c -> b p t c", p=P)
            for b in range(B):
                sp.wait_ge(s_fin, TT * (b + 1))
                sp.dma_start(out_v[b], XR[:, TT * b:TT * b + TT, :]).then_inc(s_out, 16)
            sp.wait_ge(s_out, 16 * B)

        @block.gpsimd
        def _(gp):
            gp.memset(IDN[:, :], 0.0).then_inc(s_qr, 1)
            gp.memset(QG[:, :, :], 1.0).then_inc(s_qr, 1)
            gp.memset(QO[:, :], 0.0).then_inc(s_qr, 1)
            gp.memset(SU[:, :], 1.0).then_inc(s_qr, 1)
            gp.memset(QC[:, :], 0.5).then_inc(s_qr, 1)
            gp.memset(MHALF[:, :], -0.5).then_inc(s_qr, 1)
            gp.wait_ge(s_qr, 6)
            gp.affine_select(out=IDN[:, :], in_=IDN[:, :], compare_op=ALU.not_equal, fill=1.0, base=0,
                             pattern=[[-1, P]], channel_multiplier=1).then_inc(s_cst, 1)
            gp.affine_select(out=QG[:, :, :], in_=QG[:, :, :], compare_op=ALU.is_ge, fill=0.0, base=0,
                             pattern=[[96, 3], [-1, D3]], channel_multiplier=1).then_inc(s_qr, 1)
            gp.affine_select(out=QO[:, :], in_=QO[:, :], compare_op=ALU.not_equal, fill=1.0, base=0,
                             pattern=[[-1, D3]], channel_multiplier=1).then_inc(s_qr, 1)
            gp.affine_select(out=SU[:, :], in_=SU[:, :], compare_op=ALU.is_gt, fill=0.0, base=0,
                             pattern=[[1, D3]], channel_multiplier=-1).then_inc(s_qr, 1)
            gp.wait_ge(s_qr, 9)
            gp.wait_ge(s_p, 16)

            half, vcol, oneh, sal = QC[:, 0:1], QC[:, 1:4], QC[:, 4:5], QC[:, 5:7]
            nrm, sg, sn, t_, d_, rs = (QC[:, i:i + 1] for i in range(7, 13))
            ohs, ucol, mhalf = QC[:, 13:14], QC[:, 14:17], QC[:, 17:18]
            s_, al = QC[:, 5:6], QC[:, 6:7]

            with gp.Fori(0, D3) as k:
                done = [0]

                def step(i, pace=False):
                    i.then_inc(s_qr, 1)
                    done[0] += 1
                    gp.wait_ge(s_qr, 9 + QR_OPS * k + done[0])
                    if pace:
                        gp.sem_inc(s_pace, 1)

                kk = bass.ds(k, 1)
                step(gp.memset(mhalf, -0.5))
                step(gp.tensor_tensor(vcol, QA[:, :, kk].rearrange("p c o -> p (c o)"), QG[:, :, kk].rearrange("p c o -> p (c o)"), ALU.mult))
                step(gp.tensor_copy(oneh, QO[:, kk]))
                step(gp.tensor_tensor(QM1[:, :, :], QA[:, :, :], vcol.unsqueeze(2).to_broadcast([96, 3, D3]), ALU.mult))
                step(gp.tensor_tensor(QI[:, 0, :], QM1[:, 0, :], QM1[:, 1, :], ALU.add))
                step(gp.tensor_tensor(QI[:, 0, :], QI[:, 0, :], QM1[:, 2, :], ALU.add))
                step(gp.tensor_tensor(QI[:, 1, :], QA[:, 0, :], oneh.to_broadcast([96, D3]), ALU.mult), pace=True)
                step(gp.partition_all_reduce(QS[:, :, :].rearrange("p a d -> p (a d)"), QI[:, :, :].rearrange("p a d -> p (a d)"), channels=96, reduce_op=ADD))
                step(gp.tensor_copy(sal, QS[:, :, kk].rearrange("p a o -> p (a o)")))
                step(gp.tensor_tensor(nrm, s_, half, ALU.pow), pace=True)
                step(gp.tensor_scalar(sg, al, 0.0, 2.0, ALU.is_ge, ALU.mult), pace=True)
                step(gp.tensor_scalar(sn, sg, -1.0, nrm, ALU.add, ALU.mult))
                step(gp.tensor_tensor(t_, al, sn, ALU.mult), pace=True)
                step(gp.tensor_scalar(d_, t_, s_, TINY, ALU.add, ALU.max))
                step(gp.tensor_tensor(rs, d_, mhalf, ALU.pow), pace=True)
                step(gp.tensor_scalar(QW[:, :], QS[:, 1, :], sn, rs, ALU.mult, ALU.mult), pace=True)
                step(gp.tensor_scalar(QI[:, 0, :], QS[:, 0, :], rs, 1.0, ALU.mult, ALU.mult))
                step(gp.tensor_tensor(QW[:, :], QW[:, :], QI[:, 0, :], ALU.add))
                step(gp.tensor_tensor(ohs, oneh, sn, ALU.mult))
                step(gp.tensor_tensor(vcol[:, 0:1], vcol[:, 0:1], ohs, ALU.add))
                step(gp.tensor_tensor(ucol, vcol, rs.to_broadcast([96, 3]), ALU.mult))
                step(gp.tensor_copy(QV[:, :, kk].rearrange("p c o -> p (c o)"), ucol))
                step(gp.tensor_tensor(QM1[:, :, :], ucol.unsqueeze(2).to_broadcast([96, 3, D3]), QW[:, :].unsqueeze(1).to_broadcast([96, 3, D3]), ALU.mult))
                step(gp.tensor_tensor(QA[:, :, :], QA[:, :, :], QM1[:, :, :], ALU.subtract))
                assert done[0] == QR_OPS

            for n, (l, s, b) in enumerate(POOL_NORMS):
                tiles = slice(TT * b, TT * b + TT)
                gp.wait_ge(s_ms, n + 1)
                gp.tensor_scalar(RST[:, tiles], MV[:, tiles, 1], LN_EPS, 1.0, ALU.add, ALU.mult).then_inc(s_rs, 1)
                gp.wait_ge(s_rs, 2 * n + 1)
                gp.tensor_tensor(RST[:, tiles], RST[:, tiles], MHALF[:, :], ALU.pow).then_inc(s_rs, 1)

        @block.scalar
        def _(act):
            def mod_rows(l):
                for g in range(2):
                    act.wait_ge(s_mod, l + 1)
                    act.activation(GROW[:, g, :], psum[0:B, 4 + g, 0:C], ACT.Copy).then_inc(s_gr, 1)

            def split_hi_qkv(l):
                act.wait_ge(s_ra, RA["q", l])
                for w in range(3):
                    for raw, H in QKV_CHUNKS:
                        act.activation(qkv_cols(H, w, True), qkv_cols(raw, w, False), ACT.Copy).then_inc(s_wsp, 1)

            def split_hi(kind, n, raw, H, T, s, value):
                act.wait_ge(s, value)
                if T is None:
                    act.activation(H[:, :, :], raw, ACT.Copy).then_inc(s_wsp, 1)
                else:
                    act.activation(H[:, :, :], raw[:, 0:KC, :], ACT.Copy)
                    act.activation(T[0:TB, :], raw[0:TB, KC, :], ACT.Copy).then_inc(s_wsp, 1)

            def split_hi_tile(kind, f, m):
                if kind == "1":
                    if m == 0:
                        act.wait_ge(s_ra, RA["1", f])
                    cols = slice(P * m, P * m + P)
                    act.activation(W1H[:, :, cols], RAW1[:, 0:KC, cols], ACT.Copy)
                    act.activation(W1T[0:TB, cols], RAW1[0:TB, KC, cols], ACT.Copy).then_inc(s_wsp, 1)
                else:
                    if m == 0:
                        act.wait_ge(s_rb, RB["2", f])
                    if m < HM - 1:
                        act.wait_ge(s_h2, (HM - 1) * (B * f - 1) + m + 1)
                    else:
                        act.wait_ge(s_f2, NT * f)
                    act.activation(W2H[:, m, :], RAW2[:, m, :], ACT.Copy).then_inc(s_wsp, 1)

            def turned(l, s, b, chunks=range(KC + 1)):
                n = tn(l, s, b)
                for c in chunks:
                    rows = P if c < KC else T3
                    act.wait_ge(s_tr, 3 * n + c + 1)
                    if n >= 1:
                        act.wait_ge(s_lo, n)
                    src = psum[0:rows, CHUNK_BANK[c], :]
                    if s == 1:
                        act.activation(FX[0:rows, c, :], src, ACT.Copy).then_inc(s_fx, 1)
                    else:
                        act.activation(FX[0:rows, c, :], src, ACT.Identity,
                                       bias=MODC[0:rows, l, s, c, b:b + 1], scale=MODC[0:rows, l, s + 1, c, b:b + 1]).then_inc(s_fx, 1)
                    act.wait_ge(s_fx, 3 * n + c + 1)
                    if s == 1:
                        if b >= 1:
                            act.wait_ge(s_pj, NT * l + TT * b)
                        dst = OH_[:, c, :] if c < KC else OX[0:T3, :]
                    else:
                        dst = XS[:, b, 0, c, :] if c < KC else XT[0:T3, N * b:N * b + N]
                    act.activation(dst, FX[0:rows, c, :], ACT.Copy).then_inc(s_hi, 1)

            def qk_part1(i):
                act.wait_ge(s_r1, i + 1)
                act.activation(PT[:, i % PARTS, 1, :], QR[:, i % 3, :], ACT.Copy).then_inc(s_p2, 1)

            def qk_parts(l, b):
                for m in range(2 * QM):
                    i = 2 * QM * (B * l + b) + m
                    act.wait_ge(s_qk, i + 1)
                    if i >= PARTS:
                        act.wait_ge(s_pd[i % PARTS], 16 * (i // PARTS))
                    act.activation(PT[:, i % PARTS, 0, :], psum[0:96, QK_BANK[i % 3], :], ACT.Copy).then_inc(s_p1, 1)
                    if b >= 1 or m >= 1:
                        qk_part1(i - 1)
                if b == B - 1:
                    qk_part1(i)
                for t in range(TT):
                    i = NT * l + TT * b + t
                    act.wait_ge(s_vm, i + 1)
                    act.activation(V[:, TT * b + t, :], psum[:, 5 + i % 2, 0:C], ACT.Copy).then_inc(s_v, 1)

            def o_t(l, i):
                act.wait_ge(s_av, 64 * l + 4 * i + 4)
                act.activation(OT[:, bass.ds(i, 1), :].rearrange("p o n -> p (o n)"), bk(6), ACT.Copy).then_inc(s_ot, 1)

            def attention(l, bb, g, first=False, last=False):
                i = 4 * bb + g
                for v in range(16):
                    act.wait_ge(s_st, 256 * l + 16 * i + v + 1)
                    if v % 4 == 0 and not first:
                        act.wait_ge(s_av, 64 * l + 4 * i + v // 4 - 3)
                    act.activation(PE_[:, v // 4, v % 4, :], psum[:, 4 + v % 2, :], ACT.Exp, scale=SCALE).then_inc(s_e, 1)
                    if v == 7 and not first:
                        o_t(l, 4 * bb + (g - 1))
                    if last and v % 2 == 1 and TAIL_STEPS.get((g, v // 2)) in (2, 3):
                        turned(l, 1, 0, (0, 1) if TAIL_STEPS[g, v // 2] == 2 else (2,))

            act.wait_ge(s_in, 48)
            act.activation(SCT[:, 0, :], SC[0:96, :, :].rearrange("p k b -> p (k b)"), ACT.Exp, scale=-1.0).then_inc(s_sce, 1)
            mod_rows(0)
            for l in range(LAYERS):
                if l == 0:
                    split_hi_qkv(l)
                    act.wait_ge(s_mc_, l + 1)
                    turned(l, 0, 0)
                    turned(l, 0, 1)
                    qk_parts(l, 0)
                    turned(l, 0, 2)
                    split_hi("p", l, RAWP, WPH, WPT, s_rb, RB["p", l])
                    act.wait_ge(s_wg, 64)
                    act.activation(WGH[:, :, :], WGR[:, 0:KC, :], ACT.Copy)
                    act.activation(WGT[:, :], WGR[0:T3, KC, :], ACT.Copy).then_inc(s_ce, 1)
                    qk_parts(l, 1)
                    turned(l, 0, 3)
                else:
                    split_hi_qkv(l)
                    qk_parts(l, 0)
                    qk_parts(l, 1)
                    turned(l, 0, 3)
                qk_parts(l, 2)
                qk_parts(l, 3)
                if l + 1 < LAYERS:
                    mod_rows(l + 1)
                attention(l, 0, 0, first=True)
                with act.Fori(0, B - 1) as bb:
                    for g in range(1, HG + 1):
                        attention(l, bb, g)
                for g in range(1, HG):
                    attention(l, B - 1, g, last=True)
                o_t(l, B * HG - 1)

                f0, J = first_set(l), steps_of(l)
                for j in range(FIRST, J):
                    u = j % UNITS
                    if j >= 0:
                        i = UNITS * f0 + j
                        act.wait_ge(s_f1, i + 1)
                        if i >= 2:
                            act.wait_ge(s_h, i - 1)
                        act.activation(HF[:, i % 2, :], bk(i % 2), ACT.Gelu_apprx_tanh).then_inc(s_g, 1)
                    if j == FIRST:
                        split_hi("1", f0, RAW1, W1H, W1T, s_ra, RA["1", f0])
                        split_hi("2", f0, RAW2, W2H, None, s_rb, RB["2", f0])
                    for b in range(B):
                        k = j - HM * b + O_STEPS
                        if k in (2, 8):
                            turned(l, 1 if k == 2 else 2, b, (0, 1))
                        if k in (3, 9):
                            turned(l, 1 if k == 3 else 2, b, (2,))
                    for piece in split_pieces(l, j) if j >= 0 else ():
                        split_hi_tile(*piece)
                    if l == 0 and 0 <= j < UNITS and j % HM == 7:
                        act.wait_ge(s_cw, j // HM + 1)
                        tiles = slice(TT * (j // HM), TT * (j // HM + 1))
                        act.activation(CW[:, tiles, :], LG[:, tiles, :], ACT.Exp).then_inc(s_ce, 1)
                    if l + 1 < LAYERS and j == J - UNITS + P_UNIT:
                        split_hi("p", l + 1, RAWP, WPH, WPT, s_rb, RB["p", l + 1])
                    if l + 1 < LAYERS and j >= J - UNITS:
                        for b, first in enumerate(NEXT_UNIT):
                            if u == first + 2:
                                turned(l + 1, 0, b, (0, 1))
                            if u == first + 3:
                                turned(l + 1, 0, b, (2,))

            def last_x(b):
                for c in range(KC + 1):
                    rows = P if c < KC else TAIL
                    act.wait_ge(s_zt, 3 * b + c + 1)
                    if b >= 1:
                        act.wait_ge(s_zp, 2 * b - 1)
                    act.activation(FX[0:rows, c, :], psum[0:rows, c, :], ACT.Copy).then_inc(s_zf, 1)

            last_x(0)
            for b in range(B):
                for j in range(2):
                    act.wait_ge(s_zp, 2 * b + j + 1)
                    if b >= 1:
                        act.wait_ge(s_zo if j else s_zp, TT * b if j else 2 * b)
                    act.activation(ZT[:, j, :], psum[0:D3, 3 + j, :], ACT.Copy).then_inc(s_zc, 1)
                if b + 1 < B:
                    last_x(b + 1)

        @block.tensor
        def _(pe):
            def products(dst, terms, stop=True):
                for n, (a, r) in enumerate(terms):
                    i = pe.matmul(dst, a, r, start=(n == 0), stop=(n == len(terms) - 1))
                return i

            MOD_PRODUCTS = 4 * (KC + 1) + 2

            def mod(l, n):
                if n == 0:
                    pe.wait_ge(s_ra, RA["a", l])
                    pe.wait_ge(s_rb, RB["a", l])
                if n < 4 * (KC + 1):
                    v, c = divmod(n, KC + 1)
                    vec = (0, 1, 3, 4)[v]
                    rows = P if c < KC else TAIL
                    places = [(slice(r * TAIL, r * TAIL + rows), 7, slice(P + n * B, P + n * B + B)) for r in range(1 if c < KC else 3)]
                    cols = slice((vec % 3) * C + c * P, (vec % 3) * C + c * P + rows)
                else:
                    vec = 2 + 3 * (n - 4 * (KC + 1))
                    places = [(slice(0, B), 4 + vec // 3, slice(0, C))]
                    cols = slice(2 * C, 3 * C)
                for place in places:
                    for k in range(3):
                        K = 97 if k == 0 else 96
                        w, c_ = ada(l)[vec // 3][0:K, k, cols], SC[0:K, k, :]
                        lhs, rhs = (w, c_) if n < 4 * (KC + 1) else (c_, w)
                        i = pe.matmul(psum[place], lhs, rhs, start=(k == 0), stop=(k == 2))
                if n == MOD_PRODUCTS - 1:
                    i.then_inc(s_mod, 1)

            def turn(l, s, b, chunks=range(KC + 1)):
                n = tn(l, s, b)
                for c in chunks:
                    rows = P if c < KC else T3
                    if c == 0:
                        pe.wait_ge(s_xn, n + 1)
                        if n >= 1:
                            pe.wait_ge(s_fx, 3 * n)
                    if c == 1 and l == 0 and s == 2 and b >= 1:
                        pe.wait_ge(s_lc, b)
                    if c == 2:
                        pe.wait_ge(s_fx, 3 * n + 2)
                    for t in range(TT):
                        i = pe.transpose(psum[0:rows, CHUNK_BANK[c], P * t:P * t + P], XN[n % 2][:, t, P * c:P * c + rows], IDN[:, :])
                    i.then_inc(s_tr, 1)

            def qkv(l, b):
                pe.wait_ge(s_lo, tn(l, 0, b) + 1)
                for m in range(2 * QM):
                    i = 2 * QM * (B * l + b) + m
                    if b == 0 and m % QM == 0:
                        pe.wait_ge(s_wl, split_no["q", l, (KC + 1) * (m // QM + 1) - 1] + 1)
                    if i >= 3:
                        pe.wait_ge(s_r1, i - 2)
                    if l >= 1 and b == 0 and m == 2:
                        pe.wait_ge(s_ev, NT * (sets_of(l - 1)[-1] + 1))
                    products(psum[0:96, QK_BANK[i % 3], :], split_terms(WQH, WQL, WQT, XS[:, b, 0], XS[:, b, 1], XT[:, N * b:N * b + N],
                                                                        slice(96 * m, 96 * m + 96), slice(0, N), TB)).then_inc(s_qk, 1)
                if b == 0:
                    pe.wait_ge(s_wl, split_no["q", l, 3 * (KC + 1) - 1] + 1)
                for t in range(TT):
                    i = NT * l + TT * b + t
                    if i >= 2:
                        pe.wait_ge(s_v, i - 1)
                    terms = split_terms(WQH, WQL, WQT, XS[:, b, 0], XS[:, b, 1], XT[:, N * b:N * b + N],
                                        slice(2 * C, 3 * C), slice(P * t, P * t + P), TB)
                    products(psum[:, 5 + i % 2, 0:C], [(r, a) for a, r in terms]).then_inc(s_vm, 1)

            def l_first_scores(bb, g, u):
                return isinstance(bb, int) and bb == 0 and g == 0 and u == 0

            def scores(l, bb, g, u):
                i = 4 * bb + g
                if l_first_scores(bb, g, u):
                    pe.wait_ge(s_or, 16 * (l + 1))
                if u == 0:
                    pe.wait_ge(s_ld[g], LOAD * B * l + LOAD * (bb + 1))
                need = 128 * l + 8 * i + u - 1
                if not isinstance(need, int) or need > 0:
                    pe.wait_ge(s_mx, need)
                for j in range(2):
                    qt = 2 * (u % 2) + j
                    mm = pe.matmul(psum[:, 2 * (u % 2) + j, :], Q6[0:STK, g, u // 2, P * qt:P * qt + P], K6[0:STK, g, u // 2, :], start=True, stop=True)
                mm.then_inc(s_s, 1)

            def turn_max(l, bb, g):
                i = 4 * bb + g
                pe.wait_ge(s_mx, 128 * l + 8 * (i + 1))
                pe.wait_ge(s_mc, 16 * l + i)
                pe.transpose(psum[0:16, 7, 0:P], MX[:, g % 2, :], IDN[:, :]).then_inc(s_mt, 1)

            def scores_t(l, bb, g, v, first):
                i = 4 * bb + g
                if v == 0:
                    pe.wait_ge(s_mr[g % 2], 128 * l + 16 * (2 * bb + g // 2 + 1))
                if not first or v >= 2:
                    pe.wait_ge(s_e, 256 * l + 16 * i + v - 1)
                kt, h = v // 4, v % 4
                pe.matmul(psum[:, 4 + v % 2, :], K6[0:STK + 1, g % 4, h, P * kt:P * kt + P], Q6[0:STK + 1, g % 4, h, :], start=True, stop=True).then_inc(s_st, 1)

            def use_probs(l, bb, g, kt, half, first):
                i = 4 * bb + g
                if half == 0:
                    pe.wait_ge(s_e, 256 * l + 16 * i + 4 * kt + 4)
                    if kt == 0:
                        pe.wait_ge(s_vs, 16 * l + i + 1)
                        if not first:
                            pe.wait_ge(s_ot, 16 * l + i)
                q = slice(N // 2 * half, N // 2 * (half + 1))
                for h in range(4):
                    mm = pe.matmul(psum[32 * h:32 * h + 32, 6, q], VST[:, g % 4, kt, h, :], PE_[:, kt, h, q],
                                   start=(kt == 0 and half == 0), stop=(kt == TT - 1 and half == 1))
                if half == 1:
                    mm.then_inc(s_av, 1)

            def attention(l, bb, g, first=False, last=False):
                for u in range(8):
                    scores_t(l, bb, g, 2 * u, first)
                    if u == 1 and not (last and g == 3):
                        turn_max(l, bb + (g + 1) // 4, (g + 1) % 4)
                    if not (last and g >= 2):
                        scores(l, bb + (g + 2) // 4, (g + 2) % 4, u)
                    scores_t(l, bb, g, 2 * u + 1, first)
                    if u >= 4:
                        use_probs(l, bb, g, u // 2 - 2, u % 2, first)
                    elif not first:
                        use_probs(l, bb, g - 1, 2 + u // 2, u % 2, first)
                    if last and (g, u) in TAIL_STEPS:
                        to_ffn(l, 0, TAIL_STEPS[g, u])

            def turn_o(l, b, t):
                i = NT * l + TT * b + t
                if t == 0:
                    pe.wait_ge(s_ot, 16 * l + 4 * (b + 1))
                if t <= 1:
                    pe.wait_ge(s_fx, 3 * tn(l, 1, b) - 1 + t)
                if t >= 2:
                    pe.wait_ge(s_on, i - 1)
                for g in range(HG):
                    mm = pe.transpose(psum[:, 2 + t % 2, P * g:P * g + P], OT[:, 4 * b + g, P * t:P * t + P], IDN[:, :])
                mm.then_inc(s_to, 1)

            def proj(l, b, t):
                i = NT * l + TT * b + t
                if t == 0:
                    pe.wait_ge(s_lo, tn(l, 1, b) + 1)
                    if b == 0:
                        pe.wait_ge(s_wl, split_no["p", l] + 1)
                if t >= 2:
                    pe.wait_ge(s_dvp, i - 1)
                terms = split_terms(WPH, WPL, WPT, OH_, OL, OX, slice(0, C), slice(P * t, P * t + P), TB)
                products(psum[:, 2 + t % 2, 0:C], [(r, a) for a, r in terms]).then_inc(s_pj, 1)

            def logits(b):
                pe.wait_ge(s_lo, tn(0, 2, b) + 1)
                pe.wait_ge(s_wl2, 1)
                if b + 1 < B:
                    pe.wait_ge(s_dvp, TT * (b + 2))
                for t in range(TT):
                    terms = split_terms(WGH, WGL, WGT, XS[:, b, 0], XS[:, b, 1], XT[:, N * b:N * b + N],
                                        slice(0, EXPERTS), slice(P * t, P * t + P), T3)
                    mm = products(psum[:, 3, EXPERTS * t:EXPERTS * t + EXPERTS], [(r, a) for a, r in terms])
                mm.then_inc(s_lg, 1)

            def to_ffn(l, b, k):
                if k in (0, 1):
                    turn_o(l, b, 2 * k)
                    turn_o(l, b, 2 * k + 1)
                elif k in (2, 8):
                    turn(l, 1 if k == 2 else 2, b, (0, 1))
                elif k in (3, 9):
                    turn(l, 1 if k == 3 else 2, b, (2,))
                elif k in (4, 5):
                    proj(l, b, 2 * (k - 4))
                    proj(l, b, 2 * (k - 4) + 1)

            def hidden(f, u):
                l = SETS[f][0]
                b, m = u // HM, u % HM
                i = UNITS * f + u
                if b == 0:
                    pe.wait_ge(s_wl, split_done("1", f, m))
                if m == 0:
                    pe.wait_ge(s_lo, tn(l, 2, b) + 1)
                if i >= 2:
                    pe.wait_ge(s_g, i - 1)
                products(bk(i % 2), split_terms(W1H, W1L, W1T, XS[:, b, 0], XS[:, b, 1], XT[:, N * b:N * b + N],
                                                slice(P * m, P * m + P), slice(0, N), TB)).then_inc(s_f1, 1)

            def second(f, u):
                b, m = u // HM, u % HM
                grp = B * f + b
                pe.wait_ge(s_h, UNITS * f + u + 1)
                if b == 0:
                    pe.wait_ge(s_wl, split_done("2", f, m))
                for t in range(TT):
                    if m == 0 and grp >= 1:
                        pe.wait_ge(s_ev, TT * (grp - 1) + t + 1)
                    c = slice(P * t, P * t + P)
                    for n, (h, w) in enumerate(((HH, W2H), (HH, W2L), (HL, W2H))):
                        mm = pe.matmul(psum[:, 4 + t, 0:C], h[:, m % 3, c], w[:, m, :], start=(m == 0 and n == 0), stop=(m == HM - 1 and n == 2))
                    if m == HM - 1:
                        mm.then_inc(s_f2, 1)
                if m < HM - 1:
                    mm.then_inc(s_h2, 1)

            def l3_begin(n):
                pe.wait_ge(s_pv, n)

            def expm_step(n):
                if n == 0:
                    pe.wait_ge(s_uo, 16 * (D3 - 1))
                l3_begin(n)
                if n == 0:
                    for b in range(B):
                        mm = pe.transpose(psum[0:D3, 3, D3 * b:D3 * b + D3], UO[:, b, :], IDN[0:D3, 0:D3])
                elif n == 1:
                    mm = pe.transpose(psum[0:B, 3, 0:D3], NRM[:, 0:B], IDN[0:D3, 0:D3])
                elif n == 2:
                    mm = pe.matmul(psum[0:D3, 3, 0:B], NBC[:, 4:4 + D3], IDN[0:B, 0:B], start=True, stop=True)
                else:
                    for s in range(2):
                        for b in range(B):
                            lhs = AS[:, 1 - s, b, :] if n < 3 + TAYLOR - 1 else RR[:, 1 - s, b, :]
                            mm = pe.matmul(psum[0:D3, 3, D3 * (B * s + b):D3 * (B * s + b + 1)], lhs, RR[:, s, b, :], start=True, stop=True)
                mm.then_inc(s_pp, 1)

            def u_step(n):
                if n == 0:
                    pe.wait_ge(s_qr, QR_END)
                l3_begin(EXPM_STEPS + n)
                o = psum[0:D3, 3, 0:D3]
                o2 = psum[0:D3, 3, D3:2 * D3]
                if n == 0:
                    for c in range(3):
                        mm = pe.matmul(o, QV[:, c, :], QV[:, c, :], start=(c == 0), stop=(c == 2))
                elif n == 1:
                    for c in range(3):
                        mm = pe.transpose(psum[0:D3, 3, 96 * c:96 * c + 96], QV[:, c, :], IDN[0:96, 0:96])
                elif n == 2:
                    mm = pe.transpose(o, NW[:, 0, :], IDN[0:D3, 0:D3])
                elif n < 3 + 12:
                    if n % 2 == 1:
                        mm = pe.matmul(o, NW[:, 1, :], NW[:, 2, :], start=True, stop=True)
                    else:
                        pe.matmul(o, NW[:, 3, :], NW[:, 4, :], start=True, stop=True)
                        mm = pe.matmul(o2, NW[:, 4, :], NW[:, 3, :], start=True, stop=True)
                elif n == 15:
                    mm = pe.matmul(o, NW[:, 3, :], VTR[:, 0:D3], start=True, stop=True)
                elif n == 16:
                    mm = pe.matmul(psum[0:D3, 3, 0:C], NW[:, 5, :], VTR[:, :], start=True, stop=True)
                else:
                    for c in range(KC + 1):
                        rows = P if c < KC else TAIL
                        mm = pe.transpose(psum[0:rows, 3, D3 * c:D3 * c + D3], UTT[:, P * c:P * c + rows], IDN[0:D3, 0:D3])
                mm.then_inc(s_pp, 1)

            pe.wait_ge(s_cst, 2)
            pe.wait_ge(s_sc, 2)
            for n in range(MOD_PRODUCTS):
                mod(0, n)
            for l in range(LAYERS):
                if l == 0:
                    turn(l, 0, 0)
                    turn(l, 0, 1)
                    qkv(l, 0)
                    turn(l, 0, 2)
                    qkv(l, 1)
                    turn(l, 0, 3)
                else:
                    qkv(l, 0)
                    qkv(l, 1)
                    turn(l, 0, 3)
                qkv(l, 2)
                qkv(l, 3)
                pe.wait_ge(s_v, NT * (l + 1))
                pe.wait_ge(s_r1, 2 * QM * B * (l + 1))
                pe.wait_ge(s_fx, 3 * tn(l, 1, 0))
                if l + 1 < LAYERS:
                    for n in range(MOD_PRODUCTS - 8):
                        mod(l + 1, n)
                for g in range(2):
                    for u in range(8):
                        scores(l, 0, g, u)
                        if g == 0 and l + 1 < LAYERS:
                            mod(l + 1, MOD_PRODUCTS - 8 + u)
                    if g == 0:
                        if l + 1 < LAYERS:
                            pe.wait_ge(s_mc_, l + 2)
                        turn_max(l, 0, 0)
                if l + 1 < LAYERS:
                    pe.wait_ge(s_gr, 2 * (l + 2))
                attention(l, 0, 0, first=True)
                with pe.Fori(0, B - 1) as bb:
                    for g in range(1, HG + 1):
                        attention(l, bb, g)
                for g in range(1, HG):
                    attention(l, B - 1, g, last=True)
                for u in range(4):
                    use_probs(l, B - 1, HG - 1, 2 + u // 2, u % 2, False)

                f0, J = first_set(l), steps_of(l)
                for j in range(FIRST, J + 2):
                    f, u = f0 + j // UNITS, j % UNITS
                    if 0 <= j < J:
                        hidden(f, u)
                        if f == U_SET and u >= U_UNIT:
                            u_step(2 * (u - U_UNIT))
                    if j >= 2:
                        second(f0 + (j - 2) // UNITS, (j - 2) % UNITS)
                    for b in range(B):
                        k = j - HM * b + O_STEPS
                        if 0 <= k < O_STEPS:
                            to_ffn(l, b, k)
                    if l == 0 and 0 <= j < UNITS and u % HM == 5:
                        logits(u // HM)
                    if 0 <= UNITS * f + u - EXPM_START < EXPM_STEPS:
                        expm_step(UNITS * f + u - EXPM_START)
                    if f == U_SET and u >= U_UNIT and 0 <= j:
                        u_step(2 * (u - U_UNIT) + 1)
                    if l + 1 < LAYERS and J - UNITS <= j < J:
                        for b, first in enumerate(NEXT_UNIT):
                            if u == first + 2:
                                turn(l + 1, 0, b, (0, 1))
                            if u == first + 3:
                                turn(l + 1, 0, b, (2,))

            pe.wait_ge(s_pv, EXPM_STEPS + U_STEPS)
            pe.wait_ge(s_ev, NT * len(SETS))
            def turn_last(b):
                pe.wait_ge(s_xr, NT * (len(SETS) - 1) + TT * (b + 1))
                for c in range(KC + 1):
                    rows = P if c < KC else TAIL
                    if b >= 1:
                        pe.wait_ge(s_zf, 3 * b - 2 + c)
                    for t in range(TT):
                        mm = pe.transpose(psum[0:rows, c, P * t:P * t + P], XR[:, TT * b + t, P * c:P * c + rows], IDN[:, :])
                    mm.then_inc(s_zt, 1)

            def change_last(b):
                for t in range(TT):
                    i = TT * b + t
                    if t == 0:
                        pe.wait_ge(s_zc, 2 * b + 2)
                    if i >= 2:
                        pe.wait_ge(s_fin, i - 1)
                    pe.matmul(psum[:, 5 + i % 2, 0:C], ZT[:, 1, P * t:P * t + P], UTT[:, :], start=True, stop=True).then_inc(s_zo, 1)

            turn_last(0)
            for b in range(B):
                pe.wait_ge(s_zf, 3 * b + 3)
                if b >= 1:
                    pe.wait_ge(s_zc, 2 * b - 1)
                for c in range(KC + 1):
                    rows = P if c < KC else TAIL
                    mm = pe.matmul(psum[0:D3, 3, :], UU[0:rows, c, :], FX[0:rows, c, :], start=(c == 0), stop=(c == KC))
                mm.then_inc(s_zp, 1)
                if b + 1 < B:
                    turn_last(b + 1)
                pe.wait_ge(s_zc, 2 * b + 1)
                pe.matmul(psum[0:D3, 4, :], RR[:, 0, b, :], ZT[:, 0, :], start=True, stop=True).then_inc(s_zp, 1)
                change_last(b)

        @block.vector
        def _(dve):
            steps = [0]

            def link(i):
                i.then_inc(s_dv, 1)
                steps[0] += 1
                dve.wait_ge(s_dv, steps[0])

            def mods(l):
                dve.wait_ge(s_mod, l + 1)
                mp = psum[:, 7, P:P + 4 * (KC + 1) * B].rearrange("p (v n) -> p v n", v=4)
                mc = MODC[:, l, :, :, :].rearrange("p v c b -> p v (c b)")
                for rows, cols in ((P, slice(0, KC * B)), (T3, slice(KC * B, (KC + 1) * B))):
                    dve.tensor_copy(mc[0:rows, 0:4:2, cols], mp[0:rows, 0:4:2, cols])
                    i = dve.tensor_scalar(mc[0:rows, 1:4:2, cols], mp[0:rows, 1:4:2, cols], 1.0, None, ALU.add)
                i.then_inc(s_mc_, 1)

            def split_lo_qkv(l, w):
                for n, (raw, H) in enumerate(QKV_CHUNKS):
                    dve.wait_ge(s_wsp, split_no["q", l, (KC + 1) * w + n] + 1)
                    if n < KC:
                        L, rows = WQL[:, n, :], slice(0, P)
                    else:
                        L, rows = WQT[:, :], slice(2 * TAIL, T3 + 1)
                    dve.tensor_tensor(qkv_cols(L[rows], w, True), qkv_cols(raw[rows], w, False),
                                      qkv_cols(H[rows], w, True).bitcast(F32), ALU.subtract).then_inc(s_wl, 1)

            def split_lo(key, raw, H, L, T):
                n = split_no[key]
                dve.wait_ge(s_wsp, n + 1)
                if T is None:
                    dve.tensor_tensor(L[:, :, :], raw, H[:, :, :].bitcast(F32), ALU.subtract).then_inc(s_wl, 1)
                    return
                dve.tensor_tensor(L[:, :, :], raw[:, 0:KC, :], H[:, :, :].bitcast(F32), ALU.subtract)
                dve.tensor_tensor(T[2 * TAIL:T3 + 1, :], raw[2 * TAIL:T3 + 1, KC, :], T[2 * TAIL:T3 + 1, :].bitcast(F32), ALU.subtract).then_inc(s_wl, 1)

            def stats(b, l, s):
                for t in range(TT):
                    i = dve.bn_stats(BN6[:, t, :], XR[:, TT * b + t, :])
                link(i)
                for t in range(TT):
                    i = dve.bn_aggr(MV[:, TT * b + t, :], BN6[:, t, :])
                if (l, s, b) in POOL_NORMS:
                    i.then_inc(s_ms, 1)
                    dve.wait_ge(s_ms, POOL_NORMS.index((l, s, b)) + 1)
                else:
                    link(i)
                    rstd(b)

            def rstd(b):
                v, y, t = NWT[:, 0, 0:TT], NWT[:, 1, 0:TT], NWT[:, 2, 0:TT]
                tiles = slice(TT * b, TT * b + TT)
                link(dve.tensor_scalar(v, MV[:, tiles, 1], LN_EPS, None, ALU.add))
                link(dve.tensor_scalar(t.bitcast(I32), v.bitcast(I32), 1, None, ALU.arith_shift_right))
                link(dve.tensor_scalar(y.bitcast(I32), t.bitcast(I32), -1.0, RSQRT_MAGIC, ALU.mult, ALU.add))
                for n in range(NEWTON):
                    link(dve.scalar_tensor_tensor(t, y, -0.5, y, ALU.mult, ALU.mult))
                    link(dve.tensor_tensor(t, t, v, ALU.mult))
                    link(dve.scalar_tensor_tensor(y if n < NEWTON - 1 else RST[:, tiles], t, 1.5, y, ALU.add, ALU.mult))

            def normalise(l, s, b):
                n = tn(l, s, b)
                if (l, s, b) in POOL_NORMS:
                    dve.wait_ge(s_rs, 2 * POOL_NORMS.index((l, s, b)) + 2)
                if n >= 2:
                    dve.wait_ge(s_tr, 3 * (n - 1))
                for t in range(TT):
                    i = dve.tensor_scalar(XN[n % 2][:, t, 0:C], XR[:, TT * b + t, :], MV[:, TT * b + t, 0:1], RST[:, TT * b + t:TT * b + t + 1],
                                          ALU.subtract, ALU.mult)
                link(i)
                tails(n)

            def tails(n):
                for r in range(2):
                    i = dve.tensor_copy(XN[n % 2][:, :, C + TAIL * r:C + TAIL * (r + 1)], XN[n % 2][:, :, KC * P:C])
                i.then_inc(s_xn, 1)

            def low(l, s, b):
                n = tn(l, s, b)
                dve.wait_ge(s_hi, 3 * n + 3)
                if s == 1:
                    H, L, T, cols = OH_[:, :, :], OL[:, :, :], OX, slice(0, N)
                    if b == 0:
                        dve.memset(OX[T3:TB, :].bitcast(F32), 1.0)
                    if b >= 1:
                        dve.wait_ge(s_pj, NT * l + TT * b)
                else:
                    H, L, T, cols = XS[:, b, 0], XS[:, b, 1], XT, slice(N * b, N * b + N)
                dve.tensor_tensor(L, FX[:, 0:KC, :], H.bitcast(F32), ALU.subtract)
                dve.tensor_tensor(T[TAIL:2 * TAIL, cols], FX[TAIL:2 * TAIL, KC, :], T[TAIL:2 * TAIL, cols].bitcast(F32), ALU.subtract).then_inc(s_lo, 1)

            def qk_part2(i):
                dve.wait_ge(s_p2, i + 1)
                dve.tensor_tensor(PT[:, i % PARTS, 2, :], QR[:, i % 3, :], PT[:, i % PARTS, 1, :], ALU.subtract).then_inc(s_p3, 1)

            def qkv(l, b, beside=None):
                for m in range(2 * QM):
                    i = 2 * QM * (B * l + b) + m
                    if beside and m == QM:
                        beside()
                    dve.wait_ge(s_p1, i + 1)
                    if i >= 3:
                        dve.wait_ge(s_p3, i - 2)
                    dve.tensor_tensor(QR[:, i % 3, :], psum[0:96, QK_BANK[i % 3], :], PT[:, i % PARTS, 0, :], ALU.subtract).then_inc(s_r1, 1)
                    if b >= 1 or m >= 1:
                        qk_part2(i - 1)
                if b == B - 1:
                    qk_part2(i)

            def row_max(l, bb, g, u):
                i = 4 * bb + g
                dve.wait_ge(s_s, 128 * l + 8 * i + u + 1)
                o = 2 * (u % 2)
                dve.tensor_reduce(MX[:, g % 2, 2 * u:2 * u + 2], psum[:, o:o + 2, :], AX.X, ALU.max).then_inc(s_mx, 1)

            def stage(l, bb, g):
                i = 4 * bb + g
                dve.wait_ge(s_mt, 16 * l + i + 1)
                dve.tensor_scalar(MXT[:, g % 2, :], psum[0:16, 7, 0:P], -1.0, None, ALU.mult).then_inc(s_mc, 1)
                src = V[:, bass.ds(TT * bb, TT), 4 * HD * g:4 * HD * (g + 1)].rearrange("p t (h d) -> p t h d", d=HD)
                dst = VST[:, g, :, :, 0:HD]
                dve.tensor_copy(dst, src).then_inc(s_vs, 1)

            def attention(l, bb, last):
                for g in range(HG):
                    for u in range(8):
                        if not (last and g >= 2):
                            row_max(l, bb + (g + 2) // 4, (g + 2) % 4, u)
                        if u == 2 and not (last and g == 3):
                            stage(l, bb + (g + 1) // 4, (g + 1) % 4)
                        if last and (g, u) in TAIL_STEPS:
                            to_ffn(l, 0, TAIL_STEPS[g, u])

            def o_rows(l, b, tiles):
                n = tn(l, 1, b)
                for t in tiles:
                    i = NT * l + TT * b + t
                    dve.wait_ge(s_to, i + 1)
                    if t == 0:
                        dve.wait_ge(s_tr, 3 * (n - 1))
                    if i >= 1:
                        dve.wait_ge(s_on, i)
                    src = psum[:, 2 + t % 2, :].rearrange("p (h d) -> p h d", d=32)
                    link(dve.reciprocal(RC[:, :], src[:, :, HD:HD + 1].rearrange("p h o -> p (h o)")))
                    j = dve.tensor_tensor(XN[n % 2][:, t, 0:C].rearrange("p (h d) -> p h d", d=HD), src[:, :, 0:HD],
                                          RC[:, :].unsqueeze(2).to_broadcast([P, HEADS, HD]), ALU.mult)
                    j.then_inc(s_on, 1)
                if tiles[-1] == TT - 1:
                    dve.wait_ge(s_on, NT * l + TT * b + TT)
                    tails(n)

            def attn_add(l, b, tiles):
                if b == 0 and tiles[0] == 0:
                    dve.wait_ge(s_gm, 16 * (l + 1))
                for t in tiles:
                    dve.wait_ge(s_pj, NT * l + TT * b + t + 1)
                    dve.tensor_tensor(TA[:, t % 2, :], psum[:, 2 + t % 2, 0:C], GMSA[:, b, :], ALU.mult).then_inc(s_dvp, 1)
                done = NT * l + TT * b + tiles[-1] + 1
                dve.wait_ge(s_dvp, done)
                rows = XR[:, TT * b + tiles[0]:TT * b + tiles[-1] + 1, :]
                dve.tensor_tensor(rows, rows, TA[:, :, :], ALU.add).then_inc(s_xa, 2)
                dve.wait_ge(s_xa, done)

            def to_ffn(l, b, k):
                if k in (0, 1):
                    o_rows(l, b, (2 * k, 2 * k + 1))
                elif k == 3:
                    low(l, 1, b)
                elif k in (4, 5):
                    attn_add(l, b, (2 * (k - 4), 2 * (k - 4) + 1))
                elif k == 6:
                    stats(b, l, 2)
                elif k == 7:
                    normalise(l, 2, b)
                elif k == 9:
                    low(l, 2, b)

            def gate_ranks(b):
                lg, rk, cmp = LG[:, TT * b:TT * b + TT, :], RK[:, TT * b:TT * b + TT, :], CMP[:, TT * b:TT * b + TT]
                dve.wait_ge(s_lg, b + 1)
                dve.tensor_copy(lg, psum[:, 3, 0:TT * EXPERTS].rearrange("p (t e) -> p t e", e=EXPERTS)).then_inc(s_lc, 1)
                dve.wait_ge(s_lc, b + 1)
                link(dve.memset(rk, 0.0))
                for e in range(EXPERTS):
                    for o in range(EXPERTS):
                        if o != e:
                            link(dve.tensor_tensor(cmp, lg[:, :, o], lg[:, :, e], ALU.is_ge if o < e else ALU.is_gt))
                            link(dve.tensor_tensor(rk[:, :, e], rk[:, :, e], cmp, ALU.add))
                link(dve.tensor_reduce(cmp, lg, AX.X, ALU.max))
                link(dve.tensor_scalar(rk, rk, 2.0, None, ALU.is_lt))
                dve.tensor_tensor(lg, lg, cmp.unsqueeze(2).to_broadcast([P, TT, EXPERTS]), ALU.subtract).then_inc(s_cw, 1)

            def gate_weights(b):
                cw, rk, cmp = CW[:, TT * b:TT * b + TT, :], RK[:, TT * b:TT * b + TT, :], CMP[:, TT * b:TT * b + TT]
                dve.wait_ge(s_ce, b + 2)
                link(dve.tensor_tensor(cw, cw, rk, ALU.mult))
                link(dve.tensor_reduce(cmp, cw, AX.X, ALU.add))
                link(dve.reciprocal(cmp, cmp))
                link(dve.tensor_tensor(cw, cw, cmp.unsqueeze(2).to_broadcast([P, TT, EXPERTS]), ALU.mult))

            def split_lo_tile(kind, f, m):
                dve.wait_ge(s_wsp, split_done(kind, f, m))
                if kind == "2":
                    dve.tensor_tensor(W2L[:, m, :], RAW2[:, m, :], W2H[:, m, :].bitcast(F32), ALU.subtract).then_inc(s_wl, 1)
                    return
                cols = slice(P * m, P * m + P)
                dve.tensor_tensor(W1L[:, :, cols], RAW1[:, 0:KC, cols], W1H[:, :, cols].bitcast(F32), ALU.subtract)
                dve.tensor_tensor(W1T[2 * TAIL:T3 + 1, cols], RAW1[2 * TAIL:T3 + 1, KC, cols], W1T[2 * TAIL:T3 + 1, cols].bitcast(F32), ALU.subtract).then_inc(s_wl, 1)

            def hidden_parts(f, u):
                b, m = u // HM, u % HM
                i = UNITS * f + u
                grp = B * f + b
                dve.wait_ge(s_g, i + 1)
                if m >= 3:
                    dve.wait_ge(s_h2, (HM - 1) * grp + m - 2)
                elif grp >= 1:
                    if m == 2:
                        dve.wait_ge(s_f2, TT * grp)
                    else:
                        dve.wait_ge(s_h2, (HM - 1) * (grp - 1) + m + 7)
                link(dve.tensor_copy(HH[:, m % 3, :], HF[:, i % 2, :]))
                dve.tensor_tensor(HL[:, m % 3, :], HF[:, i % 2, :], HH[:, m % 3, :].bitcast(F32), ALU.subtract).then_inc(s_h, 1)

            def ffn_take(f, b):
                grp = B * f + b
                l = SETS[f][0]
                if b == 0:
                    dve.wait_ge(s_b2[f % 2], 16 * (f // 2 + 1))
                    if f == first_set(l) and l + 1 < LAYERS:
                        dve.wait_ge(s_gd, 16 * (l + 2))
                for t in range(TT):
                    dve.wait_ge(s_f2, TT * grp + t + 1)
                    dve.tensor_tensor(T1[:, t, :], psum[:, 4 + t, 0:C], B2B[:, f % 2, :], ALU.add).then_inc(s_ev, 1)

            def ffn_add(f, b):
                l, e = SETS[f]
                if b == 0 and e == 0:
                    dve.wait_ge(s_gl, 16 * (l + 1))
                dve.wait_ge(s_ev, TT * (B * f + b + 1))
                for t in range(TT):
                    w = CW[:, TT * b + t, e:e + 1] if l == 0 else 1.0
                    i = dve.scalar_tensor_tensor(T1[:, t, :], T1[:, t, :], w, GMLP[:, b, :], ALU.mult, ALU.mult)
                link(i)
                dve.tensor_tensor(XR[:, TT * b:TT * b + TT, :], XR[:, TT * b:TT * b + TT, :], T1[:, :, :], ALU.add).then_inc(s_xr, TT)
                dve.wait_ge(s_xr, NT * f + TT * (b + 1))
                if f == sets_of(l)[-1] and l + 1 < LAYERS and b < B - 1:
                    stats(b, l + 1, 0)

            def skew_entries(u):
                if u == 0:
                    dve.wait_ge(s_l3, 48)
                t, half = u // 2, u % 2
                for b in (2 * half, 2 * half + 1):
                    link(dve.scalar_tensor_tensor(L3J[:, :], L3W[:, t, :], 1.0, SCB[0:VP, b, :], ALU.mult, ALU.mult, accum_out=VC[:, b, t:t + 1]))
                if u == 2 * VT_ - 1:
                    dve.tensor_tensor(VC[:, :, :], VC[:, :, :], BL[:, :].unsqueeze(1).to_broadcast([VP, B, VT_]), ALU.add).then_inc(s_vc, 1)

            def expm_step(n):
                dve.wait_ge(s_pp, n + 1)
                flat = "p s b d -> p (s b) d"
                p8 = psum[0:D3, 3, :].rearrange("p (s d) -> p s d", d=D3)
                if n == 0:
                    dve.tensor_tensor(AS[:, 0, :, :], UO[:, :, :], p8[:, 0:B, :], ALU.subtract)
                    link(dve.tensor_tensor(AS[:, 1, :, :], p8[:, 0:B, :], UO[:, :, :], ALU.subtract))
                    for j in range(8):
                        dve.tensor_copy(ID8[:, j, :], IDN[0:D3, 0:D3])
                    for j in range(SQUARINGS):
                        dve.memset(THR[:, j:j + 1], float(2 ** j))
                    i = dve.tensor_reduce(NRM[:, 0:B], AS[:, 0, :, :], AX.X, ALU.add, apply_absolute_value=True)
                elif n == 1:
                    link(dve.tensor_reduce(NBC[:, 0:1], psum[0:B, 3, 0:D3], AX.X, ALU.max))
                    i = dve.tensor_copy(NBC[:, 4:4 + D3], NBC[:, 0:1].to_broadcast([B, D3]))
                elif n == 2:
                    link(dve.tensor_copy(NRM[:, 4:4 + B], psum[0:D3, 3, 0:B]))
                    for s in range(2):
                        j = dve.tensor_tensor(MK[:, s, :, :], NRM[:, 4:4 + B].unsqueeze(2).to_broadcast([D3, B, SQUARINGS]),
                                              THR[:, :].unsqueeze(1).to_broadcast([D3, B, SQUARINGS]), ALU.is_gt)
                    link(j)
                    link(dve.tensor_scalar(MKH[:, :, :], MK[:, 0, :, :], -0.5, 1.0, ALU.mult, ALU.add))
                    link(dve.tensor_reduce(NRM[:, 8:8 + B], MKH[:, :, :], AX.X, ALU.mult))
                    for s in range(2):
                        j = dve.tensor_tensor(AS[:, s, :, :], AS[:, s, :, :], NRM[:, 8:8 + B].unsqueeze(2).to_broadcast([D3, B, D3]), ALU.mult)
                    link(j)
                    i = dve.scalar_tensor_tensor(RR[:, :, :, :].rearrange(flat), AS[:, :, :, :].rearrange(flat), 1.0 / TAYLOR, ID8[:, :, :], ALU.mult, ALU.add)
                elif n < 3 + TAYLOR - 1:
                    j = TAYLOR - 1 - (n - 3)
                    i = dve.scalar_tensor_tensor(RR[:, :, :, :].rearrange(flat), p8, 1.0 / j, ID8[:, :, :], ALU.mult, ALU.add)
                else:
                    k = n - (3 + TAYLOR - 1)
                    mask = MK[:, :, :, k].rearrange("p s b -> p (s b)").unsqueeze(2).to_broadcast([D3, 8, D3]).bitcast(I32)
                    i = dve.copy_predicated(RR[:, :, :, :].rearrange(flat), mask, p8)
                    if n == EXPM_STEPS - 1:
                        link(i)
                        i = dve.tensor_tensor(RR[:, 0, :, :], RR[:, 0, :, :], ID8[:, 0:B, :], ALU.subtract)
                i.then_inc(s_pv, 1)

            def u_step(n):
                dve.wait_ge(s_pp, EXPM_STEPS + n + 1)
                o = psum[0:D3, 3, 0:D3]
                o2 = psum[0:D3, 3, D3:2 * D3]
                eye = IDN[0:D3, 0:D3]
                if n == 0:
                    link(dve.memset(ET[:, :], 0.0))
                    dve.tensor_copy(ET[:, 0:D3], eye)
                    link(dve.tensor_tensor(NW[:, 5, :], o, SU[:, :], ALU.mult))
                    dve.tensor_tensor(NW[:, 0, :], NW[:, 5, :], eye, ALU.add)
                    i = dve.tensor_tensor(NW[:, 2, :], eye, NW[:, 5, :], ALU.subtract)
                elif n == 1:
                    i = dve.tensor_copy(VTR[:, :], psum[0:D3, 3, 0:C])
                elif n == 2:
                    link(dve.tensor_copy(NW[:, 1, :], o))
                    i = dve.scalar_tensor_tensor(NW[:, 3, :], eye, 2.0, NW[:, 1, :], ALU.mult, ALU.subtract)
                elif n < 3 + 12:
                    if n % 2 == 1:
                        i = dve.scalar_tensor_tensor(NW[:, 4, :], eye, 2.0, o, ALU.mult, ALU.subtract)
                    else:
                        dve.tensor_copy(NW[:, 2, :], o)
                        i = dve.tensor_copy(NW[:, 3, :], o2)
                elif n == 15:
                    i = dve.tensor_copy(NW[:, 5, :], o)
                elif n == 16:
                    i = dve.tensor_tensor(UTT[:, :], ET[:, :], psum[0:D3, 3, 0:C], ALU.subtract)
                else:
                    dve.tensor_copy(UU[:, 0:KC, :], psum[:, 3, 0:KC * D3].rearrange("p (c d) -> p c d", d=D3))
                    i = dve.tensor_copy(UU[0:TAIL, KC, :], psum[0:TAIL, 3, KC * D3:(KC + 1) * D3])
                i.then_inc(s_pv, 1)

            dve.memset(ONE[:, :, :], 1.0)
            dve.memset(UO[:, :, :], 0.0)
            dve.memset(SC[96:97, :, :], 1.0)
            dve.memset(XT[T3:TB, :].bitcast(F32), 1.0).then_inc(s_cst, 1)
            dve.wait_ge(s_sce, 1)
            link(dve.tensor_scalar(SCT[:, 0, :], SCT[:, 0, :], 1.0, None, ALU.add))
            link(dve.reciprocal(SCT[:, 1, :], SCT[:, 0, :]))
            sc = SC[0:96, :, :].rearrange("p k b -> p (k b)")
            dve.tensor_tensor(sc, sc, SCT[:, 1, :], ALU.mult).then_inc(s_sc, 2)
            for b in range(B):
                dve.wait_ge(s_x[b], 16)
                stats(b, 0, 0)
            mods(0)

            for l in range(LAYERS):
                if l == 0:
                    normalise(l, 0, 0)
                    normalise(l, 0, 1)
                    split_lo_qkv(l, 0)
                    split_lo_qkv(l, 1)
                    low(l, 0, 0)
                    split_lo_qkv(l, 2)
                    low(l, 0, 1)
                    normalise(l, 0, 2)
                    qkv(l, 0)
                    low(l, 0, 2)
                    split_lo(("p", l), RAWP, WPH, WPL, WPT)
                    normalise(l, 0, 3)
                    dve.wait_ge(s_ce, 1)
                    dve.tensor_tensor(WGL[:, :, :], WGR[:, 0:KC, :], WGH[:, :, :].bitcast(F32), ALU.subtract)
                    dve.tensor_tensor(WGT[2 * TAIL:T3, :], WGR[2 * TAIL:T3, KC, :], WGT[2 * TAIL:T3, :].bitcast(F32), ALU.subtract).then_inc(s_wl2, 1)
                    qkv(l, 1)
                    low(l, 0, 3)
                    qkv(l, 2)
                else:
                    for w in range(3):
                        split_lo_qkv(l, w)
                    ffn_take(sets_of(l - 1)[-1], B - 1)
                    ffn_add(sets_of(l - 1)[-1], B - 1)
                    qkv(l, 0, lambda: stats(B - 1, l, 0))
                    qkv(l, 1, lambda: normalise(l, 0, B - 1))
                    qkv(l, 2, lambda: low(l, 0, B - 1))
                qkv(l, 3)
                dve.wait_ge(s_v, NT * (l + 1))
                link(dve.memset(VST[:, :, :, :, HD:32], 0.0))
                link(dve.memset(VST[:, :, :, :, HD:HD + 1], 1.0))
                for g in range(2):
                    for u in range(8):
                        row_max(l, 0, g, u)
                    if g == 0 and l + 1 < LAYERS:
                        mods(l + 1)
                    if g == 0:
                        stage(l, 0, 0)
                with dve.Fori(0, B - 1) as bb:
                    attention(l, bb, False)
                attention(l, B - 1, True)

                f0, J = first_set(l), steps_of(l)
                for j in range(FIRST, J):
                    f, u = f0 + j // UNITS, j % UNITS
                    if j >= 0:
                        if f == U_SET and u >= U_UNIT:
                            u_step(2 * (u - U_UNIT))
                        hidden_parts(f, u)
                        for piece in split_pieces(l, j):
                            split_lo_tile(*piece)
                        if j >= HM and u % HM == 1:
                            ffn_take(f0 + (j - HM) // UNITS, (u // HM - 1) % B)
                        if j >= HM and u % HM == add_unit(u):
                            ffn_add(f0 + (j - HM) // UNITS, (u // HM - 1) % B)
                    for b in range(B):
                        k = j - HM * b + O_STEPS
                        if 0 <= k < O_STEPS:
                            to_ffn(l, b, k)
                    if j == W1_UNIT:
                        split_lo(("1", f0), RAW1, W1H, W1L, W1T)
                    if j == 0:
                        split_lo(("2", f0), RAW2, W2H, W2L, None)
                    if l == 0 and 0 <= j < UNITS and j % HM == 6:
                        gate_ranks(j // HM)
                    if l == 0 and 0 <= j < UNITS and j % HM == 8:
                        gate_weights(j // HM)
                    if l + 1 < LAYERS and j == J - UNITS + P_UNIT:
                        split_lo(("p", l + 1), RAWP, WPH, WPL, WPT)
                    if l + 1 < LAYERS and j >= J - UNITS:
                        for b, first in enumerate(NEXT_UNIT):
                            if u == first:
                                normalise(l + 1, 0, b)
                            if u == first + 3:
                                low(l + 1, 0, b)
                    if f == V_SET and u < 2 * VT_:
                        skew_entries(u)
                    if 0 <= UNITS * f + u - EXPM_START < EXPM_STEPS:
                        expm_step(UNITS * f + u - EXPM_START)
                    if f == U_SET and u >= U_UNIT and j >= 0:
                        u_step(2 * (u - U_UNIT) + 1)
            ffn_take(len(SETS) - 1, B - 1)
            ffn_add(len(SETS) - 1, B - 1)

            for b in range(B):
                for t in range(TT):
                    i = TT * b + t
                    dve.wait_ge(s_zo, i + 1)
                    dve.tensor_tensor(XR[:, i, :], XR[:, i, :], psum[:, 5 + i % 2, 0:C], ALU.add).then_inc(s_fin, 1)


EXPM_START = UNITS * EXPM_SET + EXPM_UNIT
EXPM_STEPS = 3 + TAYLOR - 1 + SQUARINGS
U_STEPS = 18


_L = [dict(ada_w="L0_cond_w_adaln", ada_b="L0_cond_b_adaln", qkv_w="L0_cond_w_qkv", qkv_b="L0_cond_b_qkv",
           out_w="L0_cond_w_proj", out_b="L0_cond_b_proj", w_gate="L0_cond_w_gate", w1="L0_cond_w1", b1="L0_cond_b1",
           w2="L0_cond_w2", b2="L0_cond_b2"),
      dict(ada_w="L1_cond_ada_w", ada_b="L1_cond_ada_b", qkv_w="L1_cond_qkv_w", qkv_b="L1_cond_qkv_b",
           out_w="L1_cond_out_w", out_b="L1_cond_out_b", w1="L1_cond_w1", b1="L1_cond_b1", w2="L1_cond_w2", b2="L1_cond_b2"),
      dict(ada_w="L2_cond_W_ada", ada_b="L2_cond_b_ada", qkv_w="L2_cond_W_qkv", qkv_b="L2_cond_b_qkv",
           out_w="L2_cond_W_proj", out_b="L2_cond_b_proj", w1="L2_cond_W_fc1", b1="L2_cond_b_fc1", w2="L2_cond_W_fc2", b2="L2_cond_b_fc2")]


def kernel(**inputs):
    import numpy as np
    import concourse.bacc as bacc
    from concourse import mybir as mb
    from concourse.bass_utils import run_bass_kernel_spmd as run

    nc = bacc.Bacc("TRN2", target_bir_lowering=False, num_devices=1)
    arrays, aps = {}, {}
    for name, a in inputs.items():
        a = np.ascontiguousarray(a)
        arrays[f"in_{name}"] = a
        aps[name] = nc.dram_tensor(f"in_{name}", a.shape, mb.dt.from_np(a.dtype), kind="ExternalInput").ap()
    out = nc.dram_tensor("out", inputs["x"].shape, mb.dt.float32, kind="ExternalOutput").ap()
    layers = [{k: aps[v] for k, v in d.items()} for d in _L]
    build(nc, aps["x"], aps["cond_1152"], layers, aps["L3_cond_P"], aps["L3_cond_W"], aps["L3_cond_b"], out)
    r = run(nc, [arrays], core_ids=[0])
    return r.results[0]["out"]
```

```python
import concourse.bass as bass
from concourse import mybir
from contextlib import ExitStack

F32 = mybir.dt.float32
F32R = mybir.dt.float32r
BF16 = mybir.dt.bfloat16
I32 = mybir.dt.int32
ALU = mybir.AluOpType
ACT = mybir.ActivationFunctionType
AX = mybir.AxisListType
ADD = bass.bass_isa.ReduceOp.add

B, N, C = 4, 512, 288
TOK = B * N
HEADS, HD = 16, 18
HID = 4 * C
EXPERTS = 4
LAYERS = 3
P = 128
TT = N // P
NT = TOK // P
KC = C // P
TAIL = C - KC * P
T3 = 3 * TAIL
TB = T3 + 2
HG = HEADS // 4
QM = C // 96
HM = HID // P
STK = 6 * HD
PART_RUNS = [(0, 0, 3), (3, 1, 2), (5, 2, 1)]
XNW = KC * P + T3
SETS = [(0, e) for e in range(EXPERTS)] + [(1, 0), (2, 0)]
UNITS = B * HM
LN_EPS = 1e-6
SCALE = float(HD) ** -0.5
D3 = 64
SKEW = D3 * (D3 - 1) // 2
VP = 126
VT_ = SKEW // VP
TAYLOR = 11
SQUARINGS = 16
QR_OPS = 24
QR_CUTS = (22, 53)
TINY = 1e-37
CHUNK_BANK = (2, 3, 2)
QK_BANK = (0, 1, 7)
V_SET, EXPM_SET, U_SET = 1, 2, 5
EXPM_UNIT, U_UNIT = 15, UNITS - HM
PARTS = 5
O_STEPS = 11
NEXT_UNIT = (25, 27, 32)
TAIL_STEPS = {(2, 2): 0, (2, 5): 1, (3, 0): 2, (3, 2): 3, (3, 4): 4, (3, 6): 5}
P_UNIT = 31
W1_UNIT = 8 - O_STEPS
FIRST = len(TAIL_STEPS) - O_STEPS


def build(nc, x, cond, layers, l3_P, l3_W, l3_b, out):
    ctx = ExitStack()
    with ctx:
        BASE = (nc.sbuf_base + 31) // 32 * 32
        top = [BASE]

        def at(name, shape, dt, offset):
            return nc.alloc_sbuf_tensor_at(name, shape, dt, offset=offset)

        def new(name, shape, dt):
            size = 2 if dt == BF16 else 4
            for n in shape[1:]:
                size *= n
            t = at(name, shape, dt, top[0])
            top[0] += (size + 31) // 32 * 32
            return t

        def region(size):
            top[0] += size
            return top[0] - size

        XR = new("residual", [P, NT, C], F32)
        xo = region(2 * KC * TOK * 4)
        XS = at("x_split", [P, B, 2, KC, N], F32R, xo)
        OT = at("o_t", [P, B * HG, N], F32, xo)
        XT = new("x_tail", [TB, TOK], F32R)

        ra = region(32768)
        Q6 = at("q_stack", [STK + 1, HG, 4, N], BF16, ra)
        K6 = at("k_stack", [STK + 1, HG, 4, N], BF16, ra + 16384)
        XN = [at("x_norm0", [P, TT, XNW], F32, ra), at("x_norm1", [P, TT, XNW], F32, ra + 9728)]
        OH_ = at("o_hi", [P, KC, N], F32R, ra + 5632)
        FX = at("x_mod", [P, KC + 1, N], F32, ra + 16384)
        OL = at("o_lo", [P, KC, N], F32R, ra + 22528)
        OX = at("o_tail", [TB, N], F32R, ra + 26624)
        QR = at("qk_r", [96, 3, N], F32, ra + 22528)
        HF = at("hid_f", [P, 2, N], F32, ra + 28672)
        L3W = at("l3_w", [VP, VT_, C], F32, ra)
        SCB = at("silu_c_all", [P, B, C], F32, ra + 18432)
        L3J = at("l3_junk", [VP, C], F32, ra + 23040)
        UT0 = ra
        ID8 = at("ident8", [D3, 8, D3], F32, UT0)
        AS = at("skew_pm", [D3, 2, B, D3], F32, UT0 + 2048)
        NRM = at("skew_norm", [D3, 16], F32, UT0 + 4096)
        NBC = at("norm_rows", [B, 4 + D3], F32, UT0 + 4160)
        MK = at("sq_mask", [D3, 2, B, SQUARINGS], F32, UT0 + 4448)
        MKH = at("sq_half", [D3, B, SQUARINGS], F32, UT0 + 4960)
        THR = at("sq_thr", [D3, SQUARINGS], F32, UT0 + 5216)
        NW = at("wy", [D3, 8, D3], F32, UT0)
        VTR = at("v_t", [D3, C], F32, UT0 + 2048)
        ET = at("e_t", [D3, C], F32, UT0 + 3200)
        GG = at("u_rot", [P, KC + 1, B * D3], F32, UT0 + 4352)

        rb = region(59392)
        PE_ = at("probs", [P, TT, 4, N], F32, rb)
        VST = at("v_stage", [P, HG, TT, 4, 32], F32, rb + 32768)
        V = at("v", [P, NT, C], F32, rb + 40960)
        WQH = at("wqkv_hi", [P, KC, 3 * C], F32R, rb)
        WQL = at("wqkv_lo", [P, KC, 3 * C], F32R, rb + 6912)
        WQT = at("wqkv_tail", [TB, 3 * C], F32R, rb + 13824)
        PT = at("qk_parts", [96, PARTS, 3, N], BF16, rb + 17408)
        W1H = at("w1_hi", [P, KC, HID], F32R, rb)
        W1L = at("w1_lo", [P, KC, HID], F32R, rb + 9216)
        W1T = at("w1_tail", [TB, HID], F32R, rb + 18432)
        W2H = at("w2_hi", [P, HM, C], F32R, rb + 23040)
        W2L = at("w2_lo", [P, HM, C], F32R, rb + 33408)
        TA = at("attn_branch", [P, 2, C], F32, rb + 56064)
        HH = at("hid_hi", [P, 3, N], F32R, rb + 43776)
        HL = at("hid_lo", [P, 3, N], F32R, rb + 49920)

        RAWA = new("raw_a", [P, 3 * HID], F32)
        RAWB = new("raw_b", [P, HM * C], F32)
        ADA0 = at("ada0", [P, 3, 3 * C], F32, rb + 17408)
        ADA = [RAWA[:, 0:9 * C].rearrange("p (k n) -> p k n", k=3), RAWB[:, :].rearrange("p (k n) -> p k n", k=3)]
        RAWQ = RAWA[:, 0:9 * C].rearrange("p (k n) -> p k n", k=3)
        RAW1 = RAWA[:, :].rearrange("p (k n) -> p k n", k=3)
        RAWP = RAWB[:, 0:3 * C].rearrange("p (k n) -> p k n", k=3)
        RAW2 = RAWB[:, :].rearrange("p (k n) -> p k n", k=HM)
        WPH = new("wproj_hi", [P, KC, C], F32R)
        WPL = new("wproj_lo", [P, KC, C], F32R)
        WPT = new("wproj_tail", [TB, C], F32R)
        GMSA = new("gate_msa", [P, B, C], F32)
        GMLP = new("gate_mlp", [P, B, C], F32)
        B2B = new("b2_rows", [P, 2, C], F32)
        T1 = new("branch", [P, TT, C], F32)
        GROW = at("gate_rows", [B, 2, C], F32, top[0] - TT * C * 4)
        MODC = new("mod_cols", [P, LAYERS, 4, KC + 1, B], F32)
        MV = new("ln_stats", [P, NT, 2], F32)
        BN6 = new("bn6", [P, TT, 6], F32)
        RST = new("rstd", [P, NT], F32)
        RC = new("recip", [P, HEADS], F32)
        MX = new("row_max", [P, 2, 16], F32)
        MXT = new("row_max_t", [16, 2, P], BF16)
        ONE = new("ones_bf", [16, HG, P], BF16)
        SC = new("silu_c", [97, 3, B], F32)
        SCT = new("silu_tmp", [96, 2, 3 * B], F32)
        IDN = new("ident", [P, P], F32)
        WGR = new("wgate_raw", [P, KC + 1, EXPERTS], F32)
        WGH = new("wgate_hi", [P, KC, EXPERTS], F32R)
        WGL = new("wgate_lo", [P, KC, EXPERTS], F32R)
        WGT = new("wgate_tail", [T3, EXPERTS], F32R)
        LG = new("logits", [P, NT, EXPERTS], F32)
        RK = new("rank", [P, NT, EXPERTS], F32)
        CMP = new("compare", [P, NT], F32)
        CMP2 = new("compare_pairs", [P, 2, TT, EXPERTS, EXPERTS], F32)
        LOWER = new("lower_index", [P, EXPERTS, EXPERTS], F32)
        CW = new("expert_w", [P, NT, EXPERTS], F32)
        QA = new("qr_a", [96, 3, D3], F32)
        QV = new("qr_v", [96, 3, D3], F32)
        QG = new("qr_rows_ge", [96, 3, D3], F32)
        QO = new("qr_onehot", [96, D3], F32)
        QM1 = new("qr_m", [96, 3, D3], F32)
        MHALF = new("minus_half", [P, TT], F32)
        QI = new("qr_in", [96, 2, D3], F32)
        QS = new("qr_sums", [96, 2, D3], F32)
        QC = new("qr_cols", [96, 24], F32)
        QW = new("qr_w", [96, D3], F32)
        UO = new("skew_upper", [D3, B, D3], F32)
        RR = new("rot", [D3, 2, B, D3], F32)
        VC = new("skew_col", [VP, B, VT_], F32)
        BL = new("skew_bias", [VP, VT_], F32)
        SU = new("strict_upper", [D3, D3], F32)
        UTT = new("u_t", [D3, C], F32)
        ZT = at("z_t", [D3, N], F32, ra + 22528)
        assert top[0] <= nc.sbuf_usable_end, (top[0], nc.sbuf_usable_end)

        psum = ctx.enter_context(nc.psum_tensor("psum", [P, 8, 512], F32))

        def bk(i):
            return psum[:, i, :]

        QKD = [nc.dram_tensor(f"qk_parts_d{l}", [2, 3, B, C, N], BF16, kind="Internal").ap() for l in range(LAYERS)]
        ONED = nc.dram_tensor("ones_d", [HG, 16, P], BF16, kind="Internal").ap()
        GD = [nc.dram_tensor(f"gates_d{l}", [2, B, C], F32, kind="Internal").ap() for l in range(LAYERS)]
        VD = nc.dram_tensor("skew_d", [B, SKEW], F32, kind="Internal").ap()
        SCD = nc.dram_tensor("silu_d", [B, C], F32, kind="Internal").ap()

        def sem(name):
            return ctx.enter_context(nc.semaphore(name))

        s_x = [sem(f"x_loaded{b}") for b in range(B)]
        s_in = sem("cond_loaded")
        s_ra = sem("raw_a_loaded")
        s_rb = sem("raw_b_loaded")
        s_wg = sem("wgate_loaded")
        s_cst = sem("constants_made")
        s_sce = sem("exp_of_minus_c")
        s_sc = sem("silu_made")
        s_m0 = sem("first_mod_products")
        s_mod = sem("mod_products")
        s_gr = sem("gate_rows_copied")
        s_gd = sem("gate_rows_stored")
        s_gm = sem("gate_msa_loaded")
        s_gl = sem("gate_mlp_loaded")
        s_mc_ = sem("mod_cols_made")
        s_wsp = sem("weight_hi_made")
        s_wl = sem("weight_lo_made")
        s_dv = sem("vector_steps")
        s_xn = sem("x_normalised")
        s_tr = sem("x_transposed")
        s_fx = sem("x_modulated")
        s_hi = sem("x_hi_made")
        s_lo = sem("x_lo_made")
        s_qk = sem("qk_products")
        s_p1 = sem("qk_part0")
        s_r1 = sem("qk_rest")
        s_p2 = sem("qk_part1")
        s_p3 = sem("qk_part2")
        s_pd = [sem(f"qk_parts_stored{i}") for i in range(PARTS)]
        s_vm = sem("v_products")
        s_v = sem("v_copied")
        s_one = sem("ones_stored")
        s_or = sem("ones_row_loaded")
        s_ld = [sem(f"stacks_loaded{g}") for g in range(HG)]
        s_s = sem("scores_for_max")
        s_mx = sem("row_max_made")
        s_mt = sem("row_max_turned")
        s_mc = sem("row_max_copied")
        s_mr = [sem(f"row_max_placed{g}") for g in range(2)]
        s_vs = sem("v_staged")
        s_st = sem("scores_t")
        s_e = sem("probs_made")
        s_av = sem("probs_used")
        s_ot = sem("o_t_copied")
        s_to = sem("o_turned")
        s_on = sem("o_normalised")
        s_pj = sem("proj_products")
        s_dvp = sem("proj_copied")
        s_xa = sem("attention_added")
        s_ms = sem("row_moments_made")
        s_rs = sem("rstd_made")
        s_xr = sem("ffn_added")
        s_wl2 = sem("wgate_split")
        s_lg = sem("gate_logits")
        s_lc = sem("gate_logits_copied")
        s_cw = sem("expert_logits_shifted")
        s_ce = sem("expert_exp")
        s_f1 = sem("hidden_products")
        s_g = sem("gelu_made")
        s_h = sem("hidden_lo_made")
        s_h2 = sem("hidden_used")
        s_f2 = sem("ffn_products")
        s_ev = sem("ffn_copied")
        s_b2 = [sem(f"b2_loaded{i}") for i in range(2)]
        s_scd = sem("silu_stored")
        s_l3 = sem("l3_loaded")
        s_vc = sem("skew_made")
        s_vd = sem("skew_stored")
        s_uo = sem("skew_placed")
        s_p = sem("p_loaded")
        s_qr = sem("qr_steps")
        s_pace = sem("qr_pace")
        s_pp = sem("l3_products")
        s_pv = sem("l3_copied")
        s_zt = sem("last_turned")
        s_zf = sem("last_x_copied")
        s_zp = sem("last_z_products")
        s_zc = sem("last_z_copied")
        s_zo = sem("last_products")
        s_fin = sem("last_added")
        s_out = sem("stored")

        LOAD = 16 * 2 * len(PART_RUNS)
        QR_END = 9 + D3 * QR_OPS

        def tn(l, s, b):
            return 12 * l + (b if s == 0 else 3 + s + 2 * b)

        def add_unit(u):
            return 6 if u < UNITS - HM else 2

        NORMS = [(0, 0, b) for b in range(B)] + [(0, 2, b) for b in range(B)] + [(1, 0, b) for b in range(B)]
        for l in range(1, LAYERS):
            due = [(HM * b + 6 - O_STEPS, (l, 2, b)) for b in range(B)]
            if l + 1 < LAYERS:
                due += [(HM * (b + 1) + add_unit(HM * (b + 1)), (l + 1, 0, b)) for b in range(B - 1)] + [(UNITS, (l + 1, 0, B - 1))]
            NORMS += [norm for _, norm in sorted(due)]

        def steps_beside(j):
            late = {1: 0, 2: 1}
            res = []
            for b in range(B):
                for k in range(O_STEPS):
                    at_ = HM * b - O_STEPS + k
                    if b == 1:
                        at_ = late.get(k, at_)
                    if at_ == j:
                        res.append((b, k))
            return res

        def first_set(l):
            return 0 if l == 0 else EXPERTS + l - 1

        def sets_of(l):
            return [f for f, (a, _) in enumerate(SETS) if a == l]

        def steps_of(l):
            return UNITS * len(sets_of(l))

        def split_pieces(l, j):
            f, u = first_set(l) + j // UNITS, j % UNITS
            pieces, more = [], f != sets_of(l)[-1]
            if more and u >= UNITS - HM:
                pieces.append(("1", f + 1, u - (UNITS - HM)))
            if more and u >= UNITS - HM + 3:
                pieces.append(("2", f + 1, u - (UNITS - HM + 3)))
            if f != first_set(l) and u < 3:
                pieces.append(("2", f, HM - 3 + u))
            return pieces

        events = []
        for l in range(LAYERS):
            events += [("q", l, i) for i in range(3 * (KC + 1))] + ([("p", l)] if l == 0 else [])
            events += [("1", first_set(l)), ("2", first_set(l))]
            for j in range(steps_of(l)):
                events += split_pieces(l, j)
            if l + 1 < LAYERS:
                events.append(("p", l + 1))
        split_no = {k: i for i, k in enumerate(events)}

        def split_done(kind, f, m):
            return split_no[(kind, f, m) if (kind, f, m) in split_no else (kind, f)] + 1

        def loads(order):
            total, res = 0, {}
            for key, n in order:
                total += 16 * n
                res[key] = total
            return res

        order_a, order_b = [(("a", 0), 2)], [(("a", 0), 2)]
        for l in range(LAYERS):
            order_a.append((("q", l), 6))
            order_b.append((("p", l), 6))
            if l + 1 < LAYERS:
                order_a.append((("a", l + 1), 2))
                order_b.append((("a", l + 1), 2))
            for f in sets_of(l):
                order_a.append((("1", f), 6))
                order_b.append((("2", f), 1))
        RA, RB = loads(order_a), loads(order_b)

        def split_terms(H, L, T, XHi, XLo, XTa, wc, xc, tail):
            terms = []
            for c in range(KC):
                terms += [(H[:, c, wc], XHi[:, c, xc]), (L[:, c, wc], XHi[:, c, xc]), (H[:, c, wc], XLo[:, c, xc])]
            return terms + [(T[0:tail, wc], XTa[0:tail, xc])]

        def ada(l):
            return [ADA0, ADA[1]] if l == 0 else ADA

        def gate_rows(l, g):
            return (slice(0, B), 4 if l == 0 else 7 - g, slice(192 * g, 192 * g + C))

        QKV_CHUNKS = [(RAWQ[:, c, :], WQH[:, c, :]) for c in range(KC)] + [(RAWQ[0:TB, KC, :], WQT[:, :])]

        def qkv_cols(w, i, by_channel):
            cols = w[:, C * i:C * (i + 1)]
            if i == 2:
                return cols
            if by_channel:
                return cols.rearrange("p (g d h) -> p g d h", g=HG, h=4)
            return cols.rearrange("p (g h d) -> p g d h", g=HG, d=HD)

        block = ctx.enter_context(nc.Block())

        @block.sync
        def _(sp):
            x_v = x.rearrange("b (t p) c -> b p t c", p=P)

            def load_k288(dst, w, bias, s):
                sp.dma_start(dst[:, 0:KC, :], w[0:KC * P, :].rearrange("(k p) n -> p k n", p=P)).then_inc(s, 16)
                for r in range(3):
                    sp.dma_start(dst[r * TAIL:(r + 1) * TAIL, KC, :], w[KC * P:C, :]).then_inc(s, 16)
                for r in range(2):
                    sp.dma_start(dst[T3 + r:T3 + r + 1, KC, :], bias.unsqueeze(0)).then_inc(s, 16)

            def load_ada(l, h):
                cols, s = slice(3 * C * h, 3 * C * (h + 1)), (s_ra, s_rb)[h]
                dst = ada(l)[h]
                sp.dma_start(dst[0:96, :, :], layers[l]["ada_w"][:, cols].rearrange("(k p) n -> p k n", p=96)).then_inc(s, 16)
                sp.dma_start(dst[96:97, 0, :], layers[l]["ada_b"][cols].unsqueeze(0)).then_inc(s, 16)

            def ffn_weights(f):
                l, e = SETS[f]
                w = layers[l]
                if l == 0:
                    return w["w1"][e], w["b1"][e], w["w2"][e], w["b2"][e]
                return w["w1"], w["b1"], w["w2"], w["b2"]

            def load_w1(f):
                w1, b1, _, _ = ffn_weights(f)
                load_k288(RAW1, w1, b1, s_ra)

            def load_w2(f):
                _, _, w2, b2 = ffn_weights(f)
                sp.dma_start(RAW2, w2.rearrange("(k p) n -> p k n", p=P)).then_inc(s_rb, 16)
                sp.dma_start(B2B[:, f % 2, :], b2.partition_broadcast(P)).then_inc(s_b2[f % 2], 16)

            def store_gates(l):
                sp.wait_ge(s_gr, 2 * (l + 1))
                sp.dma_start(GD[l].rearrange("g b c -> b g c"), GROW[:, :, :]).then_inc(s_gd, 16)

            def load_gate(l, g):
                sp.wait_ge(s_gd, 16 * (l + 1))
                sp.dma_start((GMSA, GMLP)[g][:, :, :], GD[l][g].partition_broadcast(P)).then_inc((s_gm, s_gl)[g], 16)

            with nc.allow_non_contiguous_dma("columns of the condition"):
                for k in range(3):
                    sp.dma_start(SC[0:96, k, :], cond[:, 96 * k:96 * k + 96].rearrange("b p -> p b")).then_inc(s_in, 16)
            load_ada(0, 0)
            for b in range(B):
                sp.dma_start(XR[:, TT * b:TT * b + TT, :], x_v[b]).then_inc(s_x[b], 16)
                if b == 1:
                    sp.wait_ge(s_ra, RA["a", 0])
                    load_k288(RAWQ, layers[0]["qkv_w"], layers[0]["qkv_b"], s_ra)
                    load_ada(0, 1)
            sp.dma_start(QA[:, :, :], l3_P.rearrange("(k p) d -> p k d", p=96)).then_inc(s_p, 16)
            wg = layers[0]["w_gate"]
            with nc.allow_non_contiguous_dma("narrow gate weight"):
                sp.dma_start(WGR[:, 0:KC, :], wg[0:KC * P, :].rearrange("(k p) n -> p k n", p=P)).then_inc(s_wg, 16)
                for r in range(3):
                    sp.dma_start(WGR[r * TAIL:(r + 1) * TAIL, KC, :], wg[KC * P:C, :]).then_inc(s_wg, 16)
            sp.wait_ge(s_cst, 2)
            sp.dma_start(ONED.rearrange("g a p -> a g p"), ONE[:, :, :]).then_inc(s_one, 16)
            sp.wait_ge(s_sc, 2)
            with nc.allow_non_contiguous_dma("columns of the condition"):
                for k in range(3):
                    sp.dma_start(SCD[:, 96 * k:96 * k + 96].rearrange("b p -> p b"), SC[0:96, k, :]).then_inc(s_scd, 16)

            for l in range(LAYERS):
                if l + 1 < LAYERS:
                    sp.wait_ge(s_wl, split_no["q", l, 3 * (KC + 1) - 1] + 1)
                    load_ada(l + 1, 0)
                def load_stacks(bb, g):
                    for j, q, count in PART_RUNS:
                        place = slice(HD * j, HD * (j + count))
                        rows = [QKD[l][w, :, bass.ds(bb, 1), 4 * HD * g:4 * HD * (g + 1), :].rearrange("a o (d h) t -> a (o d) (h t)", h=4) for w in range(2)]
                        sp.dma_start(Q6[place, g, :, :].rearrange("p h t -> p (h t)"), rows[0][q:q + 1].to_broadcast([count, HD, 4 * N])).then_inc(s_ld[g], 16)
                        sp.dma_start(K6[place, g, :, :].rearrange("p h t -> p (h t)"), rows[1][0:count]).then_inc(s_ld[g], 16)

                def parts_stored(b):
                    tiles = 2 * QM * (B * l + b + 1)
                    for i in range(PARTS):
                        sp.wait_ge(s_pd[i], 16 * ((tiles - i + PARTS - 1) // PARTS))

                for b in range(B):
                    for m in range(2 * QM):
                        i = 2 * QM * (B * l + b) + m
                        sp.wait_ge(s_p3, i + 1)
                        sp.dma_start(QKD[l][m // QM, :, b, 96 * (m % QM):96 * (m % QM) + 96, :].rearrange("a p t -> p a t"),
                                     PT[:, i % PARTS, :, :]).then_inc(s_pd[i % PARTS], 16)
                    if l == 0 and b == 2:
                        sp.wait_ge(s_wl, split_no["p", 0] + 1)
                        load_ada(1, 1)
                    if b == 2:
                        sp.wait_ge(s_one, 16)
                        sp.wait_ge(s_tr, 3 * tn(l, 1, 0))
                        sp.wait_ge(s_lo, tn(l, 1, 0))
                        parts_stored(0)
                        load_stacks(0, 0)
                        sp.dma_start(K6[STK:STK + 1, :, :, :], ONED.rearrange("g a p -> (g a p)").rearrange("(o g h n) -> o g h n", o=1, g=HG, h=4)).then_inc(s_or, 16)
                    if l == 0 and b == 0:
                        sp.wait_ge(s_mod, 1)
                        load_k288(RAWP, layers[0]["out_w"], layers[0]["out_b"], s_rb)
                        store_gates(0)

                def place_max(bb, g):
                    sp.wait_ge(s_mc, 16 * l + 4 * bb + g + 1)
                    sp.dma_start(Q6[STK:STK + 1, g, :, :].rearrange("o h n -> o (h n)").rearrange("o (r p) -> o r p", p=P),
                                 MXT[:, g % 2, :]).then_inc(s_mr[g % 2], 16)

                parts_stored(B - 1)
                load_stacks(0, 1)
                load_stacks(0, 2)
                if l == 0:
                    load_gate(0, 0)
                    load_gate(0, 1)
                place_max(0, 0)
                f0 = first_set(l)

                def ffn_loads():
                    if l + 1 < LAYERS:
                        store_gates(l + 1)
                        sp.wait_ge(s_mod, l + 2)
                    else:
                        sp.wait_ge(s_wl, split_no["p", l] + 1)
                    load_w1(f0)
                    if f0 >= 2:
                        sp.wait_ge(s_ev, 16 * (f0 - 1))
                    load_w2(f0)

                def attention_loads(bb, last, beside=None):
                    for g in range(HG):
                        if not (last and g >= 1):
                            sp.wait_ge(s_st, 256 * l + 16 * (4 * bb + g) + 1)
                            load_stacks(bb + (g + 3) // 4, (g + 3) % 4)
                        if not (last and g == 3):
                            place_max(bb + (g + 1) // 4, (g + 1) % 4)
                        if g == 0 and beside:
                            beside()

                attention_loads(0, False, ffn_loads)
                with sp.Fori(1, B - 1) as bb:
                    attention_loads(bb, False)
                attention_loads(B - 1, True)

                for f in sets_of(l):
                    last = f == sets_of(l)[-1]
                    sp.wait_ge(s_wl, split_done("1", f, HM - 1))
                    if not last:
                        load_w1(f + 1)
                    elif l + 1 < LAYERS:
                        load_k288(RAWQ, layers[l + 1]["qkv_w"], layers[l + 1]["qkv_b"], s_ra)
                    sp.wait_ge(s_wl, split_done("2", f, HM - 1))
                    if not last:
                        if f >= 1:
                            sp.wait_ge(s_ev, 16 * f)
                        load_w2(f + 1)
                    elif l + 1 < LAYERS:
                        load_k288(RAWP, layers[l + 1]["out_w"], layers[l + 1]["out_b"], s_rb)
                    if f == f0 and l + 1 < LAYERS:
                        sp.wait_ge(s_xa, NT * (l + 1))
                        load_gate(l + 1, 0)
                    if f == V_SET - 1:
                        sp.wait_ge(s_lo, tn(0, 2, B - 1) + 1)
                        sp.wait_ge(s_scd, 48)
                        sp.dma_start(L3W[:, :, :], l3_W.rearrange("(p t) c -> p t c", t=VT_)).then_inc(s_l3, 16)
                        sp.dma_start(SCB[:, :, :], SCD.partition_broadcast(P)).then_inc(s_l3, 16)
                        sp.dma_start(BL[:, :], l3_b.rearrange("(p t) -> p t", t=VT_)).then_inc(s_l3, 16)
                    if f == V_SET:
                        sp.wait_ge(s_vc, 1)
                        sp.dma_start(VD.rearrange("b (p t) -> p b t", t=VT_), VC[:, :, :]).then_inc(s_vd, 16)
                        sp.wait_ge(s_vd, 16)
                        with nc.allow_non_contiguous_dma("the last row has one entry"):
                            for i in range(D3 - 1):
                                o = i * (D3 - 1) - i * (i - 1) // 2
                                sp.dma_start(UO[i:i + 1, :, i + 1:D3], VD[:, o:o + D3 - 1 - i].unsqueeze(0)).then_inc(s_uo, 16)
                if l + 2 < LAYERS:
                    sp.wait_ge(s_wl, split_no["p", l + 1] + 1)
                    load_ada(l + 2, 1)
                if l + 1 < LAYERS:
                    sp.wait_ge(s_xr, NT * (sets_of(l)[-1] + 1))
                    load_gate(l + 1, 1)

            out_v = out.rearrange("b (t p) c -> b p t c", p=P)
            for b in range(B):
                sp.wait_ge(s_fin, TT * (b + 1))
                sp.dma_start(out_v[b], XR[:, TT * b:TT * b + TT, :]).then_inc(s_out, 16)
            sp.wait_ge(s_out, 16 * B)

        @block.gpsimd
        def _(gp):
            gp.memset(IDN[:, :], 0.0).then_inc(s_qr, 1)
            gp.memset(QG[:, :, :], 1.0).then_inc(s_qr, 1)
            gp.memset(QO[:, :], 0.0).then_inc(s_qr, 1)
            gp.memset(SU[:, :], 1.0).then_inc(s_qr, 1)
            gp.memset(QC[:, :], 0.5).then_inc(s_qr, 1)
            gp.memset(MHALF[:, :], -0.5).then_inc(s_qr, 1)
            gp.wait_ge(s_qr, 6)
            gp.affine_select(out=IDN[:, :], in_=IDN[:, :], compare_op=ALU.not_equal, fill=1.0, base=0,
                             pattern=[[-1, P]], channel_multiplier=1).then_inc(s_cst, 1)
            gp.affine_select(out=QG[:, :, :], in_=QG[:, :, :], compare_op=ALU.is_ge, fill=0.0, base=0,
                             pattern=[[96, 3], [-1, D3]], channel_multiplier=1).then_inc(s_qr, 1)
            gp.affine_select(out=QO[:, :], in_=QO[:, :], compare_op=ALU.not_equal, fill=1.0, base=0,
                             pattern=[[-1, D3]], channel_multiplier=1).then_inc(s_qr, 1)
            gp.affine_select(out=SU[:, :], in_=SU[:, :], compare_op=ALU.is_gt, fill=0.0, base=0,
                             pattern=[[1, D3]], channel_multiplier=-1).then_inc(s_qr, 1)
            gp.wait_ge(s_qr, 9)

            half, vcol, oneh, sal = QC[:, 0:1], QC[:, 1:4], QC[:, 4:5], QC[:, 5:7]
            nrm, sg, sn, t_, d_, rs = (QC[:, i:i + 1] for i in range(7, 13))
            ohs, ucol, mhalf = QC[:, 13:14], QC[:, 14:17], QC[:, 17:18]
            s_, al = QC[:, 5:6], QC[:, 6:7]

            def norms(first, end):
                for n in range(first, end):
                    tiles = slice(TT * NORMS[n][2], TT * NORMS[n][2] + TT)
                    gp.wait_ge(s_ms, n + 1)
                    gp.tensor_scalar(RST[:, tiles], MV[:, tiles, 1], LN_EPS, 1.0, ALU.add, ALU.mult).then_inc(s_rs, 1)
                    gp.wait_ge(s_rs, 2 * n + 1)
                    gp.tensor_tensor(RST[:, tiles], RST[:, tiles], MHALF[:, :], ALU.pow).then_inc(s_rs, 1)

            def reflectors(first, end):
                with gp.Fori(first, end) as k:
                    done = [0]

                    def step(i, pace=False):
                        i.then_inc(s_qr, 1)
                        done[0] += 1
                        gp.wait_ge(s_qr, 9 + QR_OPS * k + done[0])
                        if pace:
                            gp.sem_inc(s_pace, 1)

                    kk = bass.ds(k, 1)
                    step(gp.memset(mhalf, -0.5))
                    step(gp.tensor_tensor(vcol, QA[:, :, kk].rearrange("p c o -> p (c o)"), QG[:, :, kk].rearrange("p c o -> p (c o)"), ALU.mult))
                    step(gp.tensor_copy(oneh, QO[:, kk]))
                    step(gp.tensor_tensor(QM1[:, :, :], QA[:, :, :], vcol.unsqueeze(2).to_broadcast([96, 3, D3]), ALU.mult))
                    step(gp.tensor_tensor(QI[:, 0, :], QM1[:, 0, :], QM1[:, 1, :], ALU.add))
                    step(gp.tensor_tensor(QI[:, 0, :], QI[:, 0, :], QM1[:, 2, :], ALU.add))
                    step(gp.tensor_tensor(QI[:, 1, :], QA[:, 0, :], oneh.to_broadcast([96, D3]), ALU.mult), pace=True)
                    step(gp.partition_all_reduce(QS[:, :, :].rearrange("p a d -> p (a d)"), QI[:, :, :].rearrange("p a d -> p (a d)"), channels=96, reduce_op=ADD))
                    step(gp.tensor_copy(sal, QS[:, :, kk].rearrange("p a o -> p (a o)")))
                    step(gp.tensor_tensor(nrm, s_, half, ALU.pow), pace=True)
                    step(gp.tensor_scalar(sg, al, 0.0, 2.0, ALU.is_ge, ALU.mult), pace=True)
                    step(gp.tensor_scalar(sn, sg, -1.0, nrm, ALU.add, ALU.mult))
                    step(gp.tensor_tensor(t_, al, sn, ALU.mult), pace=True)
                    step(gp.tensor_scalar(d_, t_, s_, TINY, ALU.add, ALU.max))
                    step(gp.tensor_tensor(rs, d_, mhalf, ALU.pow), pace=True)
                    step(gp.tensor_scalar(QW[:, :], QS[:, 1, :], sn, rs, ALU.mult, ALU.mult), pace=True)
                    step(gp.tensor_scalar(QI[:, 0, :], QS[:, 0, :], rs, 1.0, ALU.mult, ALU.mult))
                    step(gp.tensor_tensor(QW[:, :], QW[:, :], QI[:, 0, :], ALU.add))
                    step(gp.tensor_tensor(ohs, oneh, sn, ALU.mult))
                    step(gp.tensor_tensor(vcol[:, 0:1], vcol[:, 0:1], ohs, ALU.add))
                    step(gp.tensor_tensor(ucol, vcol, rs.to_broadcast([96, 3]), ALU.mult))
                    step(gp.tensor_copy(QV[:, :, kk].rearrange("p c o -> p (c o)"), ucol))
                    step(gp.tensor_tensor(QM1[:, :, :], ucol.unsqueeze(2).to_broadcast([96, 3, D3]), QW[:, :].unsqueeze(1).to_broadcast([96, 3, D3]), ALU.mult))
                    step(gp.tensor_tensor(QA[:, :, :], QA[:, :, :], QM1[:, :, :], ALU.subtract))
                    assert done[0] == QR_OPS

            norms(0, B)
            gp.wait_ge(s_p, 16)
            reflectors(0, QR_CUTS[0])
            norms(B, 2 * B)
            reflectors(*QR_CUTS)
            norms(2 * B, 3 * B)
            reflectors(QR_CUTS[1], D3)
            norms(3 * B, len(NORMS))

        @block.scalar
        def _(act):
            def mod_row(l, g):
                if g == 0:
                    act.wait_ge(s_m0, 2 * l + 2)
                else:
                    act.wait_ge(s_mod, l + 1)
                if g == 1:
                    act.wait_ge(s_mc_, l + 2)
                act.activation(GROW[:, g, :], psum[gate_rows(l, g)], ACT.Copy).then_inc(s_gr, 1)

            def split_hi_qkv(l):
                act.wait_ge(s_ra, RA["q", l])
                for w in range(3):
                    for raw, H in QKV_CHUNKS:
                        act.activation(qkv_cols(H, w, True), qkv_cols(raw, w, False), ACT.Copy).then_inc(s_wsp, 1)

            def split_hi(kind, n, raw, H, T, s, value):
                act.wait_ge(s, value)
                if T is None:
                    act.activation(H[:, :, :], raw, ACT.Copy).then_inc(s_wsp, 1)
                else:
                    act.activation(H[:, :, :], raw[:, 0:KC, :], ACT.Copy)
                    act.activation(T[0:TB, :], raw[0:TB, KC, :], ACT.Copy).then_inc(s_wsp, 1)

            def split_hi_tile(kind, f, m):
                if kind == "1":
                    if m == 0:
                        act.wait_ge(s_ra, RA["1", f])
                    cols = slice(P * m, P * m + P)
                    act.activation(W1H[:, :, cols], RAW1[:, 0:KC, cols], ACT.Copy)
                    act.activation(W1T[0:TB, cols], RAW1[0:TB, KC, cols], ACT.Copy).then_inc(s_wsp, 1)
                else:
                    if m == 0:
                        act.wait_ge(s_rb, RB["2", f])
                    if m < HM - 1:
                        act.wait_ge(s_h2, (HM - 1) * (B * f - 1) + m + 1)
                    else:
                        act.wait_ge(s_f2, NT * f)
                    act.activation(W2H[:, m, :], RAW2[:, m, :], ACT.Copy).then_inc(s_wsp, 1)

            def turned(l, s, b, chunks=range(KC + 1)):
                n = tn(l, s, b)
                for c in chunks:
                    rows = P if c < KC else T3
                    act.wait_ge(s_tr, 3 * n + c + 1)
                    if n >= 1:
                        act.wait_ge(s_lo, n)
                    src = psum[0:rows, CHUNK_BANK[c], :]
                    if s == 1:
                        act.activation(FX[0:rows, c, :], src, ACT.Copy).then_inc(s_fx, 1)
                    else:
                        act.activation(FX[0:rows, c, :], src, ACT.Identity,
                                       bias=MODC[0:rows, l, s, c, b:b + 1], scale=MODC[0:rows, l, s + 1, c, b:b + 1]).then_inc(s_fx, 1)
                    act.wait_ge(s_fx, 3 * n + c + 1)
                    if s == 1:
                        if b >= 1:
                            act.wait_ge(s_pj, NT * l + TT * b)
                        dst = OH_[:, c, :] if c < KC else OX[0:T3, :]
                    else:
                        dst = XS[:, b, 0, c, :] if c < KC else XT[0:T3, N * b:N * b + N]
                    act.activation(dst, FX[0:rows, c, :], ACT.Copy).then_inc(s_hi, 1)

            def qk_part1(i):
                act.wait_ge(s_r1, i + 1)
                act.activation(PT[:, i % PARTS, 1, :], QR[:, i % 3, :], ACT.Copy).then_inc(s_p2, 1)

            def qk_parts(l, b):
                for m in range(2 * QM):
                    i = 2 * QM * (B * l + b) + m
                    if m == 2 * QM - 1:
                        values(l, b, (0, 1))
                    act.wait_ge(s_qk, i + 1)
                    if i >= PARTS:
                        act.wait_ge(s_pd[i % PARTS], 16 * (i // PARTS))
                    act.activation(PT[:, i % PARTS, 0, :], psum[0:96, QK_BANK[i % 3], :], ACT.Copy).then_inc(s_p1, 1)
                    if b >= 1 or m >= 1:
                        qk_part1(i - 1)
                if b == B - 1:
                    qk_part1(i)
                values(l, b, (2, 3))

            def values(l, b, tiles):
                for t in tiles:
                    i = NT * l + TT * b + t
                    act.wait_ge(s_vm, i + 1)
                    act.activation(V[:, TT * b + t, :], psum[:, 5 + i % 2, 0:C], ACT.Copy).then_inc(s_v, 1)

            def o_t(l, i):
                act.wait_ge(s_av, 64 * l + 4 * i + 4)
                act.activation(OT[:, bass.ds(i, 1), :].rearrange("p o n -> p (o n)"), bk(6), ACT.Copy).then_inc(s_ot, 1)

            def attention(l, bb, g, first=False):
                i = 4 * bb + g
                for v in range(16):
                    act.wait_ge(s_st, 256 * l + 16 * i + v + 1)
                    if v % 4 == 0 and not first:
                        act.wait_ge(s_av, 64 * l + 4 * i + v // 4 - 3)
                    act.activation(PE_[:, v // 4, v % 4, :], psum[:, 4 + v % 2, :], ACT.Exp, scale=SCALE).then_inc(s_e, 1)
                    if v == 3 and first and l + 1 < LAYERS:
                        mod_row(l + 1, 1)
                    if v == 7 and not first:
                        o_t(l, 4 * bb + (g - 1))

            act.wait_ge(s_in, 48)
            act.activation(SCT[:, 0, :], SC[0:96, :, :].rearrange("p k b -> p (k b)"), ACT.Exp, scale=-1.0).then_inc(s_sce, 1)
            for l in range(LAYERS):
                if l == 0:
                    split_hi_qkv(l)
                    act.wait_ge(s_mc_, 1)
                    turned(l, 0, 0)
                    turned(l, 0, 1)
                    mod_row(l, 0)
                    qk_parts(l, 0)
                    turned(l, 0, 2)
                    mod_row(l, 1)
                    qk_parts(l, 1)
                    turned(l, 0, 3)
                    act.wait_ge(s_wg, 64)
                    act.activation(WGH[:, :, :], WGR[:, 0:KC, :], ACT.Copy)
                    act.activation(WGT[:, :], WGR[0:T3, KC, :], ACT.Copy).then_inc(s_ce, 1)
                    split_hi("p", l, RAWP, WPH, WPT, s_rb, RB["p", l])
                else:
                    split_hi_qkv(l)
                    qk_parts(l, 0)
                    qk_parts(l, 1)
                    turned(l, 0, 3)
                qk_parts(l, 2)
                qk_parts(l, 3)
                if l + 1 < LAYERS:
                    mod_row(l + 1, 0)
                attention(l, 0, 0, first=True)
                with act.Fori(0, B - 1) as bb:
                    for g in range(1, HG + 1):
                        attention(l, bb, g)
                for g in range(1, HG):
                    attention(l, B - 1, g)
                f0, J = first_set(l), steps_of(l)
                act.wait_ge(s_ra, RA["1", f0])
                act.wait_ge(s_av, 64 * l + 4 * (B * HG - 1) + 2)
                act.activation(W1H[:, :, :], RAW1[:, 0:KC, :], ACT.Copy)
                o_t(l, B * HG - 1)

                for j in range(FIRST, J):
                    u = j % UNITS
                    if j >= 0:
                        i = UNITS * f0 + j
                        act.wait_ge(s_f1, i + 1)
                        if i >= 2:
                            act.wait_ge(s_h, i - 1)
                        act.activation(HF[:, i % 2, :], bk(i % 2), ACT.Gelu_apprx_tanh).then_inc(s_g, 1)
                    if j == FIRST:
                        act.activation(W1T[0:TB, :], RAW1[0:TB, KC, :], ACT.Copy).then_inc(s_wsp, 1)
                    for b, k in steps_beside(j):
                        if k in (2, 8):
                            turned(l, 1 if k == 2 else 2, b, (0, 1))
                        if k in (3, 9):
                            turned(l, 1 if k == 3 else 2, b, (2,))
                    if j == -1:
                        act.activation(SCT[:, 0, :], SCT[:, 1, :], ACT.Gelu_apprx_tanh)
                        split_hi("2", f0, RAW2, W2H, None, s_rb, RB["2", f0])
                    for piece in split_pieces(l, j) if j >= 0 else ():
                        split_hi_tile(*piece)
                    if l == 0 and 0 <= j < UNITS and j % HM == 7:
                        act.wait_ge(s_cw, j // HM + 1)
                        tiles = slice(TT * (j // HM), TT * (j // HM + 1))
                        act.activation(CW[:, tiles, :], LG[:, tiles, :], ACT.Exp).then_inc(s_ce, 1)
                    if l + 1 < LAYERS and j == J - UNITS + P_UNIT:
                        split_hi("p", l + 1, RAWP, WPH, WPT, s_rb, RB["p", l + 1])
                    if l + 1 < LAYERS and j >= J - UNITS:
                        for b, first in enumerate(NEXT_UNIT):
                            if u == first + 2:
                                turned(l + 1, 0, b, (0, 1))
                            if u == first + 3:
                                turned(l + 1, 0, b, (2,))

            def last_x(b):
                for c in range(KC + 1):
                    rows = P if c < KC else TAIL
                    act.wait_ge(s_zt, 3 * b + c + 1)
                    if b >= 1:
                        act.wait_ge(s_zp, b)
                    act.activation(FX[0:rows, c, :], psum[0:rows, c, :], ACT.Copy).then_inc(s_zf, 1)

            last_x(0)
            for b in range(B):
                act.wait_ge(s_zp, b + 1)
                if b >= 1:
                    act.wait_ge(s_zo, TT * b)
                act.activation(ZT[:, :], psum[0:D3, 3, :], ACT.Copy).then_inc(s_zc, 1)
                if b + 1 < B:
                    last_x(b + 1)

        @block.tensor
        def _(pe):
            def products(dst, terms, stop=True):
                for n, (a, r) in enumerate(terms):
                    i = pe.matmul(dst, a, r, start=(n == 0), stop=(n == len(terms) - 1))
                return i

            MOD_PRODUCTS = 4 * (KC + 1) + 2
            MOD_HALF = 2 * (KC + 1)
            FIRST_MODS = [*range(MOD_HALF), MOD_PRODUCTS - 2]
            LAST_MODS = [*range(MOD_HALF, 2 * MOD_HALF), MOD_PRODUCTS - 1]

            def mod(l, n):
                if n == 0:
                    pe.wait_ge(s_ra, RA["a", l])
                if n == MOD_HALF:
                    pe.wait_ge(s_rb, RB["a", l])
                    if l == 0:
                        pe.wait_ge(s_gr, 1)
                if n < 4 * (KC + 1):
                    v, c = divmod(n, KC + 1)
                    vec = (0, 1, 3, 4)[v]
                    rows = P if c < KC else TAIL
                    bank = 4 if l == 0 and n >= MOD_HALF else 6
                    place = (slice(0, rows), bank, slice(P + n * B, P + n * B + B))
                    cols = slice((vec % 3) * C + c * P, (vec % 3) * C + c * P + rows)
                else:
                    vec = 2 + 3 * (n - 4 * (KC + 1))
                    place = gate_rows(l, vec // 3)
                    cols = slice(2 * C, 3 * C)
                for k in range(3):
                    K = 97 if k == 0 else 96
                    w, c_ = ada(l)[vec // 3][0:K, k, cols], SC[0:K, k, :]
                    lhs, rhs = (w, c_) if n < 4 * (KC + 1) else (c_, w)
                    i = pe.matmul(psum[place], lhs, rhs, start=(k == 0), stop=(k == 2))
                if n in (MOD_HALF - 1, FIRST_MODS[-1]):
                    i.then_inc(s_m0, 1)
                if n == MOD_PRODUCTS - 1:
                    i.then_inc(s_mod, 1)

            def turn(l, s, b, chunks=range(KC + 1)):
                n = tn(l, s, b)
                for c in chunks:
                    rows = P if c < KC else T3
                    if c == 0:
                        pe.wait_ge(s_xn, n + 1)
                        if n >= 1:
                            pe.wait_ge(s_fx, 3 * n)
                    if c == 1 and l == 0 and s == 2 and b >= 1:
                        pe.wait_ge(s_lc, b)
                    if c == 2:
                        pe.wait_ge(s_fx, 3 * n + 1)
                    for t in range(TT):
                        i = pe.transpose(psum[0:rows, CHUNK_BANK[c], P * t:P * t + P], XN[n % 2][:, t, P * c:P * c + rows], IDN[:, :])
                    i.then_inc(s_tr, 1)

            def qkv(l, b):
                pe.wait_ge(s_lo, tn(l, 0, b) + 1)
                for m in range(2 * QM):
                    i = 2 * QM * (B * l + b) + m
                    if b == 0 and m % QM == 0:
                        pe.wait_ge(s_wl, split_no["q", l, (KC + 1) * (m // QM + 1) - 1] + 1)
                    if i >= 3:
                        pe.wait_ge(s_r1, i - 2)
                    if l >= 1 and b == 0 and m == 2:
                        pe.wait_ge(s_ev, NT * (sets_of(l - 1)[-1] + 1))
                    products(psum[0:96, QK_BANK[i % 3], :], split_terms(WQH, WQL, WQT, XS[:, b, 0], XS[:, b, 1], XT[:, N * b:N * b + N],
                                                                        slice(96 * m, 96 * m + 96), slice(0, N), TB)).then_inc(s_qk, 1)
                if b == 0:
                    pe.wait_ge(s_wl, split_no["q", l, 3 * (KC + 1) - 1] + 1)
                for t in range(TT):
                    i = NT * l + TT * b + t
                    if i >= 2:
                        pe.wait_ge(s_v, i - 1)
                    terms = split_terms(WQH, WQL, WQT, XS[:, b, 0], XS[:, b, 1], XT[:, N * b:N * b + N],
                                        slice(2 * C, 3 * C), slice(P * t, P * t + P), TB)
                    products(psum[:, 5 + i % 2, 0:C], [(r, a) for a, r in terms]).then_inc(s_vm, 1)

            def l_first_scores(bb, g, u):
                return isinstance(bb, int) and bb == 0 and g == 0 and u == 0

            def scores(l, bb, g, u):
                i = 4 * bb + g
                if l_first_scores(bb, g, u):
                    pe.wait_ge(s_or, 16 * (l + 1))
                if u == 0:
                    pe.wait_ge(s_ld[g], LOAD * B * l + LOAD * (bb + 1))
                need = 128 * l + 8 * i + u - 1
                if not isinstance(need, int) or need > 0:
                    pe.wait_ge(s_mx, need)
                for j in range(2):
                    qt = 2 * (u % 2) + j
                    mm = pe.matmul(psum[:, 2 * (u % 2) + j, :], Q6[0:STK, g, u // 2, P * qt:P * qt + P], K6[0:STK, g, u // 2, :], start=True, stop=True)
                mm.then_inc(s_s, 1)

            def turn_max(l, bb, g):
                i = 4 * bb + g
                pe.wait_ge(s_mx, 128 * l + 8 * (i + 1))
                pe.wait_ge(s_mc, 16 * l + i)
                pe.transpose(psum[0:16, 7, 0:P], MX[:, g % 2, :], IDN[:, :]).then_inc(s_mt, 1)

            def scores_t(l, bb, g, v, first):
                i = 4 * bb + g
                if v == 0:
                    pe.wait_ge(s_mr[g % 2], 128 * l + 16 * (2 * bb + g // 2 + 1))
                if not first or v >= 2:
                    pe.wait_ge(s_e, 256 * l + 16 * i + v - 1)
                kt, h = v // 4, v % 4
                pe.matmul(psum[:, 4 + v % 2, :], K6[0:STK + 1, g % 4, h, P * kt:P * kt + P], Q6[0:STK + 1, g % 4, h, :], start=True, stop=True).then_inc(s_st, 1)

            def use_probs(l, bb, g, kt, half, first):
                i = 4 * bb + g
                if half == 0:
                    pe.wait_ge(s_e, 256 * l + 16 * i + 4 * kt + 4)
                    if kt == 0:
                        pe.wait_ge(s_vs, 16 * l + i + 1)
                        if not first:
                            pe.wait_ge(s_ot, 16 * l + i)
                q = slice(N // 2 * half, N // 2 * (half + 1))
                for h in range(4):
                    mm = pe.matmul(psum[32 * h:32 * h + 32, 6, q], VST[:, g % 4, kt, h, :], PE_[:, kt, h, q],
                                   start=(kt == 0 and half == 0), stop=(kt == TT - 1 and half == 1))
                if half == 1:
                    mm.then_inc(s_av, 1)

            def attention(l, bb, g, first=False, last=False):
                for u in range(8):
                    scores_t(l, bb, g, 2 * u, first)
                    if u == 1 and not (last and g == 3):
                        turn_max(l, bb + (g + 1) // 4, (g + 1) % 4)
                    if not (last and g >= 2):
                        scores(l, bb + (g + 2) // 4, (g + 2) % 4, u)
                    scores_t(l, bb, g, 2 * u + 1, first)
                    if u == 4 and first and l + 1 < LAYERS:
                        pe.wait_ge(s_gr, 2 * (l + 2))
                    if u >= 4:
                        use_probs(l, bb, g, u // 2 - 2, u % 2, first)
                    elif not first:
                        use_probs(l, bb, g - 1, 2 + u // 2, u % 2, first)
                    if last and (g, u) in TAIL_STEPS:
                        to_ffn(l, 0, TAIL_STEPS[g, u])

            def turn_o(l, b, t):
                i = NT * l + TT * b + t
                if t == 0:
                    pe.wait_ge(s_ot, 16 * l + 4 * (b + 1))
                if t <= 1:
                    pe.wait_ge(s_fx, 3 * tn(l, 1, b) - t)
                if t >= 2:
                    pe.wait_ge(s_on, i - 1)
                for g in range(HG):
                    mm = pe.transpose(psum[:, 2 + t % 2, P * g:P * g + P], OT[:, 4 * b + g, P * t:P * t + P], IDN[:, :])
                mm.then_inc(s_to, 1)

            def proj(l, b, t):
                i = NT * l + TT * b + t
                if t == 0:
                    pe.wait_ge(s_lo, tn(l, 1, b) + 1)
                    if b == 0:
                        pe.wait_ge(s_wl, split_no["p", l] + 1)
                if t >= 2:
                    pe.wait_ge(s_dvp, i - 1)
                terms = split_terms(WPH, WPL, WPT, OH_, OL, OX, slice(0, C), slice(P * t, P * t + P), TB)
                products(psum[:, 2 + t % 2, 0:C], [(r, a) for a, r in terms]).then_inc(s_pj, 1)

            def logits(b):
                pe.wait_ge(s_lo, tn(0, 2, b) + 1)
                pe.wait_ge(s_wl2, 1)
                if b + 1 < B:
                    pe.wait_ge(s_dvp, TT * (b + 2))
                for t in range(TT):
                    terms = split_terms(WGH, WGL, WGT, XS[:, b, 0], XS[:, b, 1], XT[:, N * b:N * b + N],
                                        slice(0, EXPERTS), slice(P * t, P * t + P), T3)
                    mm = products(psum[:, 3, EXPERTS * t:EXPERTS * t + EXPERTS], [(r, a) for a, r in terms])
                mm.then_inc(s_lg, 1)

            def to_ffn(l, b, k):
                if k in (0, 1):
                    turn_o(l, b, 2 * k)
                    turn_o(l, b, 2 * k + 1)
                elif k in (2, 8):
                    turn(l, 1 if k == 2 else 2, b, (0, 1))
                elif k in (3, 9):
                    turn(l, 1 if k == 3 else 2, b, (2,))
                elif k in (4, 5):
                    proj(l, b, 2 * (k - 4))
                    proj(l, b, 2 * (k - 4) + 1)

            def hidden(f, u):
                l = SETS[f][0]
                b, m = u // HM, u % HM
                i = UNITS * f + u
                if b == 0:
                    pe.wait_ge(s_wl, split_done("1", f, m))
                if m == 0:
                    pe.wait_ge(s_lo, tn(l, 2, b) + 1)
                if i >= 2:
                    pe.wait_ge(s_g, i - 1)
                products(bk(i % 2), split_terms(W1H, W1L, W1T, XS[:, b, 0], XS[:, b, 1], XT[:, N * b:N * b + N],
                                                slice(P * m, P * m + P), slice(0, N), TB)).then_inc(s_f1, 1)

            def second(f, u):
                b, m = u // HM, u % HM
                grp = B * f + b
                pe.wait_ge(s_h, UNITS * f + u + 1)
                if b == 0:
                    pe.wait_ge(s_wl, split_done("2", f, m))
                for t in range(TT):
                    if m == 0 and grp >= 1:
                        pe.wait_ge(s_ev, TT * (grp - 1) + t + 1)
                    c = slice(P * t, P * t + P)
                    for n, (h, w) in enumerate(((HH, W2H), (HH, W2L), (HL, W2H))):
                        mm = pe.matmul(psum[:, 4 + t, 0:C], h[:, m % 3, c], w[:, m, :], start=(m == 0 and n == 0), stop=(m == HM - 1 and n == 2))
                    if m == HM - 1:
                        mm.then_inc(s_f2, 1)
                if m < HM - 1:
                    mm.then_inc(s_h2, 1)

            def l3_begin(n):
                pe.wait_ge(s_pv, n)

            def expm_step(n):
                if n == 0:
                    pe.wait_ge(s_uo, 16 * (D3 - 1))
                l3_begin(n)
                if n == 0:
                    for b in range(B):
                        mm = pe.transpose(psum[0:D3, 3, D3 * b:D3 * b + D3], UO[:, b, :], IDN[0:D3, 0:D3])
                elif n == 1:
                    mm = pe.transpose(psum[0:B, 3, 0:D3], NRM[:, 0:B], IDN[0:D3, 0:D3])
                elif n == 2:
                    mm = pe.matmul(psum[0:D3, 3, 0:B], NBC[:, 4:4 + D3], IDN[0:B, 0:B], start=True, stop=True)
                else:
                    for s in range(2):
                        for b in range(B):
                            lhs = AS[:, 1 - s, b, :] if n < 3 + TAYLOR - 1 else RR[:, 1 - s, b, :]
                            mm = pe.matmul(psum[0:D3, 3, D3 * (B * s + b):D3 * (B * s + b + 1)], lhs, RR[:, s, b, :], start=True, stop=True)
                mm.then_inc(s_pp, 1)

            def u_step(n):
                if n == 0:
                    pe.wait_ge(s_qr, QR_END)
                l3_begin(EXPM_STEPS + n)
                o = psum[0:D3, 3, 0:D3]
                o2 = psum[0:D3, 3, D3:2 * D3]
                if n == 0:
                    for c in range(3):
                        mm = pe.matmul(o, QV[:, c, :], QV[:, c, :], start=(c == 0), stop=(c == 2))
                elif n == 1:
                    for c in range(3):
                        mm = pe.transpose(psum[0:D3, 3, 96 * c:96 * c + 96], QV[:, c, :], IDN[0:96, 0:96])
                elif n == 2:
                    mm = pe.transpose(o, NW[:, 0, :], IDN[0:D3, 0:D3])
                elif n < 3 + 12:
                    if n % 2 == 1:
                        mm = pe.matmul(o, NW[:, 1, :], NW[:, 2, :], start=True, stop=True)
                    else:
                        pe.matmul(o, NW[:, 3, :], NW[:, 4, :], start=True, stop=True)
                        mm = pe.matmul(o2, NW[:, 4, :], NW[:, 3, :], start=True, stop=True)
                elif n == 15:
                    mm = pe.matmul(o, NW[:, 3, :], VTR[:, 0:D3], start=True, stop=True)
                elif n == 16:
                    mm = pe.matmul(psum[0:D3, 3, 0:C], NW[:, 5, :], VTR[:, :], start=True, stop=True)
                else:
                    for c in range(KC + 1):
                        rows = P if c < KC else TAIL
                        dst = psum[0:rows, 3, B * D3 * c:B * D3 * (c + 1)] if c < KC else psum[0:rows, 2, 0:B * D3]
                        mm = pe.matmul(dst, UTT[:, P * c:P * c + rows], RR[:, 0, :, :].rearrange("p b d -> p (b d)"), start=True, stop=True)
                mm.then_inc(s_pp, 1)

            def turn_last(b):
                pe.wait_ge(s_xr, NT * (len(SETS) - 1) + TT * (b + 1))
                if b == 0:
                    pe.wait_ge(s_g, UNITS * len(SETS))
                    pe.wait_ge(s_pv, EXPM_STEPS + U_STEPS)
                for c in range(KC + 1):
                    rows = P if c < KC else TAIL
                    if b >= 1:
                        pe.wait_ge(s_zf, 3 * b - 2 + c)
                    for t in range(TT):
                        mm = pe.transpose(psum[0:rows, c, P * t:P * t + P], XR[:, TT * b + t, P * c:P * c + rows], IDN[:, :])
                    mm.then_inc(s_zt, 1)

            def change_last(b):
                pe.wait_ge(s_zc, b + 1)
                for t in range(TT):
                    if b == 0:
                        pe.wait_ge(s_ev, NT * len(SETS))
                    else:
                        pe.wait_ge(s_fin, TT * (b - 1) + t + 1)
                    pe.matmul(psum[:, 4 + t, 0:C], ZT[:, P * t:P * t + P], UTT[:, :], start=True, stop=True).then_inc(s_zo, 1)

            pe.wait_ge(s_cst, 2)
            pe.wait_ge(s_sc, 2)
            for n in FIRST_MODS:
                mod(0, n)
            for l in range(LAYERS):
                if l == 0:
                    turn(l, 0, 0)
                    turn(l, 0, 1)
                    qkv(l, 0)
                    turn(l, 0, 2)
                    for n in LAST_MODS:
                        mod(l, n)
                    qkv(l, 1)
                    turn(l, 0, 3)
                else:
                    qkv(l, 0)
                    qkv(l, 1)
                    turn(l, 0, 3)
                qkv(l, 2)
                qkv(l, 3)
                pe.wait_ge(s_r1, 2 * QM * B * (l + 1))
                pe.wait_ge(s_fx, 3 * tn(l, 1, 0))
                for g in range(2):
                    for u in range(8):
                        scores(l, 0, g, u)
                        if g == 0 and u == 0:
                            pe.wait_ge(s_v, NT * (l + 1))
                        if (g, u) == (1, 1):
                            if l + 1 < LAYERS:
                                pe.wait_ge(s_gr, 2 * (l + 1) + 1)
                            turn_max(l, 0, 0)
                        if l + 1 < LAYERS and u < len(FIRST_MODS):
                            mod(l + 1, (FIRST_MODS, LAST_MODS)[g][u])
                attention(l, 0, 0, first=True)
                with pe.Fori(0, B - 1) as bb:
                    for g in range(1, HG + 1):
                        attention(l, bb, g)
                for g in range(1, HG):
                    attention(l, B - 1, g, last=True)
                for u in range(4):
                    use_probs(l, B - 1, HG - 1, 2 + u // 2, u % 2, False)

                f0, J = first_set(l), steps_of(l)
                for j in range(FIRST, J + 2):
                    f, u = f0 + j // UNITS, j % UNITS
                    if 0 <= j < J:
                        hidden(f, u)
                        if f == U_SET and u >= U_UNIT:
                            u_step(2 * (u - U_UNIT))
                    if j >= 2:
                        second(f0 + (j - 2) // UNITS, (j - 2) % UNITS)
                    if l == LAYERS - 1 and j == J:
                        turn_last(0)
                    for b, k in steps_beside(j):
                        to_ffn(l, b, k)
                    if l == 0 and 0 <= j < UNITS and u % HM == 5:
                        logits(u // HM)
                    if 0 <= UNITS * f + u - EXPM_START < EXPM_STEPS:
                        expm_step(UNITS * f + u - EXPM_START)
                    if f == U_SET and u >= U_UNIT and 0 <= j:
                        u_step(2 * (u - U_UNIT) + 1)
                    if l + 1 < LAYERS and J - UNITS <= j < J:
                        for b, first in enumerate(NEXT_UNIT):
                            if u == first + 2:
                                turn(l + 1, 0, b, (0, 1))
                            if u == first + 3:
                                turn(l + 1, 0, b, (2,))

            for b in range(B):
                pe.wait_ge(s_zf, 3 * b + 3)
                for c in range(KC + 1):
                    rows = P if c < KC else TAIL
                    mm = pe.matmul(psum[0:D3, 3, :], GG[0:rows, c, D3 * b:D3 * b + D3], FX[0:rows, c, :], start=(c == 0), stop=(c == KC))
                mm.then_inc(s_zp, 1)
                if b + 1 < B:
                    turn_last(b + 1)
                change_last(b)

        @block.vector
        def _(dve):
            steps = [0]

            def link(i):
                i.then_inc(s_dv, 1)
                steps[0] += 1
                dve.wait_ge(s_dv, steps[0])

            def mods(l, vecs=range(4)):
                early = l == 0 and 0 in vecs
                dve.wait_ge(*((s_m0, 1) if early else (s_mod, l + 1)))
                mp = psum[:, 4 if l == 0 and not early else 6, P:P + 4 * (KC + 1) * B].rearrange("p (v n) -> p v n", v=4)
                mc = MODC[:, l, :, :, :].rearrange("p v c b -> p v (c b)")
                shift, scale = slice(vecs[0], vecs[-1] + 1, 2), slice(vecs[1], vecs[-1] + 1, 2)
                full, tail = slice(0, KC * B), slice(KC * B, (KC + 1) * B)
                for to, rows, cols in ((0, P, full), *((r * TAIL, TAIL, tail) for r in range(3))):
                    dve.tensor_copy(mc[to:to + rows, shift, cols], mp[0:rows, shift, cols])
                    i = dve.tensor_scalar(mc[to:to + rows, scale, cols], mp[0:rows, scale, cols], 1.0, None, ALU.add)
                i.then_inc(s_mc_, 1)

            def split_lo_qkv(l, w):
                for n, (raw, H) in enumerate(QKV_CHUNKS):
                    dve.wait_ge(s_wsp, split_no["q", l, (KC + 1) * w + n] + 1)
                    if n < KC:
                        L, rows = WQL[:, n, :], slice(0, P)
                    else:
                        L, rows = WQT[:, :], slice(2 * TAIL, T3 + 1)
                    dve.tensor_tensor(qkv_cols(L[rows], w, True), qkv_cols(raw[rows], w, False),
                                      qkv_cols(H[rows], w, True).bitcast(F32), ALU.subtract).then_inc(s_wl, 1)

            def split_lo(key, raw, H, L, T):
                n = split_no[key]
                dve.wait_ge(s_wsp, n + 1)
                if T is None:
                    dve.tensor_tensor(L[:, :, :], raw, H[:, :, :].bitcast(F32), ALU.subtract).then_inc(s_wl, 1)
                    return
                dve.tensor_tensor(L[:, :, :], raw[:, 0:KC, :], H[:, :, :].bitcast(F32), ALU.subtract)
                dve.tensor_tensor(T[2 * TAIL:T3 + 1, :], raw[2 * TAIL:T3 + 1, KC, :], T[2 * TAIL:T3 + 1, :].bitcast(F32), ALU.subtract).then_inc(s_wl, 1)

            def stats(b, l, s, tiles=range(TT)):
                n = NORMS.index((l, s, b))
                if n >= 1:
                    dve.wait_ge(s_ms, n)
                for t in tiles:
                    i = dve.bn_stats(BN6[:, t, :], XR[:, TT * b + t, :])
                link(i)
                for t in tiles:
                    i = dve.bn_aggr(MV[:, TT * b + t, :], BN6[:, t, :])
                if tiles[-1] == TT - 1:
                    i.then_inc(s_ms, 1)

            def normalise(l, s, b):
                n = tn(l, s, b)
                if s == 2 and b == 0:
                    dve.wait_ge(s_st, 256 * (l + 1))
                dve.wait_ge(s_rs, 2 * NORMS.index((l, s, b)) + 2)
                if n >= 2:
                    dve.wait_ge(s_tr, 3 * (n - 1))
                for t in range(TT):
                    i = dve.tensor_scalar(XN[n % 2][:, t, 0:C], XR[:, TT * b + t, :], MV[:, TT * b + t, 0:1], RST[:, TT * b + t:TT * b + t + 1],
                                          ALU.subtract, ALU.mult)
                link(i)
                tails(n)

            def tails(n):
                for r in range(2):
                    i = dve.tensor_copy(XN[n % 2][:, :, C + TAIL * r:C + TAIL * (r + 1)], XN[n % 2][:, :, KC * P:C])
                i.then_inc(s_xn, 1)

            def low(l, s, b):
                n = tn(l, s, b)
                dve.wait_ge(s_hi, 3 * n + 2)
                if s == 1:
                    H, L, T, cols = OH_[:, :, :], OL[:, :, :], OX, slice(0, N)
                    if b == 0:
                        dve.memset(OX[T3:TB, :].bitcast(F32), 1.0)
                    if b >= 1:
                        dve.wait_ge(s_pj, NT * l + TT * b)
                else:
                    H, L, T, cols = XS[:, b, 0], XS[:, b, 1], XT, slice(N * b, N * b + N)
                dve.tensor_tensor(L, FX[:, 0:KC, :], H.bitcast(F32), ALU.subtract)
                dve.wait_ge(s_hi, 3 * n + 3)
                dve.tensor_tensor(T[TAIL:2 * TAIL, cols], FX[TAIL:2 * TAIL, KC, :], T[TAIL:2 * TAIL, cols].bitcast(F32), ALU.subtract).then_inc(s_lo, 1)

            def qk_part2(i):
                dve.wait_ge(s_p2, i + 1)
                dve.tensor_tensor(PT[:, i % PARTS, 2, :], QR[:, i % 3, :], PT[:, i % PARTS, 1, :], ALU.subtract).then_inc(s_p3, 1)

            def qkv(l, b, beside=None):
                for m in range(2 * QM):
                    i = 2 * QM * (B * l + b) + m
                    if beside and m == QM:
                        beside()
                    dve.wait_ge(s_p1, i + 1)
                    if i >= 3:
                        dve.wait_ge(s_p3, i - 2)
                    dve.tensor_tensor(QR[:, i % 3, :], psum[0:96, QK_BANK[i % 3], :], PT[:, i % PARTS, 0, :], ALU.subtract).then_inc(s_r1, 1)
                    if b >= 1 or m >= 1:
                        qk_part2(i - 1)
                if b == B - 1:
                    qk_part2(i)

            def row_max(l, bb, g, u):
                i = 4 * bb + g
                dve.wait_ge(s_s, 128 * l + 8 * i + u + 1)
                o = 2 * (u % 2)
                dve.tensor_reduce(MX[:, g % 2, 2 * u:2 * u + 2], psum[:, o:o + 2, :], AX.X, ALU.max).then_inc(s_mx, 1)

            def stage(l, bb, g):
                i = 4 * bb + g
                dve.wait_ge(s_mt, 16 * l + i + 1)
                dve.tensor_scalar(MXT[:, g % 2, :], psum[0:16, 7, 0:P], -1.0, None, ALU.mult).then_inc(s_mc, 1)
                src = V[:, bass.ds(TT * bb, TT), 4 * HD * g:4 * HD * (g + 1)].rearrange("p t (h d) -> p t h d", d=HD)
                dst = VST[:, g, :, :, 0:HD]
                dve.tensor_copy(dst, src).then_inc(s_vs, 1)

            def attention(l, bb, last):
                for g in range(HG):
                    for u in range(8):
                        if not (last and g >= 2):
                            row_max(l, bb + (g + 2) // 4, (g + 2) % 4, u)
                        if u == 2 and not (last and g == 3):
                            stage(l, bb + (g + 1) // 4, (g + 1) % 4)
                        if last and (g, u) in TAIL_STEPS:
                            to_ffn(l, 0, TAIL_STEPS[g, u])

            def o_rows(l, b, tiles):
                n = tn(l, 1, b)
                for t in tiles:
                    i = NT * l + TT * b + t
                    dve.wait_ge(s_to, i + 1)
                    if t == 0:
                        dve.wait_ge(s_tr, 3 * (n - 1))
                    if i >= 1:
                        dve.wait_ge(s_on, i)
                    src = psum[:, 2 + t % 2, :].rearrange("p (h d) -> p h d", d=32)
                    link(dve.reciprocal(RC[:, :], src[:, :, HD:HD + 1].rearrange("p h o -> p (h o)")))
                    j = dve.tensor_tensor(XN[n % 2][:, t, 0:C].rearrange("p (h d) -> p h d", d=HD), src[:, :, 0:HD],
                                          RC[:, :].unsqueeze(2).to_broadcast([P, HEADS, HD]), ALU.mult)
                    j.then_inc(s_on, 1)
                if tiles[-1] == TT - 1:
                    dve.wait_ge(s_on, NT * l + TT * b + TT)
                    tails(n)

            def turned_o(l, chunks):
                n = tn(l, 1, 0)
                for c in chunks:
                    rows = P if c < KC else T3
                    dve.wait_ge(s_tr, 3 * n + c + 1)
                    dve.tensor_copy(FX[0:rows, c, :], psum[0:rows, CHUNK_BANK[c], :]).then_inc(s_fx, 1)
                    if c == 0:
                        dve.wait_ge(s_st, 256 * l + 240)
                    dve.wait_ge(s_fx, 3 * n + c + 1)
                    dst = OH_[:, c, :] if c < KC else OX[0:T3, :]
                    dve.tensor_copy(dst, FX[0:rows, c, :]).then_inc(s_hi, 1)

            def attn_add(l, b, tiles):
                if b == 0 and tiles[0] == 0:
                    dve.wait_ge(s_gm, 16 * (l + 1))
                for t in tiles:
                    dve.wait_ge(s_pj, NT * l + TT * b + t + 1)
                    dve.tensor_tensor(TA[:, t % 2, :], psum[:, 2 + t % 2, 0:C], GMSA[:, b, :], ALU.mult).then_inc(s_dvp, 1)
                done = NT * l + TT * b + tiles[-1] + 1
                dve.wait_ge(s_dvp, done)
                rows = XR[:, TT * b + tiles[0]:TT * b + tiles[-1] + 1, :]
                dve.tensor_tensor(rows, rows, TA[:, :, :], ALU.add).then_inc(s_xa, 2)
                dve.wait_ge(s_xa, done)

            def to_ffn(l, b, k):
                if k in (0, 1):
                    o_rows(l, b, (2 * k, 2 * k + 1))
                elif k in (2, 3) and b == 0:
                    turned_o(l, (0, 1) if k == 2 else (2,))
                if k == 3:
                    low(l, 1, b)
                elif k in (4, 5):
                    tiles = (2 * (k - 4), 2 * (k - 4) + 1)
                    attn_add(l, b, tiles)
                    if b == 0:
                        stats(b, l, 2, tiles)
                elif k == 6 and b >= 1:
                    stats(b, l, 2)
                elif k == 7:
                    normalise(l, 2, b)
                elif k == 9:
                    low(l, 2, b)

            def gate_ranks(b):
                lg, rk, cmp = LG[:, TT * b:TT * b + TT, :], RK[:, TT * b:TT * b + TT, :], CMP[:, TT * b:TT * b + TT]
                dve.wait_ge(s_lg, b + 1)
                dve.tensor_copy(lg, psum[:, 3, 0:TT * EXPERTS].rearrange("p (t e) -> p t e", e=EXPERTS)).then_inc(s_lc, 1)
                dve.wait_ge(s_lc, b + 1)
                shape = [P, TT, EXPERTS, EXPERTS]
                mine, other = lg.unsqueeze(3).to_broadcast(shape), lg.unsqueeze(2).to_broadcast(shape)
                dve.tensor_tensor(CMP2[:, 0], other, mine, ALU.is_gt)
                link(dve.tensor_tensor(CMP2[:, 1], other, mine, ALU.is_equal))
                link(dve.tensor_tensor(CMP2[:, 1], CMP2[:, 1], LOWER[:, :, :].unsqueeze(1).to_broadcast(shape), ALU.mult))
                link(dve.tensor_tensor(CMP2[:, 0], CMP2[:, 0], CMP2[:, 1], ALU.add))
                link(dve.tensor_reduce(rk, CMP2[:, 0], AX.X, ALU.add))
                link(dve.tensor_reduce(cmp, lg, AX.X, ALU.max))
                link(dve.tensor_scalar(rk, rk, 2.0, None, ALU.is_lt))
                dve.tensor_tensor(lg, lg, cmp.unsqueeze(2).to_broadcast([P, TT, EXPERTS]), ALU.subtract).then_inc(s_cw, 1)

            def gate_weights(b):
                cw, rk, cmp = CW[:, TT * b:TT * b + TT, :], RK[:, TT * b:TT * b + TT, :], CMP[:, TT * b:TT * b + TT]
                dve.wait_ge(s_ce, b + 2)
                link(dve.tensor_tensor(cw, cw, rk, ALU.mult))
                link(dve.tensor_reduce(cmp, cw, AX.X, ALU.add))
                link(dve.reciprocal(cmp, cmp))
                link(dve.tensor_tensor(cw, cw, cmp.unsqueeze(2).to_broadcast([P, TT, EXPERTS]), ALU.mult))

            def split_lo_tile(kind, f, m):
                dve.wait_ge(s_wsp, split_done(kind, f, m))
                if kind == "2":
                    dve.tensor_tensor(W2L[:, m, :], RAW2[:, m, :], W2H[:, m, :].bitcast(F32), ALU.subtract).then_inc(s_wl, 1)
                    return
                cols = slice(P * m, P * m + P)
                dve.tensor_tensor(W1L[:, :, cols], RAW1[:, 0:KC, cols], W1H[:, :, cols].bitcast(F32), ALU.subtract)
                dve.tensor_tensor(W1T[2 * TAIL:T3 + 1, cols], RAW1[2 * TAIL:T3 + 1, KC, cols], W1T[2 * TAIL:T3 + 1, cols].bitcast(F32), ALU.subtract).then_inc(s_wl, 1)

            def hidden_parts(f, u):
                b, m = u // HM, u % HM
                i = UNITS * f + u
                grp = B * f + b
                dve.wait_ge(s_g, i + 1)
                if m >= 3:
                    dve.wait_ge(s_h2, (HM - 1) * grp + m - 2)
                elif grp >= 1:
                    if m == 2:
                        dve.wait_ge(s_f2, TT * grp)
                    else:
                        dve.wait_ge(s_h2, (HM - 1) * (grp - 1) + m + 7)
                link(dve.tensor_copy(HH[:, m % 3, :], HF[:, i % 2, :]))
                dve.tensor_tensor(HL[:, m % 3, :], HF[:, i % 2, :], HH[:, m % 3, :].bitcast(F32), ALU.subtract).then_inc(s_h, 1)

            def ffn_take(f, b):
                grp = B * f + b
                l = SETS[f][0]
                if b == 0:
                    dve.wait_ge(s_b2[f % 2], 16 * (f // 2 + 1))
                    if f == first_set(l) and l + 1 < LAYERS:
                        dve.wait_ge(s_gd, 16 * (l + 2))
                for t in range(TT):
                    dve.wait_ge(s_f2, TT * grp + t + 1)
                    dve.tensor_tensor(T1[:, t, :], psum[:, 4 + t, 0:C], B2B[:, f % 2, :], ALU.add).then_inc(s_ev, 1)

            def ffn_add(f, b):
                l, e = SETS[f]
                if b == 0 and e == 0:
                    dve.wait_ge(s_gl, 16 * (l + 1))
                dve.wait_ge(s_ev, TT * (B * f + b + 1))
                for t in range(TT):
                    w = CW[:, TT * b + t, e:e + 1] if l == 0 else 1.0
                    i = dve.scalar_tensor_tensor(T1[:, t, :], T1[:, t, :], w, GMLP[:, b, :], ALU.mult, ALU.mult)
                link(i)
                dve.tensor_tensor(XR[:, TT * b:TT * b + TT, :], XR[:, TT * b:TT * b + TT, :], T1[:, :, :], ALU.add).then_inc(s_xr, TT)
                dve.wait_ge(s_xr, NT * f + TT * (b + 1))
                if f == sets_of(l)[-1] and l + 1 < LAYERS and b < B - 1:
                    stats(b, l + 1, 0)

            def skew_entries(u):
                if u == 0:
                    dve.wait_ge(s_l3, 48)
                t, half = u // 2, u % 2
                for b in (2 * half, 2 * half + 1):
                    link(dve.scalar_tensor_tensor(L3J[:, :], L3W[:, t, :], 1.0, SCB[0:VP, b, :], ALU.mult, ALU.mult, accum_out=VC[:, b, t:t + 1]))
                if u == 2 * VT_ - 1:
                    dve.tensor_tensor(VC[:, :, :], VC[:, :, :], BL[:, :].unsqueeze(1).to_broadcast([VP, B, VT_]), ALU.add).then_inc(s_vc, 1)

            def expm_constants(n):
                if n < 8:
                    i = dve.tensor_copy(ID8[:, n, :], IDN[0:D3, 0:D3])
                for j in (2 * n, 2 * n + 1):
                    i = dve.memset(THR[:, j:j + 1], float(2 ** j))
                link(i)

            def expm_step(n):
                dve.wait_ge(s_pp, n + 1)
                flat = "p s b d -> p (s b) d"
                p8 = psum[0:D3, 3, :].rearrange("p (s d) -> p s d", d=D3)
                if n == 0:
                    dve.tensor_tensor(AS[:, 0, :, :], UO[:, :, :], p8[:, 0:B, :], ALU.subtract)
                    link(dve.tensor_tensor(AS[:, 1, :, :], p8[:, 0:B, :], UO[:, :, :], ALU.subtract))
                    i = dve.tensor_reduce(NRM[:, 0:B], AS[:, 0, :, :], AX.X, ALU.add, apply_absolute_value=True)
                elif n == 1:
                    link(dve.tensor_reduce(NBC[:, 0:1], psum[0:B, 3, 0:D3], AX.X, ALU.max))
                    i = dve.tensor_copy(NBC[:, 4:4 + D3], NBC[:, 0:1].to_broadcast([B, D3]))
                elif n == 2:
                    link(dve.tensor_copy(NRM[:, 4:4 + B], psum[0:D3, 3, 0:B]))
                    for s in range(2):
                        j = dve.tensor_tensor(MK[:, s, :, :], NRM[:, 4:4 + B].unsqueeze(2).to_broadcast([D3, B, SQUARINGS]),
                                              THR[:, :].unsqueeze(1).to_broadcast([D3, B, SQUARINGS]), ALU.is_gt)
                    link(j)
                    link(dve.tensor_scalar(MKH[:, :, :], MK[:, 0, :, :], -0.5, 1.0, ALU.mult, ALU.add))
                    link(dve.tensor_reduce(NRM[:, 8:8 + B], MKH[:, :, :], AX.X, ALU.mult))
                    for s in range(2):
                        j = dve.tensor_tensor(AS[:, s, :, :], AS[:, s, :, :], NRM[:, 8:8 + B].unsqueeze(2).to_broadcast([D3, B, D3]), ALU.mult)
                    link(j)
                    i = dve.scalar_tensor_tensor(RR[:, :, :, :].rearrange(flat), AS[:, :, :, :].rearrange(flat), 1.0 / TAYLOR, ID8[:, :, :], ALU.mult, ALU.add)
                elif n < 3 + TAYLOR - 1:
                    j = TAYLOR - 1 - (n - 3)
                    i = dve.scalar_tensor_tensor(RR[:, :, :, :].rearrange(flat), p8, 1.0 / j, ID8[:, :, :], ALU.mult, ALU.add)
                else:
                    k = n - (3 + TAYLOR - 1)
                    mask = MK[:, :, :, k].rearrange("p s b -> p (s b)").unsqueeze(2).to_broadcast([D3, 8, D3]).bitcast(I32)
                    i = dve.copy_predicated(RR[:, :, :, :].rearrange(flat), mask, p8)
                    if n == EXPM_STEPS - 1:
                        link(i)
                        i = dve.tensor_tensor(RR[:, 0, :, :], RR[:, 0, :, :], ID8[:, 0:B, :], ALU.subtract)
                i.then_inc(s_pv, 1)

            def u_step(n):
                dve.wait_ge(s_pp, EXPM_STEPS + n + 1)
                o = psum[0:D3, 3, 0:D3]
                o2 = psum[0:D3, 3, D3:2 * D3]
                eye = IDN[0:D3, 0:D3]
                if n == 0:
                    link(dve.memset(ET[:, :], 0.0))
                    dve.tensor_copy(ET[:, 0:D3], eye)
                    link(dve.tensor_tensor(NW[:, 5, :], o, SU[:, :], ALU.mult))
                    dve.tensor_tensor(NW[:, 0, :], NW[:, 5, :], eye, ALU.add)
                    i = dve.tensor_tensor(NW[:, 2, :], eye, NW[:, 5, :], ALU.subtract)
                elif n == 1:
                    i = dve.tensor_copy(VTR[:, :], psum[0:D3, 3, 0:C])
                elif n == 2:
                    link(dve.tensor_copy(NW[:, 1, :], o))
                    i = dve.scalar_tensor_tensor(NW[:, 3, :], eye, 2.0, NW[:, 1, :], ALU.mult, ALU.subtract)
                elif n < 3 + 12:
                    if n % 2 == 1:
                        i = dve.scalar_tensor_tensor(NW[:, 4, :], eye, 2.0, o, ALU.mult, ALU.subtract)
                    else:
                        dve.tensor_copy(NW[:, 2, :], o)
                        i = dve.tensor_copy(NW[:, 3, :], o2)
                elif n == 15:
                    i = dve.tensor_copy(NW[:, 5, :], o)
                elif n == 16:
                    i = dve.tensor_tensor(UTT[:, :], ET[:, :], psum[0:D3, 3, 0:C], ALU.subtract)
                else:
                    dve.tensor_copy(GG[:, 0:KC, :], psum[:, 3, :].rearrange("p (c d) -> p c d", c=KC))
                    i = dve.tensor_copy(GG[0:TAIL, KC, :], psum[0:TAIL, 2, 0:B * D3])
                i.then_inc(s_pv, 1)

            dve.memset(ONE[:, :, :], 1.0)
            link(dve.memset(LOWER[:, :, :], 0.0))
            for e in range(1, EXPERTS):
                i = dve.memset(LOWER[:, e, 0:e], 1.0)
            link(i)
            dve.memset(UO[:, :, :], 0.0)
            dve.memset(SC[96:97, :, :], 1.0)
            dve.memset(XT[T3:TB, :].bitcast(F32), 1.0).then_inc(s_cst, 1)
            dve.wait_ge(s_sce, 1)
            link(dve.tensor_scalar(SCT[:, 0, :], SCT[:, 0, :], 1.0, None, ALU.add))
            link(dve.reciprocal(SCT[:, 1, :], SCT[:, 0, :]))
            sc = SC[0:96, :, :].rearrange("p k b -> p (k b)")
            dve.tensor_tensor(sc, sc, SCT[:, 1, :], ALU.mult).then_inc(s_sc, 2)
            def first_stats(b):
                dve.wait_ge(s_x[b], 16)
                stats(b, 0, 0)

            first_stats(0)
            first_stats(1)
            normalise(0, 0, 0)
            normalise(0, 0, 1)
            mods(0, (0, 1))

            for l in range(LAYERS):
                if l == 0:
                    split_lo_qkv(l, 0)
                    low(l, 0, 0)
                    split_lo_qkv(l, 1)
                    split_lo_qkv(l, 2)
                    first_stats(2)
                    low(l, 0, 1)
                    qkv(l, 0, lambda: normalise(l, 0, 2))
                    first_stats(3)
                    low(l, 0, 2)
                    mods(l, (2, 3))
                    normalise(l, 0, 3)
                    qkv(l, 1)
                    low(l, 0, 3)
                    dve.wait_ge(s_ce, 1)
                    dve.tensor_tensor(WGL[:, :, :], WGR[:, 0:KC, :], WGH[:, :, :].bitcast(F32), ALU.subtract)
                    dve.tensor_tensor(WGT[2 * TAIL:T3, :], WGR[2 * TAIL:T3, KC, :], WGT[2 * TAIL:T3, :].bitcast(F32), ALU.subtract).then_inc(s_wl2, 1)
                    split_lo(("p", l), RAWP, WPH, WPL, WPT)
                    qkv(l, 2)
                else:
                    for w in range(3):
                        split_lo_qkv(l, w)
                    ffn_take(sets_of(l - 1)[-1], B - 1)
                    ffn_add(sets_of(l - 1)[-1], B - 1)
                    qkv(l, 0, lambda: stats(B - 1, l, 0))
                    qkv(l, 1, lambda: normalise(l, 0, B - 1))
                    qkv(l, 2, lambda: low(l, 0, B - 1))
                link(dve.memset(VST[:, :, :, :, HD:32], 0.0))
                link(dve.memset(VST[:, :, :, :, HD:HD + 1], 1.0))
                qkv(l, 3)
                dve.wait_ge(s_v, NT * (l + 1))
                for g in range(2):
                    for u in range(8):
                        row_max(l, 0, g, u)
                        if (g, u) == (1, 1):
                            stage(l, 0, 0)
                if l + 1 < LAYERS:
                    mods(l + 1)
                with dve.Fori(0, B - 1) as bb:
                    attention(l, bb, False)
                attention(l, B - 1, True)

                f0, J = first_set(l), steps_of(l)
                for j in range(FIRST, J):
                    f, u = f0 + j // UNITS, j % UNITS
                    if j >= 0:
                        if f == U_SET and u >= U_UNIT:
                            u_step(2 * (u - U_UNIT))
                        hidden_parts(f, u)
                        for piece in split_pieces(l, j):
                            split_lo_tile(*piece)
                        if j >= HM and u % HM == 1:
                            ffn_take(f0 + (j - HM) // UNITS, (u // HM - 1) % B)
                        if f == U_SET and u >= U_UNIT:
                            u_step(2 * (u - U_UNIT) + 1)
                        if j >= HM and u % HM == add_unit(u):
                            ffn_add(f0 + (j - HM) // UNITS, (u // HM - 1) % B)
                    for b in range(B):
                        k = j - HM * b + O_STEPS
                        if 0 <= k < O_STEPS:
                            to_ffn(l, b, k)
                    if j == W1_UNIT:
                        split_lo(("1", f0), RAW1, W1H, W1L, W1T)
                    if j == 0:
                        split_lo(("2", f0), RAW2, W2H, W2L, None)
                    if l == 0 and 0 <= j < UNITS and j % HM == 5:
                        gate_ranks(j // HM)
                    if l == 0 and 0 <= j < UNITS and j % HM == 8:
                        gate_weights(j // HM)
                    if l + 1 < LAYERS and j == J - UNITS + P_UNIT:
                        split_lo(("p", l + 1), RAWP, WPH, WPL, WPT)
                    if l + 1 < LAYERS and j >= J - UNITS:
                        for b, first in enumerate(NEXT_UNIT):
                            if u == first:
                                normalise(l + 1, 0, b)
                            if u == first + 3:
                                low(l + 1, 0, b)
                    if f == V_SET and u < 2 * VT_:
                        skew_entries(u)
                    if 0 <= UNITS * f + u - EXPM_START + 8 < 8:
                        expm_constants(UNITS * f + u - EXPM_START + 8)
                    if 0 <= UNITS * f + u - EXPM_START < EXPM_STEPS:
                        expm_step(UNITS * f + u - EXPM_START)
            ffn_take(len(SETS) - 1, B - 1)
            ffn_add(len(SETS) - 1, B - 1)

            for b in range(B):
                for t in range(TT):
                    i = TT * b + t
                    dve.wait_ge(s_zo, i + 1)
                    dve.tensor_tensor(XR[:, i, :], XR[:, i, :], psum[:, 4 + t, 0:C], ALU.add).then_inc(s_fin, 1)


EXPM_START = UNITS * EXPM_SET + EXPM_UNIT
EXPM_STEPS = 3 + TAYLOR - 1 + SQUARINGS
U_STEPS = 18


_L = [dict(ada_w="L0_cond_w_adaln", ada_b="L0_cond_b_adaln", qkv_w="L0_cond_w_qkv", qkv_b="L0_cond_b_qkv",
           out_w="L0_cond_w_proj", out_b="L0_cond_b_proj", w_gate="L0_cond_w_gate", w1="L0_cond_w1", b1="L0_cond_b1",
           w2="L0_cond_w2", b2="L0_cond_b2"),
      dict(ada_w="L1_cond_ada_w", ada_b="L1_cond_ada_b", qkv_w="L1_cond_qkv_w", qkv_b="L1_cond_qkv_b",
           out_w="L1_cond_out_w", out_b="L1_cond_out_b", w1="L1_cond_w1", b1="L1_cond_b1", w2="L1_cond_w2", b2="L1_cond_b2"),
      dict(ada_w="L2_cond_W_ada", ada_b="L2_cond_b_ada", qkv_w="L2_cond_W_qkv", qkv_b="L2_cond_b_qkv",
           out_w="L2_cond_W_proj", out_b="L2_cond_b_proj", w1="L2_cond_W_fc1", b1="L2_cond_b_fc1", w2="L2_cond_W_fc2", b2="L2_cond_b_fc2")]


def kernel(**inputs):
    import numpy as np
    import concourse.bacc as bacc
    from concourse import mybir as mb
    from concourse.bass_utils import run_bass_kernel_spmd as run

    nc = bacc.Bacc("TRN2", target_bir_lowering=False, num_devices=1)
    arrays, aps = {}, {}
    for name, a in inputs.items():
        a = np.ascontiguousarray(a)
        arrays[f"in_{name}"] = a
        aps[name] = nc.dram_tensor(f"in_{name}", a.shape, mb.dt.from_np(a.dtype), kind="ExternalInput").ap()
    out = nc.dram_tensor("out", inputs["x"].shape, mb.dt.float32, kind="ExternalOutput").ap()
    layers = [{k: aps[v] for k, v in d.items()} for d in _L]
    build(nc, aps["x"], aps["cond_1152"], layers, aps["L3_cond_P"], aps["L3_cond_W"], aps["L3_cond_b"], out)
    r = run(nc, [arrays], core_ids=[0])
    return r.results[0]["out"]
```
